# Optimizing a Trainium2 kernel written in Bass

```python
import numpy as np
import jax
import jax.numpy as jnp

def _softmax(x, axis=-1):
    return jax.nn.softmax(x, axis=axis)

def _gelu(x):
    return jax.nn.gelu(x, approximate=True)

def _silu(x):
    return jax.nn.silu(x)

def _sigmoid(x):
    return jax.nn.sigmoid(x)

def _layernorm(x, axis=-1, eps=1e-05):
    m = jnp.mean(x, axis=axis, keepdims=True)
    v = jnp.var(x, axis=axis, keepdims=True)
    return (x - m) / jnp.sqrt(v + eps)

def _scatter_add(tgt, idx, src, axis=0):
    return tgt.at[idx].add(src)

def _segment_sum(src, seg, n):
    return jax.ops.segment_sum(src, seg, n)
kernel_name = 'mk_sandwich_d1_jaxref_r8_e87f48'

def setup_inputs(seed: int=0):
    np.random.seed(seed)
    _w = jnp.asarray

    def _L0_attn_setup():
        import jax, jax.numpy as jnp
        import numpy as np
        import math
        H = 16
        KV = 8
        D = 128
        HID = 256
        LAYER_IDX = 1
        LAMBDA_INIT = 0.8 - 0.6 * math.exp(-0.3 * LAYER_IDX)
        EPS = 1e-05
        key = jax.random.key(seed)
        ks = jax.random.split(key, 8)
        B, S = (2, 256)
        op_size = H * D + 2 * KV * D
        return {'hidden_states': jax.random.normal(ks[0], (B, S, HID), jnp.float32), 'Wqkv_w': jax.random.normal(ks[1], (op_size, HID), jnp.float32) * 0.02, 'Wqkv_b': jnp.zeros((op_size,), jnp.float32), 'lambda_q1': jax.random.normal(ks[2], (D,), jnp.float32) * 0.1, 'lambda_k1': jax.random.normal(ks[3], (D,), jnp.float32) * 0.1, 'lambda_q2': jax.random.normal(ks[4], (D,), jnp.float32) * 0.1, 'lambda_k2': jax.random.normal(ks[5], (D,), jnp.float32) * 0.1, 'subln_w': jnp.ones((2 * D,), jnp.float32), 'out_w': jax.random.normal(ks[6], (HID, H * D), jnp.float32) * 0.02, 'out_b': jnp.zeros((HID,), jnp.float32)}
    _L0_attn_in = _L0_attn_setup()

    def _L0_ffn_setup():
        import jax, jax.numpy as jnp
        import numpy as np
        HIDDEN = 256
        INTER = 1024
        SCALE = 64.0

        def fwht(x):
            orig_shape = x.shape
            n = orig_shape[-1]
            x = x.reshape(-1, n)
            h = 1
            while h < n:
                x = x.reshape(-1, n // (2 * h), 2, h)
                a, b = (x[:, :, 0, :], x[:, :, 1, :])
                x = jnp.stack([a + b, a - b], axis=2).reshape(-1, n)
                h *= 2
            return (x / jnp.sqrt(jnp.asarray(n, x.dtype))).reshape(orig_shape)
        key = jax.random.key(seed)
        ks = jax.random.split(key, 8)
        inp = jax.random.normal(ks[0], (4, 256, HIDDEN), dtype=jnp.float32)
        SU_ug = jnp.where(jax.random.bernoulli(ks[1], 0.5, (HIDDEN,)), 1.0, -1.0).astype(jnp.float32)
        SU_dp = jnp.where(jax.random.bernoulli(ks[2], 0.5, (INTER,)), 1.0, -1.0).astype(jnp.float32)
        Wscale_ug = jax.random.uniform(ks[3], (2 * INTER,), jnp.float32, 0.5, 1.5)
        Wscale_dp = jax.random.uniform(ks[4], (HIDDEN,), jnp.float32, 0.5, 1.5)
        W_up = jax.random.normal(ks[5], (INTER, HIDDEN), dtype=jnp.float32) * 0.02
        W_gate = jax.random.normal(ks[6], (INTER, HIDDEN), dtype=jnp.float32) * 0.02
        W_down = jax.random.normal(ks[7], (HIDDEN, INTER), dtype=jnp.float32) * 0.02
        return {'input': inp, 'SU_ug': SU_ug, 'SU_dp': SU_dp, 'Wscale_ug': Wscale_ug, 'Wscale_dp': Wscale_dp, 'W_up': W_up, 'W_gate': W_gate, 'W_down': W_down}
    _L0_ffn_in = _L0_ffn_setup()
    _d = {'L0_attn_hidden_states': _L0_attn_in['hidden_states'], 'L0_attn_Wqkv_w': _L0_attn_in['Wqkv_w'], 'L0_attn_Wqkv_b': _L0_attn_in['Wqkv_b'], 'L0_attn_lambda_q1': _L0_attn_in['lambda_q1'], 'L0_attn_lambda_k1': _L0_attn_in['lambda_k1'], 'L0_attn_lambda_q2': _L0_attn_in['lambda_q2'], 'L0_attn_lambda_k2': _L0_attn_in['lambda_k2'], 'L0_attn_subln_w': _L0_attn_in['subln_w'], 'L0_attn_out_w': _L0_attn_in['out_w'], 'L0_attn_out_b': _L0_attn_in['out_b'], 'L0_ffn_SU_ug': _L0_ffn_in['SU_ug'], 'L0_ffn_SU_dp': _L0_ffn_in['SU_dp'], 'L0_ffn_Wscale_ug': _L0_ffn_in['Wscale_ug'], 'L0_ffn_Wscale_dp': _L0_ffn_in['Wscale_dp'], 'L0_ffn_W_up': _L0_ffn_in['W_up'], 'L0_ffn_W_gate': _L0_ffn_in['W_gate'], 'L0_ffn_W_down': _L0_ffn_in['W_down']}
    _x0 = _d['L0_attn_hidden_states']
    _d['L0_attn_hidden_states'] = jax.random.normal(jax.random.fold_in(jax.random.key(seed), 1), (1, 2048, 256), dtype=_x0.dtype)
    del _x0
    return _d

def reference(L0_attn_hidden_states, L0_attn_Wqkv_w, L0_attn_Wqkv_b, L0_attn_lambda_q1, L0_attn_lambda_k1, L0_attn_lambda_q2, L0_attn_lambda_k2, L0_attn_subln_w, L0_attn_out_w, L0_attn_out_b, L0_ffn_SU_ug, L0_ffn_SU_dp, L0_ffn_Wscale_ug, L0_ffn_Wscale_dp, L0_ffn_W_up, L0_ffn_W_gate, L0_ffn_W_down):

    def _L0_attn_ref(hidden_states, Wqkv_w, Wqkv_b, lambda_q1, lambda_k1, lambda_q2, lambda_k2, subln_w, out_w, out_b):
        import jax, jax.numpy as jnp
        import numpy as np
        import math
        H = 16
        KV = 8
        D = 128
        HID = 256
        LAYER_IDX = 1
        LAMBDA_INIT = 0.8 - 0.6 * math.exp(-0.3 * LAYER_IDX)
        EPS = 1e-05
        B, S, _ = hidden_states.shape
        qkv = hidden_states @ Wqkv_w.T + Wqkv_b
        q, k, v = jnp.split(qkv, [H * D, H * D + KV * D], axis=-1)
        q = q.reshape(B, S, H // 2, 2, D)
        k = k.reshape(B, S, KV // 2, 2, D)
        v = v.reshape(B, S, KV // 2, 2 * D)
        rep = H // KV
        k = jnp.repeat(k, rep, axis=2)
        v = jnp.repeat(v, rep, axis=2)
        scale = D ** (-0.5)
        causal = jnp.tril(jnp.ones((S, S), bool))
        neg = jnp.finfo(jnp.float32).min

        def attn_map(qi, ki):
            s = jnp.einsum('bqhd,bkhd->bhqk', qi, ki) * scale
            s = jnp.where(causal, s, neg)
            return jax.nn.softmax(s, axis=-1)
        p1 = attn_map(q[:, :, :, 0], k[:, :, :, 0])
        p2 = attn_map(q[:, :, :, 1], k[:, :, :, 1])
        lam1 = jnp.exp(jnp.sum(lambda_q1 * lambda_k1))
        lam2 = jnp.exp(jnp.sum(lambda_q2 * lambda_k2))
        lam = lam1 - lam2 + LAMBDA_INIT
        p = p1 - lam * p2
        o = jnp.einsum('bhqk,bkhe->bqhe', p, v)
        rms = jax.lax.rsqrt(jnp.mean(o * o, axis=-1, keepdims=True) + EPS)
        o = o * rms * subln_w
        o = o * (1.0 - LAMBDA_INIT)
        o = o.reshape(B, S, H * D)
        return o @ out_w.T + out_b

    def _L0_ffn_ref(input, SU_ug, SU_dp, Wscale_ug, Wscale_dp, W_up, W_gate, W_down):
        import jax, jax.numpy as jnp
        import numpy as np
        HIDDEN = 256
        INTER = 1024
        SCALE = 64.0

        def fwht(x):
            orig_shape = x.shape
            n = orig_shape[-1]
            x = x.reshape(-1, n)
            h = 1
            while h < n:
                x = x.reshape(-1, n // (2 * h), 2, h)
                a, b = (x[:, :, 0, :], x[:, :, 1, :])
                x = jnp.stack([a + b, a - b], axis=2).reshape(-1, n)
                h *= 2
            return (x / jnp.sqrt(jnp.asarray(n, x.dtype))).reshape(orig_shape)
        n = SU_ug.shape[0]
        x = input.reshape(-1, n)
        x = fwht(x * SU_ug) / SCALE
        x_up = x @ W_up.T * (Wscale_ug[:INTER] * SCALE)
        x_gate = x @ W_gate.T * (Wscale_ug[INTER:] * SCALE)
        x = jax.nn.silu(x_gate) * x_up
        x = fwht(x * SU_dp) / SCALE
        x = x @ W_down.T * (Wscale_dp * SCALE)
        return x.reshape(input.shape)
    x = L0_attn_hidden_states
    x = x + _layernorm(_L0_attn_ref(_layernorm(x, axis=-1), L0_attn_Wqkv_w, L0_attn_Wqkv_b, L0_attn_lambda_q1, L0_attn_lambda_k1, L0_attn_lambda_q2, L0_attn_lambda_k2, L0_attn_subln_w, L0_attn_out_w, L0_attn_out_b), axis=-1)
    x = x + _layernorm(_L0_ffn_ref(_layernorm(x, axis=-1), L0_ffn_SU_ug, L0_ffn_SU_dp, L0_ffn_Wscale_ug, L0_ffn_Wscale_dp, L0_ffn_W_up, L0_ffn_W_gate, L0_ffn_W_down), axis=-1)
    return x

_drawn_inputs = setup_inputs


def setup_inputs(seed=0):
    import zlib

    import numpy as np

    out = dict(_drawn_inputs(seed))
    spreads = {'L0_attn_Wqkv_b': (0.0, 0.1), 'L0_attn_subln_w': (1.0, 0.2), 'L0_attn_out_b': (0.0, 0.1)}
    factors = {'L0_attn_lambda_q1': 3.445, 'L0_attn_lambda_k1': 8.0, 'L0_attn_lambda_q2': 8.0}
    for name, (base, spread) in spreads.items():
        noise = np.random.default_rng([zlib.crc32(name.encode()), seed]).standard_normal(out[name].shape)
        drawn = base * np.exp(spread * noise) if base else spread * noise
        out[name] = jnp.asarray(drawn.astype(out[name].dtype))
    for name, factor in factors.items():
        out[name] = (out[name] * factor).astype(out[name].dtype)
    return out
```

```python
import math
from contextlib import ExitStack

import concourse.bass as bass
from concourse import mybir

F32 = mybir.dt.float32
F32R = mybir.dt.float32r
BF16 = mybir.dt.bfloat16
ALU = mybir.AluOpType
ACT = mybir.ActivationFunctionType
X = mybir.AxisListType.X

P = 128
SEQ = 2048
HID = 256
D = 128
NQH = 16
NKH = 8
GROUPS = NKH // 2
INTER = 1024
TILES = SEQ // P
CT = HID // P
LAMBDA_INIT = 0.8 - 0.6 * math.exp(-0.3 * 1)
SCALE = float(D) ** -0.5
EPS = 1e-5
BANK = 512
QB = BANK // P
DUOS = TILES
CHUNKS = 5
NS = 4
E1_SLOTS = 2 * CHUNKS
E2_SLOTS = CHUNKS
MASKED = -1e30


def duo_chunks(d):
    out = []
    for s, i in ((0, TILES - 1 - d), (1, d)):
        keys = (i + 1) * P
        for c in range(-(-keys // BANK)):
            w = min(BANK, keys - c * BANK)
            out.append((s, i, c, w, (c + 1) * BANK >= keys))
    assert len(out) == CHUNKS
    return out


def attention_steps():
    steps, pending, late, due, mixing = [], [], [], [], []

    def emit(kind, what):
        exps = [pending.pop(0)] if pending and pending[0][1] < len(steps) else []
        exps = [e[0] for e in exps]
        n = len(steps)
        ratios = [r for r in due if r[1] <= n]
        for r in ratios:
            due.remove(r)
        assert kind != "T" or what not in mixing
        pool = [("mix", mixing.pop(0))] if mixing else []
        if kind == "OT":
            pool.append(("norm", what))
        steps.append((kind, what, exps, [r[0] for r in ratios], pool))
        for r in ratios:
            mixing.extend((r[0][0], j) for j, ch in enumerate(duo_chunks(r[0][0])) if ch[0] == r[0][1])
        for (d, m, j) in exps:
            s, _, _, _, last = duo_chunks(d)[j]
            if m == 1 and last:
                due.append(((d, s), n + 2))
        if kind == "S":
            d, m, j = what
            s, _, _, _, last = duo_chunks(d)[j]
            if last:
                for jj, ch in enumerate(duo_chunks(d)):
                    if ch[0] == s:
                        pending.append(((d, m, jj), n))
        if kind == "PV":
            d, j = what
            s, _, _, _, last = duo_chunks(d)[j]
            if last:
                late.append(("OT", 2 * d + s, n + 3))
        if kind == "OT":
            late.append(("OP", what, n + 4))
        for x in list(late):
            if x[2] <= n and x in late:
                late.remove(x)
                emit(x[0], x[1])

    for h in range(2 * DUOS + 3):
        d, m = divmod(h, 2)
        scores = [("S", (d, m, j)) for j in range(CHUNKS)] if d < DUOS else []
        db = (h - 3) // 2 if m == 1 else (h - 4) // 2
        rest = []
        if 0 <= db < DUOS:
            widths = [c[3] for c in duo_chunks(db)]
            cut = min(range(1, CHUNKS), key=lambda n: abs(sum(widths[:n]) - sum(widths[n:])))
            part = range(cut) if m == 1 else range(cut, CHUNKS)
            part = list(part)
            rest.append(("T", (db, part[0])))
            for a, j in enumerate(part):
                if a + 1 < len(part):
                    rest.append(("T", (db, part[a + 1])))
                rest.append(("PV", (db, j)))
        if h // 4 + 1 < DUOS // 2:
            scores.insert(3, ("QP", (h // 4 + 1, h % 4 // 2, h % 2)))
        while rest or scores:
            if rest:
                emit(*rest.pop(0))
            if scores:
                emit(*scores.pop(0))
    while pending or late or due or mixing:
        emit("END", None)
        late.sort(key=lambda x: x[2])
    return steps


def build(nc, hidden, wqkv, bqkv, lq1, lk1, lq2, lk2, subln, out_w, out_b, su_ug, su_dp, ws_ug, ws_dp,
          w_up, w_gate, w_down, out):
    x_tiles = hidden[0].rearrange("(t p) c -> p t c", p=P)
    out_tiles = out[0].rearrange("(t p) c -> p t c", p=P)
    K0 = NQH * D
    V0 = K0 + NKH * D
    steps = attention_steps()

    with ExitStack() as whole:
        def tensors(stack):
            return lambda name, shape, dt=F32: stack.enter_context(nc.sbuf_tensor(name, shape, dt))

        def semaphores(stack, *names):
            return [stack.enter_context(nc.semaphore(n)) for n in names]

        sb = tensors(whole)
        whole.enter_context(nc.allow_non_contiguous_dma(reason="short columns of biases and scales"))
        S = [whole.enter_context(nc.psum_tensor(f"score_bank{b}", [P, BANK], F32)) for b in range(NS)]
        T = [whole.enter_context(nc.psum_tensor(f"turn_bank{b}", [P, BANK], F32)) for b in range(2)]
        O = whole.enter_context(nc.psum_tensor("pv_bank", [P, BANK], F32))
        R = whole.enter_context(nc.psum_tensor("proj_bank", [P, BANK], F32))

        xT_hi = sb("xT_hi", [P, CT, SEQ], F32R)
        xT_lo = sb("xT_lo", [P, CT, SEQ], F32R)
        acc = sb("acc", [P, TILES, HID])
        ident = sb("ident", [P, P])
        ident_bf = sb("ident_bf", [P, P], BF16)
        mask_bf = sb("mask_bf", [P, P], BF16)
        had = sb("had", [P, P], F32R)
        had_neg = sb("had_neg", [P, P], F32R)
        half_neg = sb("half_neg", [P, 4])
        neg_lam = sb("neg_lam", [P, 1])
        subln_col = sb("subln_col", [P, CT])

        with ExitStack() as att:
            sa = tensors(att)
            w_raw = sa("w_raw", [P, 8, HID])
            wo_raw = sa("wo_raw", [P, CT, 2 * HID])
            bqk_raw = sa("bqk_raw", [P, 6])
            bv = sa("bv", [P, 2, HID])

            with ExitStack() as pro:
                sp_ = tensors(pro)
                x_in = sp_("x_in", [P, TILES, HID])
                xn = sp_("xn", [P, TILES, HID])
                stats = sp_("stats", [P, TILES, 6])
                mv = sp_("mv", [P, TILES, 2])
                var_eps = sp_("var_eps", [P, TILES])
                rstd = sp_("rstd", [P, TILES])
                lam_in = sp_("lam_in", [P, 4, D])
                lam_junk = sp_("lam_junk", [P, 2, D])
                lam_dot = sp_("lam_dot", [P, 2])
                lam_exp = sp_("lam_exp", [P, 2])
                lam_diff = sp_("lam_diff", [P, 1])
                hd = [sp_(f"hd{k}", [P, P]) for k in range(2)]
                x_in_sems = semaphores(pro, *[f"x_landed{q}" for q in range(4)])
                (small_landed, lam_landed, w_landed, ident_base, ident_ready, consts_ready, stats_ready,
                 rstd_step, rstd_ready, xn_ready, turned, hi_ready, lo_ready, lam_dots, lam_exps, lam_step,
                 had_step) = semaphores(
                    pro, "small_landed", "lam_landed", "w_landed", "ident_base", "ident_ready", "consts_ready",
                    "stats_ready", "rstd_step", "rstd_ready", "xn_ready", "turned", "hi_ready", "lo_ready",
                    "lam_dots", "lam_exps", "lam_step", "had_step")
                block = pro.enter_context(nc.Block())

                @block.sync
                def _(sp):
                    for q in range(4):
                        sp.dma_start(x_in[:, 4 * q:4 * q + 4, :], x_tiles[:, 4 * q:4 * q + 4, :])\
                          .then_inc(x_in_sems[q], 16)
                    for k, v in enumerate((lq1, lk1, lq2, lk2)):
                        sp.dma_start(lam_in[:, k, :], v.rearrange("(a d) -> a d", a=1).broadcast_to([P, D]))\
                          .then_inc(lam_landed, 16)
                    sp.dma_start(subln_col[:, :], subln.rearrange("(t p) -> p t", p=P)).then_inc(small_landed, 16)
                    sp.dma_start(w_raw[:, 0:4, :], wqkv[0:4 * D, :].rearrange("(r p) c -> p r c", p=P))\
                      .then_inc(w_landed, 16)
                    sp.dma_start(w_raw[:, 4:6, :], wqkv[K0:K0 + 2 * D, :].rearrange("(r p) c -> p r c", p=P))\
                      .then_inc(w_landed, 16)
                    sp.dma_start(w_raw[:, 6:8, :], wqkv[V0:V0 + 2 * D, :].rearrange("(r p) c -> p r c", p=P))\
                      .then_inc(w_landed, 16)
                    sp.dma_start(wo_raw[:, :, :], out_w[:, 0:2 * HID].rearrange("(t p) c -> p t c", p=P))\
                      .then_inc(w_landed, 16)
                    sp.dma_start(bqk_raw[:, 0:4], bqkv[0:4 * D].rearrange("(r p) -> p r", p=P))\
                      .then_inc(w_landed, 16)
                    sp.dma_start(bqk_raw[:, 4:6], bqkv[K0:K0 + 2 * D].rearrange("(r p) -> p r", p=P))\
                      .then_inc(w_landed, 16)
                    for k in range(2):
                        sp.dma_start(bv[:, k, :], bqkv[V0:V0 + HID].rearrange("(a d) -> a d", a=1)
                                     .broadcast_to([P, HID])).then_inc(w_landed, 16)
                    sp.wait_ge(small_landed, 16)
                    sp.wait_ge(w_landed, 128)

                @block.gpsimd
                def _(pool):
                    pool.memset(ident[:, :], 0.0).then_inc(ident_base, 1)
                    pool.memset(mask_bf[:, :], 0.0).then_inc(ident_base, 1)
                    pool.memset(half_neg[:, :], -0.5).then_inc(ident_base, 1)
                    pool.wait_ge(ident_base, 3)
                    pool.affine_select(out=ident[:, :], in_=ident[:, :], compare_op=ALU.not_equal, fill=1.0,
                                       base=0, pattern=[[-1, P]], channel_multiplier=1).then_inc(ident_ready, 1)
                    pool.wait_ge(ident_ready, 1)
                    pool.tensor_copy(ident_bf[:, :], ident[:, :]).then_inc(consts_ready, 1)
                    pool.affine_select(out=mask_bf[:, :], in_=mask_bf[:, :], compare_op=ALU.is_ge, fill=MASKED,
                                       base=0, pattern=[[-1, P]], channel_multiplier=1).then_inc(consts_ready, 1)
                    for q in range(4):
                        t = slice(4 * q, 4 * q + 4)
                        pool.wait_ge(stats_ready, 4 * q + 4)
                        pool.tensor_scalar(var_eps[:, t], mv[:, t, 1], 1.0, EPS, ALU.mult, ALU.add)\
                            .then_inc(rstd_step, 1)
                        pool.wait_ge(rstd_step, q + 1)
                        pool.tensor_tensor(rstd[:, t], var_eps[:, t], half_neg[:, :], ALU.pow)\
                            .then_inc(rstd_ready, 1)
                    pool.memset(acc[:, :, :], 0.0).then_inc(consts_ready, 1)

                @block.vector
                def _(dve):
                    def split_x(q):
                        for ct in range(CT):
                            u = CT * q + ct
                            dve.wait_ge(hi_ready, u + 1)
                            dve.tensor_tensor(xT_lo[:, ct, q * BANK:(q + 1) * BANK], T[u % 2][:, :],
                                              xT_hi[:, ct, q * BANK:(q + 1) * BANK].bitcast(F32), ALU.subtract)\
                               .then_inc(lo_ready, 1)

                    n = 0
                    for q in range(4):
                        dve.wait_ge(x_in_sems[q], 16)
                        for t in range(4 * q, 4 * q + 4):
                            dve.bn_stats(stats[:, t, :], x_in[:, t, :]).then_inc(lam_step, 1)
                            n += 1
                            dve.wait_ge(lam_step, n)
                            dve.bn_aggr(mv[:, t, :], stats[:, t, :]).then_inc(stats_ready, 1)
                        if q > 0:
                            normalise = range(4 * q - 4, 4 * q)
                            dve.wait_ge(rstd_ready, q)
                            for t in normalise:
                                dve.tensor_scalar(xn[:, t, :], x_in[:, t, :], mv[:, t, 0:1], rstd[:, t:t + 1],
                                                  ALU.subtract, ALU.mult).then_inc(xn_ready, 1)
                            split_x(q - 1)
                    dve.wait_ge(rstd_ready, 4)
                    for t in range(12, 16):
                        dve.tensor_scalar(xn[:, t, :], x_in[:, t, :], mv[:, t, 0:1], rstd[:, t:t + 1],
                                          ALU.subtract, ALU.mult).then_inc(xn_ready, 1)
                    split_x(3)
                    dve.wait_ge(lam_landed, 64)
                    for k in range(2):
                        dve.tensor_tensor_reduce(out=lam_junk[:, k, :], in0=lam_in[:, 2 * k, :],
                                                 in1=lam_in[:, 2 * k + 1, :], scale=1.0, scalar=0.0,
                                                 op0=ALU.mult, op1=ALU.add, accum_out=lam_dot[:, k:k + 1])\
                           .then_inc(lam_dots, 1)
                    dve.wait_ge(lam_exps, 1)
                    dve.tensor_tensor(lam_diff[:, :], lam_exp[:, 1:2], lam_exp[:, 0:1], ALU.subtract)\
                       .then_inc(lam_step, 1)
                    n += 1
                    dve.wait_ge(lam_step, n)
                    dve.tensor_scalar(neg_lam[:, :], lam_diff[:, :], -LAMBDA_INIT, None, ALU.add)\
                       .then_inc(lam_step, 1)
                    dve.wait_ge(ident_ready, 1)
                    src = ident
                    k = 0
                    for stage in range(7):
                        h = 1 << stage
                        dst = hd[stage % 2]
                        a = src[:, :].rearrange("p (n two h) -> p n two h", two=2, h=h)
                        b = dst[:, :].rearrange("p (n two h) -> p n two h", two=2, h=h)
                        dve.tensor_tensor(b[:, :, 0, :], a[:, :, 0, :], a[:, :, 1, :], ALU.add).then_inc(had_step, 1)
                        dve.tensor_tensor(b[:, :, 1, :], a[:, :, 0, :], a[:, :, 1, :], ALU.subtract)\
                           .then_inc(had_step, 1)
                        k += 2
                        dve.wait_ge(had_step, k)
                        src = dst
                    dve.tensor_copy(had[:, :], src[:, :]).then_inc(had_step, 1)
                    dve.tensor_scalar(had_neg[:, :], src[:, :], -1.0, None, ALU.mult).then_inc(had_step, 1)

                @block.scalar
                def _(act):
                    for q in range(4):
                        for ct in range(CT):
                            act.wait_ge(turned, CT * q + ct + 1)
                            act.activation(xT_hi[:, ct, q * BANK:(q + 1) * BANK], T[(CT * q + ct) % 2][:, :],
                                           ACT.Copy).then_inc(hi_ready, 1)
                    act.wait_ge(lam_dots, 2)
                    act.activation(lam_exp[:, :], lam_dot[:, :], ACT.Exp).then_inc(lam_exps, 1)

                @block.tensor
                def _(pe):
                    pe.wait_ge(ident_ready, 1)
                    for q in range(4):
                        pe.wait_ge(xn_ready, 4 * q + 4)
                        for ct in range(CT):
                            u = CT * q + ct
                            if u >= 2:
                                pe.wait_ge(lo_ready, u - 1)
                            for t in range(4):
                                mm = pe.transpose(T[u % 2][:, t * P:(t + 1) * P],
                                                  xn[:, 4 * q + t, ct * P:(ct + 1) * P], ident[:, :])
                            mm.then_inc(turned, 1)

            with ExitStack() as shared:
                ss = tensors(shared)
                wkv_hi = ss("wkv_hi", [P, CT, 2 * HID], F32R)
                wkv_lo = ss("wkv_lo", [P, CT, 2 * HID], F32R)
            e2 = sa("e2", [P, E2_SLOTS, BANK])
            e1 = sa("e1", [P, E1_SLOTS, BANK])
            q_hi = sa("q_hi", [P, 2, 2, 2, HID], F32R)
            q_lo = sa("q_lo", [P, 2, 2, 2, HID], F32R)
            k_hi = sa("k_hi", [P, 2, SEQ], F32R)
            k_lo = sa("k_lo", [P, 2, SEQ], F32R)
            v_hl = sa("v_hl", [P, TILES, 2 * HID], F32R)
            pT_hi = sa("pT_hi", [P, 2, BANK], F32R)
            pT_lo = sa("pT_lo", [P, 2, BANK], F32R)
            wq_hi = sa("wq_hi", [P, CT, 4 * D], F32R)
            wq_lo = sa("wq_lo", [P, CT, 4 * D], F32R)
            wo_hi = sa("wo_hi", [P, 2, CT, HID], F32R)
            wo_lo = sa("wo_lo", [P, 2, CT, HID], F32R)
            o_half = sa("o_half", [P, 2, HID])
            o_sum = sa("o_sum", [P, 2, HID])
            oT_hi = sa("oT_hi", [P, 2, HID], F32R)
            oT_lo = sa("oT_lo", [P, 2, HID], F32R)
            bqk = sa("bqk", [P, 6])
            subln_s = sa("subln_s", [P, CT])
            mx = sa("mx", [P, 2, 2, 2, 4])
            negmx = sa("negmx", [P, 2, 2, 2])
            ssum = sa("ssum", [P, 4, 2, 2, 4])
            s12 = sa("s12", [P, 4, 2, 2])
            inv_s2 = sa("inv_s2", [P, 4, 2])
            ratio = sa("ratio", [P, 4, 2])
            msq = sa("msq", [P, 4])
            rms_a = sa("rms_a", [P, 4])
            rms_b = sa("rms_b", [P, 4])
            rms = sa("rms", [P, 4])

            names = ("w_next", "b_ready", "s_full", "s_act", "s_dve", "t_full", "t_hi", "t_lo", "r_full", "r_hi",
                     "r_free", "v_lo", "neg_ready", "ratio_step", "ratio_ready", "e2_scaled", "p_ready",
                     "pv_done", "o_half_ready", "o_ready", "msq_ready", "rms_step", "rms_ready")
            sems = semaphores(att, *names)
            (w_next, b_ready, s_full, s_act, s_dve, t_full, t_hi, t_lo, r_full, r_hi, r_free, v_lo, neg_ready,
             ratio_step, ratio_ready, e2_scaled, p_ready, pv_done, o_half_ready, o_ready, msq_ready, rms_step,
             rms_ready) = sems
            assert [s.num for s in sems] == list(range(sems[0].num, sems[0].num + len(sems)))

            W_TURNS, KV_USES, K_USES = 6, 16, 8
            t_use, r_use, n_qp = {}, {}, {}
            for n in range(4):
                r_use["QP", (0, n // 2, n % 2)] = n
                n_qp[(0, n // 2, n % 2)] = n
            for kind, what, *_ in steps:
                if kind in ("T", "OT"):
                    t_use[kind, what] = W_TURNS + len(t_use)
                if kind in ("QP", "OP"):
                    r_use[kind, what] = len(r_use)
                if kind == "QP":
                    n_qp[what] = len(n_qp)

            def s_use(d, m, j):
                return KV_USES + CHUNKS * (2 * d + m) + j

            def q_cols(s, i):
                return (i % 2) * P

            def first_q_token(u, s):
                return (TILES - 2 - 2 * u) * P if s == 0 else 2 * u * P

            with nc.Fori(0, GROUPS) as g:
                with nc.Block() as block:

                    @block.sync
                    def _(sp):
                        nxt = (g + 1) % GROUPS
                        sp.wait_ge(t_full, 4)
                        sp.dma_start(w_raw[:, 0:4, :], wqkv[bass.ds(nxt * (4 * D), 4 * D), :]
                                     .rearrange("(r p) c -> p r c", p=P)).then_inc(w_next, 16)
                        sp.dma_start(w_raw[:, 4:6, :], wqkv[bass.ds(nxt * (2 * D) + K0, 2 * D), :]
                                     .rearrange("(r p) c -> p r c", p=P)).then_inc(w_next, 16)
                        sp.dma_start(w_raw[:, 6:8, :], wqkv[bass.ds(nxt * (2 * D) + V0, 2 * D), :]
                                     .rearrange("(r p) c -> p r c", p=P)).then_inc(w_next, 16)
                        sp.wait_ge(t_full, W_TURNS)
                        sp.dma_start(wo_raw[:, :, :], out_w[:, bass.ds(nxt * (2 * HID), 2 * HID)]
                                     .rearrange("(t p) c -> p t c", p=P)).then_inc(w_next, 16)
                        sp.wait_ge(b_ready, 2)
                        sp.dma_start(bqk_raw[:, 0:4], bqkv[bass.ds(nxt * (4 * D), 4 * D)]
                                     .rearrange("(r p) -> p r", p=P)).then_inc(w_next, 16)
                        sp.dma_start(bqk_raw[:, 4:6], bqkv[bass.ds(nxt * (2 * D) + K0, 2 * D)]
                                     .rearrange("(r p) -> p r", p=P)).then_inc(w_next, 16)
                        sp.wait_ge(s_dve, KV_USES)
                        for k in range(2):
                            sp.dma_start(bv[:, k, :], bqkv[bass.ds(nxt * HID + V0, HID)]
                                         .rearrange("(a d) -> a d", a=1).broadcast_to([P, HID])).then_inc(w_next, 16)
                        sp.wait_ge(w_next, 8 * 16)

                    @block.tensor
                    def _(pe):
                        def turn_bank(u):
                            if u >= 2:
                                pe.wait_ge(t_lo, u - 1)
                            return T[u % 2]

                        def score_bank(k):
                            if k >= NS:
                                pe.wait_ge(s_act, k - NS + 1)
                                pe.wait_ge(s_dve, k - NS + 1)
                            return S[k % NS]

                        def proj_bank(u):
                            if u >= 1:
                                pe.wait_ge(r_free, u)
                            return R

                        def project_q(what):
                            u, s, m = what
                            bank = proj_bank(r_use["QP", what])
                            if u == 0 and s == 0 and m == 0:
                                pe.wait_ge(t_lo, 4)
                            head, tok = (2 * s + m) * D, first_q_token(u, s)
                            n = 0
                            for ct in range(CT):
                                for w, x in ((wq_hi, xT_hi), (wq_hi, xT_lo), (wq_lo, xT_hi)):
                                    mm = pe.matmul(bank[:, 0:HID], w[:, ct, head:head + D],
                                                   x[:, ct, tok:tok + HID], start=(n == 0), stop=(n == 5))
                                    n += 1
                            mm.then_inc(r_full, 1)

                        for u in range(4):
                            bank = turn_bank(u)
                            for rr in range(2):
                                for ct in range(CT):
                                    mm = pe.transpose(bank[:, ct * HID + rr * P:ct * HID + (rr + 1) * P],
                                                      w_raw[:, 2 * u + rr, ct * P:(ct + 1) * P], ident[:, :])
                            mm.then_inc(t_full, 1)
                        for s in range(2):
                            bank = turn_bank(4 + s)
                            for et in range(CT):
                                for nt in range(CT):
                                    mm = pe.transpose(bank[:, et * HID + nt * P:et * HID + (nt + 1) * P],
                                                      wo_raw[:, nt, s * HID + et * P:s * HID + (et + 1) * P],
                                                      ident[:, :])
                            mm.then_inc(t_full, 1)
                        pe.wait_ge(t_lo, 4)
                        for k in range(K_USES):
                            m, c = divmod(k, 4)
                            bank = score_bank(k)
                            n = 0
                            for ct in range(CT):
                                for w, x in ((wkv_hi, xT_hi), (wkv_hi, xT_lo), (wkv_lo, xT_hi)):
                                    mm = pe.matmul(bank[:, :], w[:, ct, m * D:(m + 1) * D],
                                                   x[:, ct, c * BANK:(c + 1) * BANK], start=(n == 0), stop=(n == 5))
                                    n += 1
                            mm.then_inc(s_full, 1)
                            if k < 4:
                                project_q((0, k // 2, k % 2))
                        for v in range(KV_USES - K_USES):
                            bank = score_bank(K_USES + v)
                            for tt in range(2):
                                tok, n = (2 * v + tt) * P, 0
                                for ct in range(CT):
                                    for x, w in ((xT_hi, wkv_hi), (xT_hi, wkv_lo), (xT_lo, wkv_hi)):
                                        mm = pe.matmul(bank[:, tt * HID:(tt + 1) * HID], x[:, ct, tok:tok + P],
                                                       w[:, ct, HID:2 * HID], start=(n == 0), stop=(n == 5))
                                        n += 1
                            mm.then_inc(s_full, 1)
                        pe.wait_ge(s_dve, K_USES)

                        for kind, what, *_ in steps:
                            if kind == "S":
                                d, m, j = what
                                s, i, c, w, diagonal = duo_chunks(d)[j]
                                if d % 2 == 0:
                                    pe.wait_ge(r_free, r_use["QP", (d // 2, s, m)] + 1)
                                bank = score_bank(s_use(d, m, j))
                                col = q_cols(s, i)
                                qh = q_hi[:, d // 2 % 2, s, m, col:col + P]
                                ql = q_lo[:, d // 2 % 2, s, m, col:col + P]
                                kh = k_hi[:, m, c * BANK:c * BANK + w]
                                kl = k_lo[:, m, c * BANK:c * BANK + w]
                                pe.matmul(bank[:, 0:w], qh, kh, start=True, stop=False)
                                if diagonal:
                                    pe.matmul(bank[:, w - P:w], ident_bf[:, :], mask_bf[:, :],
                                              start=False, stop=False)
                                pe.matmul(bank[:, 0:w], qh, kl, start=False, stop=False)
                                pe.matmul(bank[:, 0:w], ql, kh, start=False, stop=True).then_inc(s_full, 1)
                            elif kind == "T":
                                d, j = what
                                w, q = duo_chunks(d)[j][3], CHUNKS * d + j
                                pe.wait_ge(p_ready, q + 1)
                                bank = turn_bank(t_use[kind, what])
                                for b in range(w // P):
                                    mm = pe.transpose(bank[:, b * P:(b + 1) * P],
                                                      e1[:, q % E1_SLOTS, b * P:(b + 1) * P], ident[:, :])
                                mm.then_inc(t_full, 1)
                            elif kind == "PV":
                                d, j = what
                                s, i, c, w, last = duo_chunks(d)[j]
                                q, o = CHUNKS * d + j, 2 * d + s
                                if q == 0:
                                    pe.wait_ge(v_lo, KV_USES - K_USES)
                                if c == 0 and o >= 1:
                                    pe.wait_ge(o_ready, o)
                                pe.wait_ge(t_lo, t_use["T", what] + 1)
                                for b in range(w // P):
                                    kt = c * QB + b
                                    pe.matmul(O[:, :], pT_hi[:, q % 2, b * P:(b + 1) * P], v_hl[:, kt, :],
                                              start=(kt == 0), stop=False)
                                    mm = pe.matmul(O[:, 0:HID], pT_lo[:, q % 2, b * P:(b + 1) * P],
                                                   v_hl[:, kt, 0:HID], start=False, stop=(kt == i))
                                mm.then_inc(pv_done, 1)
                            elif kind == "OT":
                                pe.wait_ge(o_ready, what + 1)
                                bank = turn_bank(t_use[kind, what])
                                for et in range(CT):
                                    mm = pe.transpose(bank[:, et * P:(et + 1) * P],
                                                      o_sum[:, what % 2, et * P:(et + 1) * P], ident[:, :])
                                mm.then_inc(t_full, 1)
                            elif kind == "OP":
                                o, s = what, what % 2
                                bank = proj_bank(r_use[kind, what])
                                pe.wait_ge(t_lo, t_use["OT", o] + 1)
                                n = 0
                                for et in range(CT):
                                    for a, w in ((oT_hi, wo_hi), (oT_hi, wo_lo), (oT_lo, wo_hi)):
                                        mm = pe.matmul(bank[:, 0:HID], a[:, o % 2, et * P:(et + 1) * P],
                                                       w[:, s, et, :], start=(n == 0), stop=(n == 5))
                                        n += 1
                                mm.then_inc(r_full, 1)
                            elif kind == "QP":
                                project_q(what)

                    @block.scalar
                    def _(act):
                        def q_high(what):
                            u, s, m = what
                            act.wait_ge(r_full, r_use["QP", what] + 1)
                            act.activation(q_hi[:, u % 2, s, m, :], R[:, 0:HID], ACT.Identity,
                                           bias=bqk[:, 2 * s + m:2 * s + m + 1]).then_inc(r_hi, 1)

                        for u in range(4):
                            act.wait_ge(t_full, u + 1)
                            src = T[u % 2][:, :].rearrange("p (c n) -> p c n", c=CT)
                            dst = wq_hi if u < 2 else wkv_hi
                            act.activation(dst[:, :, u % 2 * HID:(u % 2 + 1) * HID], src, ACT.Copy,
                                           scale=SCALE if u < 2 else 1.0).then_inc(t_hi, 1)
                        act.wait_ge(b_ready, 3)
                        for s in range(2):
                            act.wait_ge(t_full, 5 + s)
                            for et in range(CT):
                                ins = act.activation(wo_hi[:, s, et, :], T[s][:, et * HID:(et + 1) * HID], ACT.Copy,
                                                     scale=subln_s[:, et:et + 1])
                            ins.then_inc(t_hi, 1)
                        for k in range(K_USES):
                            m, c = divmod(k, 4)
                            act.wait_ge(s_full, k + 1)
                            act.activation(k_hi[:, m, c * BANK:(c + 1) * BANK], S[k % NS][:, :], ACT.Identity,
                                           bias=bqk[:, 4 + m:5 + m]).then_inc(s_act, 1)
                            if k < 4:
                                q_high((0, k // 2, k % 2))
                        for v in range(KV_USES - K_USES):
                            act.wait_ge(s_dve, K_USES + v + 1)
                            act.activation(v_hl[:, 2 * v:2 * v + 2, 0:HID],
                                           e1[:, v % 2, :].rearrange("p (t n) -> p t n", t=2), ACT.Copy)\
                               .then_inc(s_act, 1)
                        act.wait_ge(v_lo, KV_USES - K_USES)

                        for kind, what, exps, _, _ in steps:
                            if kind == "T":
                                d, j = what
                                w, q, u = duo_chunks(d)[j][3], CHUNKS * d + j, t_use[kind, what]
                                act.wait_ge(t_full, u + 1)
                                if q >= 2:
                                    act.wait_ge(pv_done, q - 1)
                                act.activation(pT_hi[:, q % 2, 0:w], T[u % 2][:, 0:w], ACT.Copy).then_inc(t_hi, 1)
                            elif kind == "PV":
                                d, j = what
                                s, _, _, _, last = duo_chunks(d)[j]
                                if last:
                                    o = 2 * d + s
                                    act.wait_ge(pv_done, CHUNKS * d + j + 1)
                                    if o >= 2:
                                        act.wait_ge(msq_ready, o - 1)
                                    act.activation(o_half[:, o % 2, :], O[:, HID:2 * HID], ACT.Copy)\
                                       .then_inc(o_half_ready, 1)
                            elif kind == "OT":
                                o, u = what, t_use[kind, what]
                                act.wait_ge(t_full, u + 1)
                                if o >= 2:
                                    act.wait_ge(r_full, r_use["OP", o - 2] + 1)
                                act.activation(oT_hi[:, o % 2, :], T[u % 2][:, 0:HID], ACT.Copy).then_inc(t_hi, 1)
                                act.activation(o_half[:, o % 2, :], o_sum[:, o % 2, :], ACT.Square,
                                               scale=float(2 * D) ** -0.5, accum_out=msq[:, o % 4:o % 4 + 1])\
                                   .then_inc(msq_ready, 1)
                            elif kind == "QP":
                                q_high(what)
                            for d, m, j in exps:
                                s, _, c, w, _ = duo_chunks(d)[j]
                                q, k = CHUNKS * d + j, s_use(d, m, j)
                                act.wait_ge(neg_ready, 2 * (2 * d + m) + s + 1)
                                if m == 0 and q >= E1_SLOTS:
                                    act.wait_ge(t_full, t_use["T", divmod(q - E1_SLOTS, CHUNKS)] + 1)
                                if m == 1 and q >= E2_SLOTS:
                                    act.wait_ge(p_ready, q - E2_SLOTS + 1)
                                e = e1[:, q % E1_SLOTS, 0:w] if m == 0 else e2[:, q % E2_SLOTS, 0:w]
                                act.activation(e, S[k % NS][:, 0:w], ACT.Exp, bias=negmx[:, d % 2, m, s:s + 1],
                                               accum_out=ssum[:, d % 4, s, m, c:c + 1]).then_inc(s_act, 1)

                    @block.vector
                    def _(dve):
                        n_ratio = 0

                        def q_low(what):
                            u, s, m = what
                            dve.wait_ge(r_hi, n_qp[what] + 1)
                            dve.scalar_tensor_tensor(out=q_lo[:, u % 2, s, m, :], in0=R[:, 0:HID],
                                                     scalar=bqk[:, 2 * s + m:2 * s + m + 1],
                                                     in1=q_hi[:, u % 2, s, m, :].bitcast(F32),
                                                     op0=ALU.add, op1=ALU.subtract).then_inc(r_free, 1)

                        dve.tensor_scalar(bqk[:, 0:4], bqk_raw[:, 0:4], SCALE, None, ALU.mult).then_inc(b_ready, 1)
                        dve.tensor_copy(bqk[:, 4:6], bqk_raw[:, 4:6]).then_inc(b_ready, 1)
                        dve.tensor_scalar(subln_s[:, :], subln_col[:, :], 1.0 - LAMBDA_INIT, None, ALU.mult)\
                           .then_inc(b_ready, 1)
                        for u in range(4):
                            dve.wait_ge(t_hi, u + 1)
                            src = T[u % 2][:, :].rearrange("p (c n) -> p c n", c=CT)
                            hi, lo = (wq_hi, wq_lo) if u < 2 else (wkv_hi, wkv_lo)
                            cols = slice(u % 2 * HID, (u % 2 + 1) * HID)
                            dve.scalar_tensor_tensor(out=lo[:, :, cols], in0=src, scalar=SCALE if u < 2 else 1.0,
                                                     in1=hi[:, :, cols].bitcast(F32), op0=ALU.mult,
                                                     op1=ALU.subtract).then_inc(t_lo, 1)
                        dve.wait_ge(b_ready, 3)
                        for s in range(2):
                            dve.wait_ge(t_hi, 5 + s)
                            for et in range(CT):
                                ins = dve.scalar_tensor_tensor(
                                    out=wo_lo[:, s, et, :], in0=T[s][:, et * HID:(et + 1) * HID],
                                    scalar=subln_s[:, et:et + 1], in1=wo_hi[:, s, et, :].bitcast(F32),
                                    op0=ALU.mult, op1=ALU.subtract)
                            ins.then_inc(t_lo, 1)
                        for k in range(K_USES):
                            m, c = divmod(k, 4)
                            cols = slice(c * BANK, (c + 1) * BANK)
                            dve.wait_ge(s_act, k + 1)
                            dve.scalar_tensor_tensor(out=k_lo[:, m, cols], in0=S[k % NS][:, :],
                                                     scalar=bqk[:, 4 + m:5 + m], in1=k_hi[:, m, cols].bitcast(F32),
                                                     op0=ALU.add, op1=ALU.subtract).then_inc(s_dve, 1)
                            if k < 4:
                                q_low((0, k // 2, k % 2))
                        for v in range(KV_USES - K_USES):
                            dve.wait_ge(s_full, K_USES + v + 1)
                            if v >= 2:
                                dve.wait_ge(v_lo, v - 1)
                            dve.tensor_tensor(e1[:, v % 2, :], S[v % NS][:, :],
                                              bv[:, :, :].rearrange("p t n -> p (t n)"), ALU.add).then_inc(s_dve, 1)

                        for kind, what, _, ratios, _ in steps:
                            if kind == "S":
                                d, m, j = what
                                s, _, c, w, last = duo_chunks(d)[j]
                                k = s_use(d, m, j)
                                dve.wait_ge(s_full, k + 1)
                                dve.tensor_reduce(mx[:, d % 2, m, s, c:c + 1], S[k % NS][:, 0:w], X, ALU.max)\
                                   .then_inc(s_dve, 1)
                                if last:
                                    dve.wait_ge(s_dve, k + 1)
                                    dve.tensor_reduce(negmx[:, d % 2, m, s:s + 1], mx[:, d % 2, m, s, 0:c + 1], X,
                                                      ALU.max, negate=True).then_inc(neg_ready, 1)
                            elif kind == "T":
                                d, j = what
                                w, q, u = duo_chunks(d)[j][3], CHUNKS * d + j, t_use[kind, what]
                                dve.wait_ge(t_hi, u + 1)
                                dve.tensor_tensor(pT_lo[:, q % 2, 0:w], T[u % 2][:, 0:w],
                                                  pT_hi[:, q % 2, 0:w].bitcast(F32), ALU.subtract).then_inc(t_lo, 1)
                            elif kind == "PV":
                                d, j = what
                                s, _, _, _, last = duo_chunks(d)[j]
                                if last:
                                    o = 2 * d + s
                                    dve.wait_ge(o_half_ready, o + 1)
                                    if o >= 2:
                                        dve.wait_ge(t_full, t_use["OT", o - 2] + 1)
                                        dve.wait_ge(msq_ready, o - 1)
                                    dve.tensor_tensor(o_sum[:, o % 2, :], O[:, 0:HID], o_half[:, o % 2, :], ALU.add)\
                                       .then_inc(o_ready, 1)
                            elif kind == "OT":
                                o, u = what, t_use[kind, what]
                                dve.wait_ge(t_hi, u + 1)
                                dve.tensor_tensor(oT_lo[:, o % 2, :], T[u % 2][:, 0:HID],
                                                  oT_hi[:, o % 2, :].bitcast(F32), ALU.subtract).then_inc(t_lo, 1)
                            elif kind == "QP":
                                q_low(what)
                            elif kind == "OP":
                                o, u = what, r_use[kind, what]
                                i = TILES - 1 - o // 2 if o % 2 == 0 else o // 2
                                dve.wait_ge(r_full, u + 1)
                                dve.wait_ge(rms_ready, o + 1)
                                dve.wait_ge(r_free, u)
                                dve.scalar_tensor_tensor(out=acc[:, i, :], in0=R[:, 0:HID],
                                                         scalar=rms[:, o % 4:o % 4 + 1], in1=acc[:, i, :],
                                                         op0=ALU.mult, op1=ALU.add).then_inc(r_free, 1)
                            for d, s in ratios:
                                chunks = duo_chunks(d)
                                nch = sum(ch[0] == s for ch in chunks)
                                last_j = max(j for j, ch in enumerate(chunks) if ch[0] == s)
                                dve.wait_ge(s_act, s_use(d, 1, last_j) + 1)
                                dve.tensor_reduce(s12[:, d % 4, s, :], ssum[:, d % 4, s, :, 0:nch], X, ALU.add)\
                                   .then_inc(ratio_step, 1)
                                dve.wait_ge(ratio_step, n_ratio + 1)
                                dve.reciprocal(inv_s2[:, d % 4, s:s + 1], s12[:, d % 4, s, 1:2]).then_inc(ratio_step, 1)
                                dve.wait_ge(ratio_step, n_ratio + 2)
                                n_ratio += 2
                                dve.tensor_scalar(ratio[:, d % 4, s:s + 1], s12[:, d % 4, s, 0:1],
                                                  inv_s2[:, d % 4, s:s + 1], neg_lam[:, 0:1], ALU.mult, ALU.mult)\
                                   .then_inc(ratio_ready, 1)

                    @block.gpsimd
                    def _(pool):
                        for v in range(KV_USES - K_USES):
                            pool.wait_ge(s_act, K_USES + v + 1)
                            pool.tensor_tensor(v_hl[:, 2 * v:2 * v + 2, HID:2 * HID],
                                               e1[:, v % 2, :].rearrange("p (t n) -> p t n", t=2),
                                               v_hl[:, 2 * v:2 * v + 2, 0:HID].bitcast(F32), ALU.subtract)\
                                .then_inc(v_lo, 1)

                        def mix(d, j):
                            s, _, _, w, _ = duo_chunks(d)[j]
                            q = CHUNKS * d + j
                            a, b = e1[:, q % E1_SLOTS, 0:w], e2[:, q % E2_SLOTS, 0:w]
                            pool.wait_ge(ratio_ready, 2 * d + s + 1)
                            pool.tensor_scalar(b, b, ratio[:, d % 4, s:s + 1], 0.0, ALU.mult, ALU.add)\
                                .then_inc(e2_scaled, 1)
                            pool.wait_ge(e2_scaled, q + 1)
                            pool.tensor_tensor(a, a, b, ALU.add).then_inc(p_ready, 1)

                        def norm(o):
                            d, s, c = o // 2, o % 2, slice(o % 4, o % 4 + 1)
                            s1 = s12[:, d % 4, s, 0:1]
                            pool.wait_ge(msq_ready, o + 1)
                            pool.tensor_tensor(rms_a[:, c], s1, s1, ALU.mult).then_inc(rms_step, 1)
                            pool.wait_ge(rms_step, 2 * o + 1)
                            pool.tensor_scalar(rms_b[:, c], rms_a[:, c], EPS, msq[:, c], ALU.mult, ALU.add)\
                                .then_inc(rms_step, 1)
                            pool.wait_ge(rms_step, 2 * o + 2)
                            if o >= 4:
                                pool.wait_ge(r_free, r_use["OP", o - 4] + 1)
                            pool.tensor_tensor(rms[:, c], rms_b[:, c], half_neg[:, 0:1], ALU.pow)\
                                .then_inc(rms_ready, 1)

                        for *_, work in steps:
                            for kind, what in work:
                                if kind == "mix":
                                    mix(*what)
                                else:
                                    norm(what)

                nc.all_engine_barrier(sems_to_clear=range(sems[0].num, sems[-1].num + 1))

        with ExitStack() as ffn:
            sf = tensors(ffn)
            wug_hi = sf("wug_hi", [P, CT, 2 * INTER], F32R)
            wug_lo = sf("wug_lo", [P, CT, 2 * INTER], F32R)
            JT = INTER // P
            wd_hl = sf("wd_hl", [P, JT, 2 * HID], F32R)
            x_res = sf("x_res", [P, TILES, HID])
            out_b_row = sf("out_b_row", [P, HID])
            x_landed, = semaphores(ffn, "x_res_landed")

            with ExitStack() as fold:
                sg = tensors(fold)
                raw = sg("raw", [P, 2 * JT, HID])
                raw_d = sg("raw_d", [P, CT, INTER])
                bf = [sg(f"bf{k}", [P, CT, INTER]) for k in range(2)]
                wt_hi = sg("wt_hi", [P, 2, CT, BANK], F32R)
                wt_lo = sg("wt_lo", [P, 2, CT, BANK], F32R)
                scol = sg("scol", [P, 2 * JT])
                sdcol = sg("sdcol", [P, CT])
                su_col = sg("su_col", [P, CT])
                sud_col = sg("sud_col", [P, JT])
                scaled_col = sg("scaled_col", [P, 2 * JT + CT])
                raw_landed = semaphores(fold, *[f"raw_landed{q}" for q in range(4)])
                (down_landed, cols_landed, cols_ready, raw_scaled, down_step, ft_full, ft_hi, ft_lo, fs_full,
                 fs_hi, fs_lo) = semaphores(
                    fold, "down_landed", "cols_landed", "cols_ready", "raw_scaled", "down_step", "ft_full", "ft_hi",
                    "ft_lo", "fs_full", "fs_hi", "fs_lo")
                block = fold.enter_context(nc.Block())

                @block.sync
                def _(sp):
                    sp.dma_start(scol[:, :], ws_ug.rearrange("(t p) -> p t", p=P)).then_inc(cols_landed, 16)
                    sp.dma_start(sdcol[:, :], ws_dp.rearrange("(t p) -> p t", p=P)).then_inc(cols_landed, 16)
                    sp.dma_start(su_col[:, :], su_ug.rearrange("(t p) -> p t", p=P)).then_inc(cols_landed, 16)
                    sp.dma_start(sud_col[:, :], su_dp.rearrange("(t p) -> p t", p=P)).then_inc(cols_landed, 16)
                    for q in range(4):
                        w = (w_up if q < 2 else w_gate).rearrange("(t p) c -> p t c", p=P)
                        sp.dma_start(raw[:, 4 * q:4 * q + 4, :], w[:, q % 2 * 4:q % 2 * 4 + 4, :])\
                          .then_inc(raw_landed[q], 16)
                    sp.dma_start(raw_d[:, :, :], w_down.rearrange("(t p) c -> p t c", p=P)).then_inc(down_landed, 16)
                    sp.dma_start(out_b_row[:, :], out_b.rearrange("(a d) -> a d", a=1).broadcast_to([P, HID]))\
                      .then_inc(x_landed, 16)
                    sp.dma_start(x_res[:, :, :], x_tiles).then_inc(x_landed, 16)
                    sp.wait_ge(x_landed, 32)

                @block.tensor
                def _(pe):
                    def turn(u):
                        if u >= 2:
                            pe.wait_ge(ft_lo, u - 1)
                        if u < 8:
                            q, ct = divmod(u, CT)
                            if ct == 0:
                                pe.wait_ge(raw_scaled, 4 * q + 4)
                            for t in range(4):
                                mm = pe.transpose(T[u % 2][:, t * P:(t + 1) * P],
                                                  raw[:, 4 * q + t, ct * P:(ct + 1) * P], ident[:, :])
                        else:
                            if u == 8:
                                pe.wait_ge(down_step, 14)
                            for k in range(2):
                                for it in range(CT):
                                    jt = 2 * (u - 8) + k
                                    mm = pe.transpose(T[u % 2][:, k * HID + it * P:k * HID + (it + 1) * P],
                                                      bf[0][:, it, jt * P:(jt + 1) * P], ident[:, :])
                        mm.then_inc(ft_full, 1)

                    def bank(k):
                        if k >= NS:
                            pe.wait_ge(fs_lo, k - NS + 1)
                        return S[k % NS]

                    turn(0)
                    turn(1)
                    for q in range(4):
                        turn(2 * q + 2)
                        turn(2 * q + 3)
                        pe.wait_ge(ft_lo, 2 * q + 2)
                        for co in range(CT):
                            b, n = bank(2 * q + co), 0
                            for ct in range(CT):
                                h = had_neg if co == 1 and ct == 1 else had
                                for w in (wt_hi, wt_lo):
                                    mm = pe.matmul(b[:, :], h[:, :], w[:, q % 2, ct, :], start=(n == 0),
                                                   stop=(n == 3))
                                    n += 1
                            mm.then_inc(fs_full, 1)
                    for u in range(8, 12):
                        if u + 2 < 12:
                            turn(u + 2)
                        pe.wait_ge(ft_lo, u + 1)
                        b = bank(u)
                        pe.matmul(b[:, :], had[:, :], wt_hi[:, u // 2 % 2, u % 2, :], start=True, stop=False)
                        pe.matmul(b[:, :], had[:, :], wt_lo[:, u // 2 % 2, u % 2, :], start=False, stop=True)\
                          .then_inc(fs_full, 1)

                def hi_of_turn(act, u):
                    act.wait_ge(ft_full, u + 1)
                    if u >= 4:
                        act.wait_ge(fs_full, u - u % 2 - 2)
                    act.activation(wt_hi[:, u // 2 % 2, u % 2, :], T[u % 2][:, :], ACT.Copy).then_inc(ft_hi, 1)

                def hi_of_fold(act, k):
                    act.wait_ge(fs_full, k + 1)
                    if k < 8:
                        q, co = divmod(k, CT)
                        act.activation(wug_hi[:, co, q * BANK:(q + 1) * BANK], S[k % NS][:, :], ACT.Copy,
                                       scale=su_col[:, co:co + 1]).then_inc(fs_hi, 1)
                    else:
                        for a in range(2):
                            jt = 2 * (k - 8) + a
                            ins = act.activation(wd_hl[:, jt, 0:HID], S[k % NS][:, a * HID:(a + 1) * HID], ACT.Copy,
                                                 scale=sud_col[:, jt:jt + 1])
                        ins.then_inc(fs_hi, 1)

                def lo_of_turn(dve, u):
                    dve.wait_ge(ft_hi, u + 1)
                    dve.tensor_tensor(wt_lo[:, u // 2 % 2, u % 2, :], T[u % 2][:, :],
                                      wt_hi[:, u // 2 % 2, u % 2, :].bitcast(F32), ALU.subtract).then_inc(ft_lo, 1)

                def lo_of_fold(dve, k):
                    dve.wait_ge(fs_hi, k + 1)
                    if k < 8:
                        q, co = divmod(k, CT)
                        dve.scalar_tensor_tensor(out=wug_lo[:, co, q * BANK:(q + 1) * BANK], in0=S[k % NS][:, :],
                                                 scalar=su_col[:, co:co + 1],
                                                 in1=wug_hi[:, co, q * BANK:(q + 1) * BANK].bitcast(F32),
                                                 op0=ALU.mult, op1=ALU.subtract).then_inc(fs_lo, 1)
                    else:
                        for a in range(2):
                            jt = 2 * (k - 8) + a
                            ins = dve.scalar_tensor_tensor(out=wd_hl[:, jt, HID:2 * HID],
                                                           in0=S[k % NS][:, a * HID:(a + 1) * HID],
                                                           scalar=sud_col[:, jt:jt + 1],
                                                           in1=wd_hl[:, jt, 0:HID].bitcast(F32),
                                                           op0=ALU.mult, op1=ALU.subtract)
                        ins.then_inc(fs_lo, 1)

                @block.scalar
                def _(act):
                    act.wait_ge(cols_landed, 64)
                    hi_of_turn(act, 0)
                    hi_of_turn(act, 1)
                    for q in range(4):
                        hi_of_turn(act, 2 * q + 2)
                        hi_of_turn(act, 2 * q + 3)
                        hi_of_fold(act, 2 * q)
                        hi_of_fold(act, 2 * q + 1)
                    for u in range(8, 12):
                        if u + 2 < 12:
                            hi_of_turn(act, u + 2)
                        hi_of_fold(act, u)

                @block.gpsimd
                def _(pool):
                    pool.wait_ge(cols_ready, 2)
                    for t in range(2 * JT):
                        if t % 4 == 0:
                            pool.wait_ge(raw_landed[t // 4], 16)
                        pool.tensor_scalar(raw[:, t, :], raw[:, t, :], scaled_col[:, t:t + 1], 0.0, ALU.mult,
                                           ALU.add).then_inc(raw_scaled, 1)

                @block.vector
                def _(dve):
                    dve.wait_ge(cols_landed, 64)
                    dve.tensor_scalar(scaled_col[:, 0:2 * JT], scol[:, :], float(HID) ** -0.5, None, ALU.mult)\
                       .then_inc(cols_ready, 1)
                    dve.tensor_scalar(scaled_col[:, 2 * JT:], sdcol[:, :], float(INTER) ** -0.5, None, ALU.mult)\
                       .then_inc(cols_ready, 1)
                    dve.wait_ge(cols_ready, 2)
                    lo_of_turn(dve, 0)
                    lo_of_turn(dve, 1)
                    dve.wait_ge(down_landed, 16)
                    for it in range(CT):
                        dve.tensor_scalar(bf[1][:, it, :], raw_d[:, it, :], scaled_col[:, 2 * JT + it:2 * JT + it + 1],
                                          None, ALU.mult).then_inc(down_step, 1)
                    n = 2
                    for stage in range(3):
                        src, dst = bf[(stage + 1) % 2], bf[stage % 2]
                        h = P << stage
                        dve.wait_ge(down_step, n)
                        for it in range(CT):
                            a = src[:, it, :].rearrange("p (n two h) -> p n two h", two=2, h=h)
                            b = dst[:, it, :].rearrange("p (n two h) -> p n two h", two=2, h=h)
                            dve.tensor_tensor(b[:, :, 0, :], a[:, :, 0, :], a[:, :, 1, :], ALU.add)\
                               .then_inc(down_step, 1)
                            dve.tensor_tensor(b[:, :, 1, :], a[:, :, 0, :], a[:, :, 1, :], ALU.subtract)\
                               .then_inc(down_step, 1)
                            n += 2
                    for q in range(4):
                        lo_of_turn(dve, 2 * q + 2)
                        lo_of_turn(dve, 2 * q + 3)
                        lo_of_fold(dve, 2 * q)
                        lo_of_fold(dve, 2 * q + 1)
                    for u in range(8, 12):
                        if u + 2 < 12:
                            lo_of_turn(dve, u + 2)
                        lo_of_fold(dve, u)

            h_hi = sf("h_hi", [P, 2, JT, BANK], F32R)
            h_lo = sf("h_lo", [P, 2, JT, BANK], F32R)
            z = sf("z", [P, 4, HID])
            gate = sf("gate", [P, 2, BANK])
            h_f = sf("h_f", [P, 2, BANK])
            stats = sf("stats4", [P, 4, 6])
            mv = sf("mv4", [P, 4, 2])
            ve = sf("ve4", [P, 4])
            rs = sf("rs4", [P, 4])
            mr = sf("mr4", [P, 4])
            stats2 = sf("stats5", [P, 4, 6])
            mv2 = sf("mv5", [P, 4, 2])
            ve2 = sf("ve5", [P, 4])
            rs2 = sf("rs5", [P, 4])
            d_half = sf("d_half", [P, 2, HID])
            d_sum = sf("d_sum", [P, 2, HID])
            d_out = sf("d_out", [P, 2, HID])
            st3 = sf("st6", [P, 2, 6])
            mv3 = sf("mv6", [P, 2, 2])
            ve3 = sf("ve6", [P, 2])
            rs3 = sf("rs6", [P, 2])
            mr3 = sf("mr6", [P, 2])
            (y_ready, y_step, y_rstd_step, y_rstd, x2_stats, z_rstd, z_ready, z_full, z_hi, z_lo, g_full, u_full,
             g_act, h_ready, h_hi_ready, h_lo_ready, d_full, d_half_ready, d_stats, d_rstd, d_final,
             stored_even, stored_odd, d_step, pool_step) = semaphores(
                ffn, "y_ready", "y_step", "y_rstd_step", "y_rstd", "x2_stats", "z_rstd", "z_ready", "z_full", "z_hi",
                "z_lo", "g_full", "u_full", "g_act", "h_ready", "h_hi_ready", "h_lo_ready", "d_full",
                "d_half_ready", "d_stats", "d_rstd", "d_final", "stored_even", "stored_odd", "d_step",
                "pool_step")
            stored = (stored_even, stored_odd)
            NC = SEQ // BANK
            D_BANKS = (O, R)
            block = ffn.enter_context(nc.Block())

            order = []
            for c in range(NC):
                order.append(("UG", c))
                if c >= 1:
                    order.append(("DN", c - 1))
            order.append(("DN", NC - 1))

            @block.sync
            def _(sp):
                for t in range(TILES):
                    sp.wait_ge(d_final, t + 1)
                    sp.dma_start(out_tiles[:, t, :], d_out[:, t % 2, :]).then_inc(stored[t % 2], 16)
                for parity in range(2):
                    sp.wait_ge(stored[parity], 16 * (TILES // 2))

            @block.tensor
            def _(pe):
                def turn_z(c):
                    pe.wait_ge(z_ready, 4 * c + 4)
                    for ct in range(CT):
                        u = CT * c + ct
                        if u >= 2:
                            pe.wait_ge(z_lo, u - 1)
                        for t in range(4):
                            mm = pe.transpose(T[u % 2][:, t * P:(t + 1) * P], z[:, t, ct * P:(ct + 1) * P],
                                              ident[:, :])
                        mm.then_inc(z_full, 1)

                turn_z(0)
                for kind, c in order:
                    if kind == "UG":
                        pe.wait_ge(z_lo, CT * c + CT)
                        for jt in range(JT):
                            k = JT * c + jt
                            for part, bank, full in ((1, S[2 * (k % 2)], g_full), (0, S[2 * (k % 2) + 1], u_full)):
                                if k >= 2:
                                    pe.wait_ge(g_act if part else h_ready, k - 1)
                                col, n = part * INTER + jt * P, 0
                                for ct in range(CT):
                                    for w, x in ((wug_hi, xT_hi), (wug_hi, xT_lo), (wug_lo, xT_hi)):
                                        mm = pe.matmul(bank[:, :], w[:, ct, col:col + P],
                                                       x[:, ct, c * BANK:(c + 1) * BANK], start=(n == 0),
                                                       stop=(n == 5))
                                        n += 1
                                mm.then_inc(full, 1)
                        if c + 1 < NC:
                            turn_z(c + 1)
                    else:
                        pe.wait_ge(h_lo_ready, JT * c + JT)
                        for tt in range(QB):
                            t = QB * c + tt
                            bank = D_BANKS[t % 2]
                            if t >= 2:
                                pe.wait_ge(d_step, t - 1)
                            for jt in range(JT):
                                pe.matmul(bank[:, :], h_hi[:, c % 2, jt, tt * P:(tt + 1) * P], wd_hl[:, jt, :],
                                          start=(jt == 0), stop=False)
                                mm = pe.matmul(bank[:, 0:HID], h_lo[:, c % 2, jt, tt * P:(tt + 1) * P],
                                               wd_hl[:, jt, 0:HID], start=False, stop=(jt == JT - 1))
                            mm.then_inc(d_full, 1)

            @block.scalar
            def _(act):
                def hi_z(c):
                    for ct in range(CT):
                        u = CT * c + ct
                        act.wait_ge(z_full, u + 1)
                        act.activation(xT_hi[:, ct, c * BANK:(c + 1) * BANK], T[u % 2][:, :], ACT.Copy)\
                           .then_inc(z_hi, 1)

                hi_z(0)
                for kind, c in order:
                    if kind == "UG":
                        for jt in range(JT + 1):
                            k = JT * c + jt
                            if jt < JT:
                                act.wait_ge(g_full, k + 1)
                                if k >= 2:
                                    act.wait_ge(h_ready, k - 1)
                                act.activation(gate[:, k % 2, :], S[2 * (k % 2)][:, :], ACT.Silu).then_inc(g_act, 1)
                            if jt >= 1:
                                act.wait_ge(h_ready, k)
                                if c >= 2:
                                    act.wait_ge(d_full, QB * (c - 1))
                                act.activation(h_hi[:, c % 2, jt - 1, :], h_f[:, (k - 1) % 2, :], ACT.Copy)\
                                   .then_inc(h_hi_ready, 1)
                        if c + 1 < NC:
                            hi_z(c + 1)
                    else:
                        for t in range(QB * c, QB * c + QB):
                            act.wait_ge(d_full, t + 1)
                            if t >= 2:
                                act.wait_ge(d_step, t - 1)
                            act.activation(d_half[:, t % 2, :], D_BANKS[t % 2][:, HID:2 * HID], ACT.Copy)\
                               .then_inc(d_half_ready, 1)

            @block.vector
            def _(dve):
                count = {"y": 0, "d": 0}

                def norms(c):
                    tiles = range(4 * c, 4 * c + 4)
                    dve.wait_ge(y_ready, c + 1)
                    for t in tiles:
                        dve.bn_stats(stats[:, t % 4, :], acc[:, t, :]).then_inc(y_step, 1)
                    count["y"] += 4
                    dve.wait_ge(y_step, count["y"])
                    for t in tiles:
                        dve.bn_aggr(mv[:, t % 4, :], stats[:, t % 4, :]).then_inc(y_step, 1)
                    count["y"] += 4
                    dve.wait_ge(y_rstd, c + 1)
                    for t in tiles:
                        dve.scalar_tensor_tensor(out=acc[:, t, :], in0=acc[:, t, :], scalar=rs[:, t % 4:t % 4 + 1],
                                                 in1=x_res[:, t, :], op0=ALU.mult, op1=ALU.add).then_inc(y_step, 1)
                    count["y"] += 4
                    dve.wait_ge(y_step, count["y"])
                    for t in tiles:
                        dve.tensor_scalar(acc[:, t, :], acc[:, t, :], mr[:, t % 4:t % 4 + 1], None, ALU.subtract)\
                           .then_inc(y_step, 1)
                    count["y"] += 4
                    dve.wait_ge(y_step, count["y"])
                    for t in tiles:
                        dve.bn_stats(stats2[:, t % 4, :], acc[:, t, :]).then_inc(y_step, 1)
                    count["y"] += 4
                    dve.wait_ge(y_step, count["y"])
                    for t in tiles:
                        dve.bn_aggr(mv2[:, t % 4, :], stats2[:, t % 4, :]).then_inc(y_step, 1)
                    count["y"] += 4
                    dve.wait_ge(z_rstd, c + 1)
                    if c >= 1:
                        dve.wait_ge(z_full, CT * c)
                    for t in tiles:
                        dve.tensor_scalar(z[:, t % 4, :], acc[:, t, :], mv2[:, t % 4, 0:1], rs2[:, t % 4:t % 4 + 1],
                                          ALU.subtract, ALU.mult).then_inc(z_ready, 1)

                def lo_z(c):
                    for ct in range(CT):
                        u = CT * c + ct
                        dve.wait_ge(z_hi, u + 1)
                        dve.tensor_tensor(xT_lo[:, ct, c * BANK:(c + 1) * BANK], T[u % 2][:, :],
                                          xT_hi[:, ct, c * BANK:(c + 1) * BANK].bitcast(F32), ALU.subtract)\
                           .then_inc(z_lo, 1)

                def finish(t):
                    dve.wait_ge(d_rstd, t + 1)
                    if t >= 2:
                        dve.wait_ge(stored[t % 2], 16 * (t // 2))
                    dve.scalar_tensor_tensor(out=d_out[:, t % 2, :], in0=d_sum[:, t % 2, :],
                                             scalar=rs3[:, t % 2:t % 2 + 1], in1=acc[:, t, :], op0=ALU.mult,
                                             op1=ALU.add).then_inc(d_stats, 1)
                    count["d"] += 1
                    dve.wait_ge(d_stats, count["d"])
                    dve.tensor_scalar(d_out[:, t % 2, :], d_out[:, t % 2, :], mr3[:, t % 2:t % 2 + 1], None,
                                      ALU.subtract).then_inc(d_final, 1)

                norms(0)
                lo_z(0)
                for kind, c in order:
                    if kind == "UG":
                        if c + 1 < NC:
                            norms(c + 1)
                        for jt in range(JT):
                            k = JT * c + jt
                            dve.wait_ge(g_act, k + 1)
                            dve.wait_ge(u_full, k + 1)
                            if k >= 2:
                                dve.wait_ge(h_lo_ready, k - 1)
                            dve.tensor_tensor(h_f[:, k % 2, :], S[2 * (k % 2) + 1][:, :], gate[:, k % 2, :],
                                              ALU.mult).then_inc(h_ready, 1)
                        if c + 1 < NC:
                            lo_z(c + 1)
                    else:
                        for t in range(QB * c, QB * c + QB):
                            dve.wait_ge(d_half_ready, t + 1)
                            if t >= 2:
                                dve.wait_ge(d_final, t - 1)
                            dve.tensor_tensor(d_sum[:, t % 2, :], D_BANKS[t % 2][:, 0:HID], d_half[:, t % 2, :],
                                              ALU.add).then_inc(d_step, 1)
                            dve.wait_ge(d_step, t + 1)
                            dve.bn_stats(st3[:, t % 2, :], d_sum[:, t % 2, :]).then_inc(d_stats, 1)
                            count["d"] += 1
                            dve.wait_ge(d_stats, count["d"])
                            dve.bn_aggr(mv3[:, t % 2, :], st3[:, t % 2, :]).then_inc(d_stats, 1)
                            count["d"] += 1
                            dve.wait_ge(d_stats, count["d"])
                            if t >= 1:
                                finish(t - 1)
                finish(TILES - 1)

            def planned_d_counts():
                n, out_ = 0, []
                for t in range(TILES):
                    n += 2
                    out_.append(n)
                    if t >= 1:
                        n += 1
                return out_

            @block.gpsimd
            def _(pool):
                step = 0
                dc = planned_d_counts()

                def inverse_std(dst, tmp, var, w):
                    nonlocal step
                    pool.tensor_scalar(tmp, var, 1.0, EPS, ALU.mult, ALU.add).then_inc(pool_step, 1)
                    step += 1
                    pool.wait_ge(pool_step, step)
                    pool.tensor_tensor(dst, tmp, half_neg[:, 0:w], ALU.pow).then_inc(pool_step, 1)
                    step += 1
                    pool.wait_ge(pool_step, step)

                def norms(c):
                    pool.wait_ge(y_step, 24 * c + 8)
                    inverse_std(rs[:, :], ve[:, :], mv[:, :, 1], 4)
                    pool.tensor_tensor(mr[:, :], rs[:, :], mv[:, :, 0], ALU.mult).then_inc(y_rstd, 1)
                    pool.wait_ge(y_step, 24 * c + 24)
                    pool.tensor_scalar(ve2[:, :], mv2[:, :, 1], 1.0, EPS, ALU.mult, ALU.add).then_inc(pool_step, 1)
                    nonlocal step
                    step += 1
                    pool.wait_ge(pool_step, step)
                    pool.tensor_tensor(rs2[:, :], ve2[:, :], half_neg[:, :], ALU.pow).then_inc(z_rstd, 1)

                for c in range(NC):
                    for t in range(4 * c, 4 * c + 4):
                        ins = pool.tensor_tensor(acc[:, t, :], acc[:, t, :], out_b_row[:, :], ALU.add)
                    ins.then_inc(y_ready, 1)
                    if c == 0:
                        norms(0)
                for kind, c in order:
                    if kind == "UG":
                        if c + 1 < NC:
                            norms(c + 1)
                        for jt in range(JT):
                            k = JT * c + jt
                            pool.wait_ge(h_hi_ready, k + 1)
                            pool.tensor_tensor(h_lo[:, c % 2, jt, :], h_f[:, k % 2, :],
                                               h_hi[:, c % 2, jt, :].bitcast(F32), ALU.subtract)\
                                .then_inc(h_lo_ready, 1)
                    else:
                        for t in range(QB * c, QB * c + QB):
                            b = slice(t % 2, t % 2 + 1)
                            pool.wait_ge(d_stats, dc[t])
                            inverse_std(rs3[:, b], ve3[:, b], mv3[:, t % 2, 1:2], 1)
                            pool.tensor_tensor(mr3[:, b], rs3[:, b], mv3[:, t % 2, 0:1], ALU.mult)\
                                .then_inc(d_rstd, 1)


_INS = ['L0_attn_hidden_states', 'L0_attn_Wqkv_w', 'L0_attn_Wqkv_b', 'L0_attn_lambda_q1', 'L0_attn_lambda_k1',
        'L0_attn_lambda_q2', 'L0_attn_lambda_k2', 'L0_attn_subln_w', 'L0_attn_out_w', 'L0_attn_out_b',
        'L0_ffn_SU_ug', 'L0_ffn_SU_dp', 'L0_ffn_Wscale_ug', 'L0_ffn_Wscale_dp', 'L0_ffn_W_up', 'L0_ffn_W_gate',
        'L0_ffn_W_down']


def kernel(**inputs):
    import numpy as _np
    import concourse.bacc as _bacc
    from concourse import mybir as _mybir
    from concourse.bass_utils import run_bass_kernel_spmd as _run

    nc = _bacc.Bacc("TRN2", target_bir_lowering=False, num_devices=1)
    arrays, args = {}, []
    for name in _INS:
        a = _np.ascontiguousarray(inputs[name])
        arrays[f"in_{name}_dram"] = a
        args.append(nc.dram_tensor(f"in_{name}_dram", a.shape, _mybir.dt.from_np(a.dtype), kind="ExternalInput").ap())
    out = nc.dram_tensor("out_0_dram", (1, SEQ, HID), _mybir.dt.float32, kind="ExternalOutput").ap()
    build(nc, *args, out)
    r = _run(nc, [arrays], core_ids=[0])
    return r.results[0]["out_0_dram"]
```

```python
import math
from contextlib import ExitStack

import concourse.bass as bass
from concourse import mybir

F32 = mybir.dt.float32
F32R = mybir.dt.float32r
BF16 = mybir.dt.bfloat16
ALU = mybir.AluOpType
ACT = mybir.ActivationFunctionType
X = mybir.AxisListType.X

P = 128
SEQ = 2048
HID = 256
D = 128
NQH = 16
NKH = 8
GROUPS = NKH // 2
INTER = 1024
TILES = SEQ // P
CT = HID // P
LAMBDA_INIT = 0.8 - 0.6 * math.exp(-0.3 * 1)
SCALE = float(D) ** -0.5
EPS = 1e-5
BANK = 512
QB = BANK // P
DUOS = TILES
CHUNKS = 5
NS = 4
E1_SLOTS = 2 * CHUNKS
E2_SLOTS = CHUNKS
MASKED = -1e30
HALVES = ('STSOSSTPSoTTPQPTP', 'STSOSSTPSoTPQTPTP')
SMALL_IN_R = False
PT_SLOTS = 3
DVE_MIXES = (1,)
EXPS_AT = {'PV': 2, 'OT': 0, 'QP': 0, 'T': 0, 'S': 2, 'OP': 0}
FACTOR_LAG = 3
MIXES_A_STEP = 1


def duo_chunks(d):
    out = []
    for n, (i, s) in enumerate(sorted(((TILES - 1 - d, 0), (d, 1)))):
        keys = (i + 1) * P
        for c in range(-(-keys // BANK)):
            w = min(BANK, keys - c * BANK)
            out.append((2 * d + n, s, i, c, w, (c + 1) * BANK >= keys))
    assert len(out) == CHUNKS
    return out


def attention_steps():
    steps, exps_due, factors_due, mixes_due = [], [], [], []
    to_turn, to_project = [], []

    def emit(kind, what):
        n = len(steps)
        exps = [exps_due.pop(0)[0] for _ in range(EXPS_AT.get(kind, 1))
                if exps_due and exps_due[0][1] < n]
        factors = [f for f, at in factors_due if at <= n]
        factors_due[:] = [x for x in factors_due if x[1] > n]
        mixes = [mixes_due.pop(0) for _ in range(MIXES_A_STEP) if mixes_due]
        assert kind != "T" or what not in mixes + mixes_due
        steps.append((kind, what, exps, factors, mixes))
        for d, m, j in exps:
            if m == 1 and duo_chunks(d)[j][5]:
                factors_due.append((duo_chunks(d)[j][0], n + FACTOR_LAG))
        for o in factors:
            mixes_due.extend((o // 2, j) for j, ch in enumerate(duo_chunks(o // 2)) if ch[0] == o)
        if kind == "S":
            d, m, j = what
            o, last = duo_chunks(d)[j][0], duo_chunks(d)[j][5]
            if last:
                exps_due.extend(((d, m, jj), n) for jj, ch in enumerate(duo_chunks(d)) if ch[0] == o)
        if kind == "PV" and duo_chunks(what[0])[what[1]][5]:
            to_turn.append(duo_chunks(what[0])[what[1]][0])
        if kind == "OT":
            to_project.append(what)

    def pv_part(h):
        db = (h - 3) // 2 if h % 2 else (h - 4) // 2
        if not 0 <= db < DUOS:
            return []
        widths = [c[4] for c in duo_chunks(db)]
        cut = min(range(1, CHUNKS), key=lambda n: abs(sum(widths[:n]) - sum(widths[n:])))
        return [(db, j) for j in (range(cut) if h % 2 else range(cut, CHUNKS))]

    for h in range(2 * DUOS + 3):
        d, m = divmod(h, 2)
        scores = [("S", (d, m, j)) for j in range(CHUNKS)] if d < DUOS else []
        part = pv_part(h)
        turns, products = [("T", x) for x in part], [("PV", x) for x in part]
        extra = [("QP", (h // 4 + 1, h % 4 // 2, h % 2))] if h // 4 + 1 < DUOS // 2 else []
        for what in HALVES[m]:
            if what == "o":
                if to_turn:
                    emit("OT", to_turn.pop(0))
            elif what == "O":
                if to_project:
                    emit("OP", to_project.pop(0))
            else:
                queue = {"T": turns, "S": scores, "P": products, "Q": extra}[what]
                if queue:
                    emit(*queue.pop(0))
        for what in (*turns, *scores, *products):
            emit(*what)
    while exps_due or factors_due or mixes_due:
        emit("END", None)
    for what in to_turn:
        emit("OT", what)
    for what in to_project:
        emit("OP", what)
    return steps


def build(nc, hidden, wqkv, bqkv, lq1, lk1, lq2, lk2, subln, out_w, out_b, su_ug, su_dp, ws_ug, ws_dp,
          w_up, w_gate, w_down, out):
    x_tiles = hidden[0].rearrange("(t p) c -> p t c", p=P)
    out_tiles = out[0].rearrange("(t p) c -> p t c", p=P)
    K0 = NQH * D
    V0 = K0 + NKH * D
    steps = attention_steps()

    with ExitStack() as whole:
        def tensors(stack):
            return lambda name, shape, dt=F32: stack.enter_context(nc.sbuf_tensor(name, shape, dt))

        def semaphores(stack, *names):
            return [stack.enter_context(nc.semaphore(n)) for n in names]

        sb = tensors(whole)
        whole.enter_context(nc.allow_non_contiguous_dma(reason="short columns of biases and scales"))
        S = [whole.enter_context(nc.psum_tensor(f"score_bank{b}", [P, BANK], F32)) for b in range(NS)]
        T = [whole.enter_context(nc.psum_tensor(f"turn_bank{b}", [P, BANK], F32)) for b in range(2)]
        O = whole.enter_context(nc.psum_tensor("pv_bank", [P, BANK], F32))
        R = whole.enter_context(nc.psum_tensor("proj_bank", [P, BANK], F32))

        xT_hi = sb("xT_hi", [P, CT, SEQ], F32R)
        xT_lo = sb("xT_lo", [P, CT, SEQ], F32R)
        acc = sb("acc", [P, TILES, HID])
        ident = sb("ident", [P, P])
        ident_bf = sb("ident_bf", [P, P], BF16)
        mask_bf = sb("mask_bf", [P, P], BF16)
        half_neg = sb("half_neg", [P, 4])
        neg_one = sb("neg_one", [P, 1])
        neg_lam = sb("neg_lam", [P, 1])
        subln_col = sb("subln_col", [P, CT])

        with ExitStack() as att:
            sa = tensors(att)
            w_raw = sa("w_raw", [P, 8, HID])
            bqk_raw = sa("bqk_raw", [P, 6])
            bv = sa("bv", [P, 2, HID])

            with ExitStack() as pro:
                sp_ = tensors(pro)
                x_in = sp_("x_in", [P, TILES, HID])
                xn = sp_("xn", [P, TILES, HID])
                stats = sp_("stats", [P, TILES, 6])
                mv = sp_("mv", [P, TILES, 2])
                var_eps = sp_("var_eps", [P, TILES])
                rstd = sp_("rstd", [P, TILES])
                out_b_row = sp_("out_b_row", [P, HID])
                lam_in = sp_("lam_in", [P, 4, D])
                lam_junk = sp_("lam_junk", [P, 2, D])
                lam_dot = sp_("lam_dot", [P, 2])
                lam_exp = sp_("lam_exp", [P, 2])
                lam_diff = sp_("lam_diff", [P, 1])
                x_in_sems = semaphores(pro, *[f"x_landed{q}" for q in range(4)])
                (small_landed, out_b_landed, lam_landed, w_landed, ident_base, ident_ready, consts_ready, stats_ready,
                 rstd_step, rstd_ready, xn_ready, turned, hi_ready, lo_ready, lam_dots, lam_exps, lam_step
                 ) = semaphores(
                    pro, "small_landed", "out_b_landed", "lam_landed", "w_landed", "ident_base", "ident_ready", "consts_ready",
                    "stats_ready", "rstd_step", "rstd_ready", "xn_ready", "turned", "hi_ready", "lo_ready",
                    "lam_dots", "lam_exps", "lam_step")
                block = pro.enter_context(nc.Block())

                @block.sync
                def _(sp):
                    for q in range(4):
                        sp.dma_start(x_in[:, 4 * q:4 * q + 4, :], x_tiles[:, 4 * q:4 * q + 4, :])\
                          .then_inc(x_in_sems[q], 16)
                    sp.dma_start(out_b_row[:, :], out_b.rearrange("(a d) -> a d", a=1).broadcast_to([P, HID]))\
                      .then_inc(out_b_landed, 16)
                    for k, v in enumerate((lq1, lk1, lq2, lk2)):
                        sp.dma_start(lam_in[:, k, :], v.rearrange("(a d) -> a d", a=1).broadcast_to([P, D]))\
                          .then_inc(lam_landed, 16)
                    sp.dma_start(subln_col[:, :], subln.rearrange("(t p) -> p t", p=P)).then_inc(small_landed, 16)
                    sp.dma_start(w_raw[:, 0:4, :], wqkv[0:4 * D, :].rearrange("(r p) c -> p r c", p=P))\
                      .then_inc(w_landed, 16)
                    sp.dma_start(w_raw[:, 4:6, :], wqkv[K0:K0 + 2 * D, :].rearrange("(r p) c -> p r c", p=P))\
                      .then_inc(w_landed, 16)
                    sp.dma_start(w_raw[:, 6:8, :], wqkv[V0:V0 + 2 * D, :].rearrange("(r p) c -> p r c", p=P))\
                      .then_inc(w_landed, 16)
                    sp.dma_start(bqk_raw[:, 0:4], bqkv[0:4 * D].rearrange("(r p) -> p r", p=P))\
                      .then_inc(w_landed, 16)
                    sp.dma_start(bqk_raw[:, 4:6], bqkv[K0:K0 + 2 * D].rearrange("(r p) -> p r", p=P))\
                      .then_inc(w_landed, 16)
                    for k in range(2):
                        sp.dma_start(bv[:, k, :], bqkv[V0:V0 + HID].rearrange("(a d) -> a d", a=1)
                                     .broadcast_to([P, HID])).then_inc(w_landed, 16)
                    sp.wait_ge(small_landed, 16)
                    sp.wait_ge(w_landed, 112)

                @block.gpsimd
                def _(pool):
                    pool.memset(ident[:, :], 0.0).then_inc(ident_base, 1)
                    pool.memset(mask_bf[:, :], 0.0).then_inc(ident_base, 1)
                    pool.memset(half_neg[:, :], -0.5).then_inc(ident_base, 1)
                    pool.memset(neg_one[:, :], -1.0).then_inc(ident_base, 1)
                    pool.wait_ge(ident_base, 4)
                    pool.affine_select(out=ident[:, :], in_=ident[:, :], compare_op=ALU.not_equal, fill=1.0,
                                       base=0, pattern=[[-1, P]], channel_multiplier=1).then_inc(ident_ready, 1)
                    pool.wait_ge(ident_ready, 1)
                    pool.tensor_copy(ident_bf[:, :], ident[:, :]).then_inc(consts_ready, 1)
                    pool.affine_select(out=mask_bf[:, :], in_=mask_bf[:, :], compare_op=ALU.is_ge, fill=MASKED,
                                       base=0, pattern=[[-1, P]], channel_multiplier=1).then_inc(consts_ready, 1)
                    for q in range(4):
                        t = slice(4 * q, 4 * q + 4)
                        pool.wait_ge(stats_ready, 4 * q + 4)
                        pool.tensor_scalar(var_eps[:, t], mv[:, t, 1], 1.0, EPS, ALU.mult, ALU.add)\
                            .then_inc(rstd_step, 1)
                        pool.wait_ge(rstd_step, q + 1)
                        pool.tensor_tensor(rstd[:, t], var_eps[:, t], half_neg[:, :], ALU.pow)\
                            .then_inc(rstd_ready, 1)

                @block.vector
                def _(dve):
                    def split_x(q):
                        for ct in range(CT):
                            u = CT * q + ct
                            dve.wait_ge(hi_ready, u + 1)
                            dve.tensor_tensor(xT_lo[:, ct, q * BANK:(q + 1) * BANK], T[u % 2][:, :],
                                              xT_hi[:, ct, q * BANK:(q + 1) * BANK].bitcast(F32), ALU.subtract)\
                               .then_inc(lo_ready, 1)

                    n = 0
                    for q in range(4):
                        dve.wait_ge(x_in_sems[q], 16)
                        for t in range(4 * q, 4 * q + 4):
                            dve.bn_stats(stats[:, t, :], x_in[:, t, :]).then_inc(lam_step, 1)
                            n += 1
                            dve.wait_ge(lam_step, n)
                            dve.bn_aggr(mv[:, t, :], stats[:, t, :]).then_inc(stats_ready, 1)
                        if q > 0:
                            normalise = range(4 * q - 4, 4 * q)
                            dve.wait_ge(rstd_ready, q)
                            for t in normalise:
                                dve.tensor_scalar(xn[:, t, :], x_in[:, t, :], mv[:, t, 0:1], rstd[:, t:t + 1],
                                                  ALU.subtract, ALU.mult).then_inc(xn_ready, 1)
                            split_x(q - 1)
                    dve.wait_ge(rstd_ready, 4)
                    for t in range(12, 16):
                        dve.tensor_scalar(xn[:, t, :], x_in[:, t, :], mv[:, t, 0:1], rstd[:, t:t + 1],
                                          ALU.subtract, ALU.mult).then_inc(xn_ready, 1)
                    split_x(3)
                    dve.wait_ge(lam_landed, 64)
                    for k in range(2):
                        dve.tensor_tensor_reduce(out=lam_junk[:, k, :], in0=lam_in[:, 2 * k, :],
                                                 in1=lam_in[:, 2 * k + 1, :], scale=1.0, scalar=0.0,
                                                 op0=ALU.mult, op1=ALU.add, accum_out=lam_dot[:, k:k + 1])\
                           .then_inc(lam_dots, 1)
                    dve.wait_ge(lam_exps, 1)
                    dve.tensor_tensor(lam_diff[:, :], lam_exp[:, 1:2], lam_exp[:, 0:1], ALU.subtract)\
                       .then_inc(lam_step, 1)
                    n += 1
                    dve.wait_ge(lam_step, n)
                    dve.tensor_scalar(neg_lam[:, :], lam_diff[:, :], -LAMBDA_INIT, None, ALU.add)\
                       .then_inc(lam_step, 1)

                @block.scalar
                def _(act):
                    for q in range(4):
                        for ct in range(CT):
                            act.wait_ge(turned, CT * q + ct + 1)
                            act.activation(xT_hi[:, ct, q * BANK:(q + 1) * BANK], T[(CT * q + ct) % 2][:, :],
                                           ACT.Copy).then_inc(hi_ready, 1)
                        if q == 0:
                            act.wait_ge(out_b_landed, 16)
                        for t in range(4 * q, 4 * q + 4):
                            act.activation(acc[:, t, :], out_b_row[:, :], ACT.Copy).then_inc(consts_ready, 1)
                    act.wait_ge(lam_dots, 2)
                    act.activation(lam_exp[:, :], lam_dot[:, :], ACT.Exp).then_inc(lam_exps, 1)

                @block.tensor
                def _(pe):
                    pe.wait_ge(ident_ready, 1)
                    for q in range(4):
                        pe.wait_ge(xn_ready, 4 * q + 4)
                        for ct in range(CT):
                            u = CT * q + ct
                            if u >= 2:
                                pe.wait_ge(lo_ready, u - 1)
                            for t in range(4):
                                mm = pe.transpose(T[u % 2][:, t * P:(t + 1) * P],
                                                  xn[:, 4 * q + t, ct * P:(ct + 1) * P], ident[:, :])
                            mm.then_inc(turned, 1)

            with ExitStack() as shared:
                ss = tensors(shared)
                wkv_hi = ss("wkv_hi", [P, CT, 2 * HID], F32R)
                wkv_lo = ss("wkv_lo", [P, CT, 2 * HID], F32R)
            e2 = sa("e2", [P, E2_SLOTS, BANK])
            e1 = sa("e1", [P, E1_SLOTS, BANK])
            wo_raw = e1[:, 2:4, :]
            q_hi = sa("q_hi", [P, 2, 2, 2, HID], F32R)
            q_lo = sa("q_lo", [P, 2, 2, 2, HID], F32R)
            k_hi = sa("k_hi", [P, 2, SEQ], F32R)
            k_lo = sa("k_lo", [P, 2, SEQ], F32R)
            v_hl = sa("v_hl", [P, TILES, 2 * HID], F32R)
            pT_hi = sa("pT_hi", [P, PT_SLOTS, BANK], F32R)
            pT_lo = sa("pT_lo", [P, PT_SLOTS, BANK], F32R)
            wq_hi = sa("wq_hi", [P, CT, 4 * D], F32R)
            wq_lo = sa("wq_lo", [P, CT, 4 * D], F32R)
            wo_hi = sa("wo_hi", [P, 2, CT, HID], F32R)
            wo_lo = sa("wo_lo", [P, 2, CT, HID], F32R)
            o_half = sa("o_half", [P, 2, HID])
            o_sum = sa("o_sum", [P, 2, HID])
            oT_hi = sa("oT_hi", [P, 2, HID], F32R)
            oT_lo = sa("oT_lo", [P, 2, HID], F32R)
            bqk = sa("bqk", [P, 6])
            subln_s = sa("subln_s", [P, CT])
            mx = sa("mx", [P, 2, 2, 2, 4])
            negmx = sa("negmx", [P, 2, 2, 2])
            ssum = sa("ssum", [P, 4, 2, 2, 4])
            s12 = sa("s12", [P, 4, 2, 2])
            inv_s2 = sa("inv_s2", [P, 4, 2])
            ratio = sa("ratio", [P, 4, 2])
            msq = sa("msq", [P, 4])
            rms_a = sa("rms_a", [P, 4])
            rms_b = sa("rms_b", [P, 4])
            rms = sa("rms", [P, 4])

            names = ("wo_landed", "w_next", "b_ready", "s_full", "s_act", "s_dve", "t_full", "t_hi", "t_lo", "r_full", "r_hi",
                     "r_free", "v_lo", "neg_ready", "sums_ready", "ratio_step", "ratio_ready", "e2_scaled", "p_pool", "p_dve",
                     "pv_done", "o_half_ready", "o_ready", "msq_ready", "rms_step", "rms_ready")
            sems = semaphores(att, *names)
            (wo_landed, w_next, b_ready, s_full, s_act, s_dve, t_full, t_hi, t_lo, r_full, r_hi, r_free, v_lo, neg_ready,
             sums_ready, ratio_step, ratio_ready, e2_scaled, p_pool, p_dve, pv_done, o_half_ready, o_ready, msq_ready, rms_step,
             rms_ready) = sems
            assert [s.num for s in sems] == list(range(sems[0].num, sems[0].num + len(sems)))

            W_TURNS, KV_USES, K_USES = 6, 16, 8
            t_use, r_use, n_qp = {}, {}, {}
            for n in range(4):
                r_use["QP", (0, n // 2, n % 2)] = n
                n_qp[(0, n // 2, n % 2)] = n
            r_before, r_last = {}, ("QP", (0, 1, 1))
            for kind, what, *_ in steps:
                tile = duo_chunks(what[0])[what[1]] if kind == "PV" else None
                if not SMALL_IN_R:
                    continue
                if kind in ("QP", "OP"):
                    r_before[kind, what], r_last = r_last, (kind, what)
                elif tile and tile[0] % 2 == 0 and tile[3] == 0:
                    r_before["PV", tile[0]], r_last = r_last, ("PV", tile[0])
                elif tile and tile[0] % 2 == 0:
                    assert r_last == ("PV", tile[0])
            for kind, what, *_ in steps:
                if kind in ("T", "OT"):
                    t_use[kind, what] = W_TURNS + len(t_use)
                if kind in ("QP", "OP"):
                    r_use[kind, what] = len(r_use)
                if kind == "QP":
                    n_qp[what] = len(n_qp)

            pool_mixed, dve_mixed = [], []
            for q in range(CHUNKS * DUOS):
                on_dve = q % CHUNKS in DVE_MIXES
                pool_mixed.append((pool_mixed or [0])[-1] + (not on_dve))
                dve_mixed.append((dve_mixed or [0])[-1] + on_dve)

            def pv_bank(o):
                return R if o % 2 == 0 and SMALL_IN_R else O

            def wait_mixed(eng, q):
                if q % CHUNKS in DVE_MIXES:
                    eng.wait_ge(p_dve, dve_mixed[q])
                else:
                    eng.wait_ge(p_pool, pool_mixed[q])

            def tile_of(o):
                return next(ch[1:3] for ch in duo_chunks(o // 2) if ch[0] == o)

            def s_use(d, m, j):
                return KV_USES + CHUNKS * (2 * d + m) + j

            def q_cols(s, i):
                return (i % 2) * P

            def first_q_token(u, s):
                return (TILES - 2 - 2 * u) * P if s == 0 else 2 * u * P

            with nc.Fori(0, GROUPS) as g:
                with nc.Block() as block:

                    @block.sync
                    def _(sp):
                        sp.dma_start(wo_raw, out_w[:, bass.ds(g * (2 * HID), 2 * HID)]
                                     .rearrange("(t p) c -> p t c", p=P)).then_inc(wo_landed, 16)
                        nxt = (g + 1) % GROUPS
                        sp.wait_ge(t_full, 4)
                        sp.dma_start(w_raw[:, 0:4, :], wqkv[bass.ds(nxt * (4 * D), 4 * D), :]
                                     .rearrange("(r p) c -> p r c", p=P)).then_inc(w_next, 16)
                        sp.dma_start(w_raw[:, 4:6, :], wqkv[bass.ds(nxt * (2 * D) + K0, 2 * D), :]
                                     .rearrange("(r p) c -> p r c", p=P)).then_inc(w_next, 16)
                        sp.dma_start(w_raw[:, 6:8, :], wqkv[bass.ds(nxt * (2 * D) + V0, 2 * D), :]
                                     .rearrange("(r p) c -> p r c", p=P)).then_inc(w_next, 16)
                        sp.wait_ge(b_ready, 2)
                        sp.dma_start(bqk_raw[:, 0:4], bqkv[bass.ds(nxt * (4 * D), 4 * D)]
                                     .rearrange("(r p) -> p r", p=P)).then_inc(w_next, 16)
                        sp.dma_start(bqk_raw[:, 4:6], bqkv[bass.ds(nxt * (2 * D) + K0, 2 * D)]
                                     .rearrange("(r p) -> p r", p=P)).then_inc(w_next, 16)
                        sp.wait_ge(s_dve, KV_USES)
                        for k in range(2):
                            sp.dma_start(bv[:, k, :], bqkv[bass.ds(nxt * HID + V0, HID)]
                                         .rearrange("(a d) -> a d", a=1).broadcast_to([P, HID])).then_inc(w_next, 16)
                        sp.wait_ge(w_next, 7 * 16)

                    @block.tensor
                    def _(pe):
                        def turn_bank(u):
                            if u >= 2:
                                pe.wait_ge(t_lo, u - 1)
                            return T[u % 2]

                        def score_bank(k):
                            if k >= NS:
                                pe.wait_ge(s_act, k - NS + 1)
                                pe.wait_ge(s_dve, k - NS + 1)
                            return S[k % NS]

                        def proj_bank(use):
                            last = r_before.get(use)
                            if last and last[0] == "PV":
                                pe.wait_ge(o_ready, last[1] + 1)
                            elif last:
                                pe.wait_ge(r_free, r_use[last] + 1)
                            elif use[0] != "PV" and r_use[use] >= 1:
                                pe.wait_ge(r_free, r_use[use])
                            return R

                        def project_q(what):
                            u, s, m = what
                            bank = proj_bank(("QP", what))
                            if u == 0 and s == 0 and m == 0:
                                pe.wait_ge(t_lo, 4)
                            head, tok = (2 * s + m) * D, first_q_token(u, s)
                            n = 0
                            for ct in range(CT):
                                for w, x in ((wq_hi, xT_hi), (wq_hi, xT_lo), (wq_lo, xT_hi)):
                                    mm = pe.matmul(bank[:, 0:HID], w[:, ct, head:head + D],
                                                   x[:, ct, tok:tok + HID], start=(n == 0), stop=(n == 5))
                                    n += 1
                            mm.then_inc(r_full, 1)

                        for u in range(4):
                            bank = turn_bank(u)
                            for rr in range(2):
                                for ct in range(CT):
                                    mm = pe.transpose(bank[:, ct * HID + rr * P:ct * HID + (rr + 1) * P],
                                                      w_raw[:, 2 * u + rr, ct * P:(ct + 1) * P], ident[:, :])
                            mm.then_inc(t_full, 1)
                        pe.wait_ge(t_lo, 4)
                        for k in range(K_USES):
                            m, c = divmod(k, 4)
                            bank = score_bank(k)
                            n = 0
                            for ct in range(CT):
                                for w, x in ((wkv_hi, xT_hi), (wkv_hi, xT_lo), (wkv_lo, xT_hi)):
                                    mm = pe.matmul(bank[:, :], w[:, ct, m * D:(m + 1) * D],
                                                   x[:, ct, c * BANK:(c + 1) * BANK], start=(n == 0), stop=(n == 5))
                                    n += 1
                            mm.then_inc(s_full, 1)
                            if k < 4:
                                project_q((0, k // 2, k % 2))
                        pe.wait_ge(wo_landed, 16)
                        for s in range(2):
                            bank = turn_bank(4 + s)
                            for et in range(CT):
                                for nt in range(CT):
                                    mm = pe.transpose(bank[:, et * HID + nt * P:et * HID + (nt + 1) * P],
                                                      wo_raw[:, nt, s * HID + et * P:s * HID + (et + 1) * P],
                                                      ident[:, :])
                            mm.then_inc(t_full, 1)
                        for v in range(KV_USES - K_USES):
                            bank = score_bank(K_USES + v)
                            for tt in range(2):
                                tok, n = (2 * v + tt) * P, 0
                                for ct in range(CT):
                                    for x, w in ((xT_hi, wkv_hi), (xT_hi, wkv_lo), (xT_lo, wkv_hi)):
                                        mm = pe.matmul(bank[:, tt * HID:(tt + 1) * HID], x[:, ct, tok:tok + P],
                                                       w[:, ct, HID:2 * HID], start=(n == 0), stop=(n == 5))
                                        n += 1
                            mm.then_inc(s_full, 1)
                        pe.wait_ge(s_dve, K_USES)

                        for kind, what, *_ in steps:
                            if kind == "S":
                                d, m, j = what
                                _, s, i, c, w, diagonal = duo_chunks(d)[j]
                                if d % 2 == 0:
                                    pe.wait_ge(r_free, r_use["QP", (d // 2, s, m)] + 1)
                                bank = score_bank(s_use(d, m, j))
                                col = q_cols(s, i)
                                qh = q_hi[:, d // 2 % 2, s, m, col:col + P]
                                ql = q_lo[:, d // 2 % 2, s, m, col:col + P]
                                kh = k_hi[:, m, c * BANK:c * BANK + w]
                                kl = k_lo[:, m, c * BANK:c * BANK + w]
                                pe.matmul(bank[:, 0:w], qh, kh, start=True, stop=False)
                                if diagonal:
                                    pe.matmul(bank[:, w - P:w], ident_bf[:, :], mask_bf[:, :],
                                              start=False, stop=False)
                                pe.matmul(bank[:, 0:w], qh, kl, start=False, stop=False)
                                pe.matmul(bank[:, 0:w], ql, kh, start=False, stop=True).then_inc(s_full, 1)
                            elif kind == "T":
                                d, j = what
                                w, q = duo_chunks(d)[j][4], CHUNKS * d + j
                                wait_mixed(pe, q)
                                bank = turn_bank(t_use[kind, what])
                                for b in range(w // P):
                                    mm = pe.transpose(bank[:, b * P:(b + 1) * P],
                                                      e1[:, q % E1_SLOTS, b * P:(b + 1) * P], ident[:, :])
                                mm.then_inc(t_full, 1)
                            elif kind == "PV":
                                d, j = what
                                o, _, i, c, w, _ = duo_chunks(d)[j]
                                q = CHUNKS * d + j
                                if q == 0:
                                    pe.wait_ge(v_lo, KV_USES - K_USES)
                                bank = pv_bank(o)
                                if c == 0 and not SMALL_IN_R and o >= 1:
                                    pe.wait_ge(o_ready, o)
                                elif c == 0 and o % 2 == 0:
                                    proj_bank(("PV", o))
                                elif c == 0 and SMALL_IN_R and o >= 2:
                                    pe.wait_ge(o_ready, o - 1)
                                pe.wait_ge(t_lo, t_use["T", what] + 1)
                                for b in range(w // P):
                                    kt = c * QB + b
                                    pe.matmul(bank[:, :], pT_hi[:, q % PT_SLOTS, b * P:(b + 1) * P], v_hl[:, kt, :],
                                              start=(kt == 0), stop=False)
                                    mm = pe.matmul(bank[:, 0:HID], pT_lo[:, q % PT_SLOTS, b * P:(b + 1) * P],
                                                   v_hl[:, kt, 0:HID], start=False, stop=(kt == i))
                                mm.then_inc(pv_done, 1)
                            elif kind == "OT":
                                pe.wait_ge(o_ready, what + 1)
                                bank = turn_bank(t_use[kind, what])
                                for et in range(CT):
                                    mm = pe.transpose(bank[:, et * P:(et + 1) * P],
                                                      o_sum[:, what % 2, et * P:(et + 1) * P], ident[:, :])
                                mm.then_inc(t_full, 1)
                            elif kind == "OP":
                                o, s = what, tile_of(what)[0]
                                bank = proj_bank((kind, what))
                                pe.wait_ge(t_lo, t_use["OT", o] + 1)
                                n = 0
                                for et in range(CT):
                                    for a, w in ((oT_hi, wo_hi), (oT_hi, wo_lo), (oT_lo, wo_hi)):
                                        mm = pe.matmul(bank[:, 0:HID], a[:, o % 2, et * P:(et + 1) * P],
                                                       w[:, s, et, :], start=(n == 0), stop=(n == 5))
                                        n += 1
                                mm.then_inc(r_full, 1)
                            elif kind == "QP":
                                project_q(what)

                    @block.scalar
                    def _(act):
                        def q_high(what):
                            u, s, m = what
                            act.wait_ge(r_full, r_use["QP", what] + 1)
                            act.activation(q_hi[:, u % 2, s, m, :], R[:, 0:HID], ACT.Identity,
                                           bias=bqk[:, 2 * s + m:2 * s + m + 1]).then_inc(r_hi, 1)

                        for u in range(4):
                            act.wait_ge(t_full, u + 1)
                            src = T[u % 2][:, :].rearrange("p (c n) -> p c n", c=CT)
                            dst = wq_hi if u < 2 else wkv_hi
                            act.activation(dst[:, :, u % 2 * HID:(u % 2 + 1) * HID], src, ACT.Copy,
                                           scale=SCALE if u < 2 else 1.0).then_inc(t_hi, 1)
                        act.wait_ge(b_ready, 3)
                        for k in range(K_USES):
                            m, c = divmod(k, 4)
                            act.wait_ge(s_full, k + 1)
                            act.activation(k_hi[:, m, c * BANK:(c + 1) * BANK], S[k % NS][:, :], ACT.Identity,
                                           bias=bqk[:, 4 + m:5 + m]).then_inc(s_act, 1)
                            if k < 4:
                                q_high((0, k // 2, k % 2))
                        for s in range(2):
                            act.wait_ge(t_full, 5 + s)
                            for et in range(CT):
                                ins = act.activation(wo_hi[:, s, et, :], T[s][:, et * HID:(et + 1) * HID], ACT.Copy,
                                                     scale=subln_s[:, et:et + 1])
                            ins.then_inc(t_hi, 1)
                        for v in range(KV_USES - K_USES):
                            act.wait_ge(s_dve, K_USES + v + 1)
                            act.activation(v_hl[:, 2 * v:2 * v + 2, 0:HID],
                                           e1[:, v % 2, :].rearrange("p (t n) -> p t n", t=2), ACT.Copy)\
                               .then_inc(s_act, 1)
                        act.wait_ge(v_lo, KV_USES - K_USES)

                        def exponentials(exps):
                            for d, m, j in exps:
                                o, s, _, c, w, _ = duo_chunks(d)[j]
                                q, k = CHUNKS * d + j, s_use(d, m, j)
                                act.wait_ge(neg_ready, 4 * d + 2 * m + o % 2 + 1)
                                if m == 0 and q >= E1_SLOTS:
                                    act.wait_ge(t_full, t_use["T", divmod(q - E1_SLOTS, CHUNKS)] + 1)
                                if m == 1 and q >= E2_SLOTS:
                                    wait_mixed(act, q - E2_SLOTS)
                                e = e1[:, q % E1_SLOTS, 0:w] if m == 0 else e2[:, q % E2_SLOTS, 0:w]
                                act.activation(e, S[k % NS][:, 0:w], ACT.Exp, bias=negmx[:, d % 2, m, s:s + 1],
                                               accum_out=ssum[:, d % 4, s, m, c:c + 1]).then_inc(s_act, 1)

                        for kind, what, exps, _, _ in steps:
                            exponentials(exps)
                            if kind == "T":
                                d, j = what
                                w, q, u = duo_chunks(d)[j][4], CHUNKS * d + j, t_use[kind, what]
                                act.wait_ge(t_full, u + 1)
                                if q >= PT_SLOTS:
                                    act.wait_ge(pv_done, q - PT_SLOTS + 1)
                                act.activation(pT_hi[:, q % PT_SLOTS, 0:w], T[u % 2][:, 0:w], ACT.Copy).then_inc(t_hi, 1)
                            elif kind == "PV":
                                d, j = what
                                o, _, _, _, _, last = duo_chunks(d)[j]
                                if last:
                                    act.wait_ge(pv_done, CHUNKS * d + j + 1)
                                    if o >= 2:
                                        act.wait_ge(msq_ready, o - 1)
                                    act.activation(o_half[:, o % 2, :], pv_bank(o)[:, HID:2 * HID], ACT.Copy)\
                                       .then_inc(o_half_ready, 1)
                            elif kind == "OT":
                                o, u = what, t_use[kind, what]
                                act.wait_ge(t_full, u + 1)
                                if o >= 2:
                                    act.wait_ge(r_full, r_use["OP", o - 2] + 1)
                                act.activation(oT_hi[:, o % 2, :], T[u % 2][:, 0:HID], ACT.Copy).then_inc(t_hi, 1)
                                act.activation(o_half[:, o % 2, :], o_sum[:, o % 2, :], ACT.Square,
                                               scale=float(2 * D) ** -0.5, accum_out=msq[:, o % 4:o % 4 + 1])\
                                   .then_inc(msq_ready, 1)
                            elif kind == "QP":
                                q_high(what)

                    @block.vector
                    def _(dve):
                        def q_low(what):
                            u, s, m = what
                            dve.wait_ge(r_hi, n_qp[what] + 1)
                            dve.scalar_tensor_tensor(out=q_lo[:, u % 2, s, m, :], in0=R[:, 0:HID],
                                                     scalar=bqk[:, 2 * s + m:2 * s + m + 1],
                                                     in1=q_hi[:, u % 2, s, m, :].bitcast(F32),
                                                     op0=ALU.add, op1=ALU.subtract).then_inc(r_free, 1)

                        dve.tensor_scalar(bqk[:, 0:4], bqk_raw[:, 0:4], SCALE, None, ALU.mult).then_inc(b_ready, 1)
                        dve.tensor_copy(bqk[:, 4:6], bqk_raw[:, 4:6]).then_inc(b_ready, 1)
                        dve.tensor_scalar(subln_s[:, :], subln_col[:, :], 1.0 - LAMBDA_INIT, None, ALU.mult)\
                           .then_inc(b_ready, 1)
                        for u in range(4):
                            dve.wait_ge(t_hi, u + 1)
                            src = T[u % 2][:, :].rearrange("p (c n) -> p c n", c=CT)
                            hi, lo = (wq_hi, wq_lo) if u < 2 else (wkv_hi, wkv_lo)
                            cols = slice(u % 2 * HID, (u % 2 + 1) * HID)
                            dve.scalar_tensor_tensor(out=lo[:, :, cols], in0=src, scalar=SCALE if u < 2 else 1.0,
                                                     in1=hi[:, :, cols].bitcast(F32), op0=ALU.mult,
                                                     op1=ALU.subtract).then_inc(t_lo, 1)
                        dve.wait_ge(b_ready, 3)
                        for k in range(K_USES):
                            m, c = divmod(k, 4)
                            cols = slice(c * BANK, (c + 1) * BANK)
                            dve.wait_ge(s_act, k + 1)
                            dve.scalar_tensor_tensor(out=k_lo[:, m, cols], in0=S[k % NS][:, :],
                                                     scalar=bqk[:, 4 + m:5 + m], in1=k_hi[:, m, cols].bitcast(F32),
                                                     op0=ALU.add, op1=ALU.subtract).then_inc(s_dve, 1)
                            if k < 4:
                                q_low((0, k // 2, k % 2))
                        for s in range(2):
                            dve.wait_ge(t_hi, 5 + s)
                            for et in range(CT):
                                ins = dve.scalar_tensor_tensor(
                                    out=wo_lo[:, s, et, :], in0=T[s][:, et * HID:(et + 1) * HID],
                                    scalar=subln_s[:, et:et + 1], in1=wo_hi[:, s, et, :].bitcast(F32),
                                    op0=ALU.mult, op1=ALU.subtract)
                            ins.then_inc(t_lo, 1)
                        for v in range(KV_USES - K_USES):
                            dve.wait_ge(s_full, K_USES + v + 1)
                            if v >= 2:
                                dve.wait_ge(v_lo, v - 1)
                            dve.tensor_tensor(e1[:, v % 2, :], S[v % NS][:, :],
                                              bv[:, :, :].rearrange("p t n -> p (t n)"), ALU.add).then_inc(s_dve, 1)

                        for kind, what, _, factors, mixes in steps:
                            if kind == "S":
                                d, m, j = what
                                _, s, _, c, w, last = duo_chunks(d)[j]
                                k = s_use(d, m, j)
                                dve.wait_ge(s_full, k + 1)
                                dve.tensor_reduce(mx[:, d % 2, m, s, c:c + 1], S[k % NS][:, 0:w], X, ALU.max)\
                                   .then_inc(s_dve, 1)
                                if last:
                                    dve.wait_ge(s_dve, k + 1)
                                    dve.tensor_reduce(negmx[:, d % 2, m, s:s + 1], mx[:, d % 2, m, s, 0:c + 1], X,
                                                      ALU.max, negate=True).then_inc(neg_ready, 1)
                            elif kind == "T":
                                d, j = what
                                w, q, u = duo_chunks(d)[j][4], CHUNKS * d + j, t_use[kind, what]
                                dve.wait_ge(t_hi, u + 1)
                                dve.tensor_tensor(pT_lo[:, q % PT_SLOTS, 0:w], T[u % 2][:, 0:w],
                                                  pT_hi[:, q % PT_SLOTS, 0:w].bitcast(F32), ALU.subtract).then_inc(t_lo, 1)
                            elif kind == "PV":
                                d, j = what
                                o, _, _, _, _, last = duo_chunks(d)[j]
                                if last:
                                    dve.wait_ge(o_half_ready, o + 1)
                                    if o >= 2:
                                        dve.wait_ge(t_full, t_use["OT", o - 2] + 1)
                                        dve.wait_ge(msq_ready, o - 1)
                                    dve.tensor_tensor(o_sum[:, o % 2, :], pv_bank(o)[:, 0:HID],
                                                      o_half[:, o % 2, :], ALU.add)\
                                       .then_inc(o_ready, 1)
                            elif kind == "OT":
                                o, u = what, t_use[kind, what]
                                dve.wait_ge(t_hi, u + 1)
                                dve.tensor_tensor(oT_lo[:, o % 2, :], T[u % 2][:, 0:HID],
                                                  oT_hi[:, o % 2, :].bitcast(F32), ALU.subtract).then_inc(t_lo, 1)
                            elif kind == "QP":
                                q_low(what)
                            elif kind == "OP":
                                o, u = what, r_use[kind, what]
                                _, i = tile_of(o)
                                dve.wait_ge(r_full, u + 1)
                                dve.wait_ge(rms_ready, o + 1)
                                dve.wait_ge(r_free, u)
                                dve.scalar_tensor_tensor(out=acc[:, i, :], in0=R[:, 0:HID],
                                                         scalar=rms[:, o % 4:o % 4 + 1], in1=acc[:, i, :],
                                                         op0=ALU.mult, op1=ALU.add).then_inc(r_free, 1)
                            for o in factors:
                                d, chunks = o // 2, [ch for ch in duo_chunks(o // 2) if ch[0] == o]
                                s, nch = chunks[0][1], len(chunks)
                                last_j = max(j for j, ch in enumerate(duo_chunks(d)) if ch[0] == o)
                                dve.wait_ge(s_act, s_use(d, 1, last_j) + 1)
                                dve.tensor_reduce(s12[:, d % 4, s, :], ssum[:, d % 4, s, :, 0:nch], X, ALU.add)\
                                   .then_inc(sums_ready, 1)
                            for d, j in mixes:
                                if j in DVE_MIXES:
                                    o, s, _, _, w, _ = duo_chunks(d)[j]
                                    q = CHUNKS * d + j
                                    a, b = e1[:, q % E1_SLOTS, 0:w], e2[:, q % E2_SLOTS, 0:w]
                                    dve.wait_ge(ratio_ready, o + 1)
                                    dve.scalar_tensor_tensor(out=a, in0=b, scalar=ratio[:, d % 4, s:s + 1], in1=a,
                                                             op0=ALU.mult, op1=ALU.add).then_inc(p_dve, 1)

                    @block.gpsimd
                    def _(pool):
                        for v in range(KV_USES - K_USES):
                            pool.wait_ge(s_act, K_USES + v + 1)
                            pool.tensor_tensor(v_hl[:, 2 * v:2 * v + 2, HID:2 * HID],
                                               e1[:, v % 2, :].rearrange("p (t n) -> p t n", t=2),
                                               v_hl[:, 2 * v:2 * v + 2, 0:HID].bitcast(F32), ALU.subtract)\
                                .then_inc(v_lo, 1)

                        def factor(o):
                            d, s = o // 2, tile_of(o)[0]
                            pool.wait_ge(sums_ready, o + 1)
                            pool.tensor_tensor(inv_s2[:, d % 4, s:s + 1], s12[:, d % 4, s, 1:2], neg_one[:, :],
                                               ALU.pow).then_inc(ratio_step, 1)
                            pool.wait_ge(ratio_step, o + 1)
                            pool.tensor_scalar(ratio[:, d % 4, s:s + 1], s12[:, d % 4, s, 0:1],
                                               inv_s2[:, d % 4, s:s + 1], neg_lam[:, 0:1], ALU.mult, ALU.mult)\
                                .then_inc(ratio_ready, 1)

                        def mix(d, j):
                            o, s, _, _, w, _ = duo_chunks(d)[j]
                            q = CHUNKS * d + j
                            a, b = e1[:, q % E1_SLOTS, 0:w], e2[:, q % E2_SLOTS, 0:w]
                            pool.wait_ge(ratio_ready, o + 1)
                            pool.tensor_scalar(b, b, ratio[:, d % 4, s:s + 1], 0.0, ALU.mult, ALU.add)\
                                .then_inc(e2_scaled, 1)
                            pool.wait_ge(e2_scaled, pool_mixed[q])
                            pool.tensor_tensor(a, a, b, ALU.add).then_inc(p_pool, 1)

                        def norm(o):
                            d, s, c = o // 2, tile_of(o)[0], slice(o % 4, o % 4 + 1)
                            s1 = s12[:, d % 4, s, 0:1]
                            pool.wait_ge(msq_ready, o + 1)
                            pool.tensor_tensor(rms_a[:, c], s1, s1, ALU.mult).then_inc(rms_step, 1)
                            pool.wait_ge(rms_step, 2 * o + 1)
                            pool.tensor_scalar(rms_b[:, c], rms_a[:, c], EPS, msq[:, c], ALU.mult, ALU.add)\
                                .then_inc(rms_step, 1)
                            pool.wait_ge(rms_step, 2 * o + 2)
                            if o >= 4:
                                pool.wait_ge(r_free, r_use["OP", o - 4] + 1)
                            pool.tensor_tensor(rms[:, c], rms_b[:, c], half_neg[:, 0:1], ALU.pow)\
                                .then_inc(rms_ready, 1)

                        for kind, what, _, factors, mixes in steps:
                            for o in factors:
                                factor(o)
                            if kind == "OT":
                                norm(what)
                            for d, j in mixes:
                                if j not in DVE_MIXES:
                                    mix(d, j)

                nc.all_engine_barrier(sems_to_clear=range(sems[0].num, sems[-1].num + 1))

        with ExitStack() as ffn:
            sf = tensors(ffn)
            wug_hi = sf("wug_hi", [P, CT, 2 * INTER], F32R)
            wug_lo = sf("wug_lo", [P, CT, 2 * INTER], F32R)
            JT = INTER // P
            wd_hl = sf("wd_hl", [P, JT, 2 * HID], F32R)
            x_res = sf("x_res", [P, TILES, HID])
            z = sf("z", [P, 4, HID])
            y_stats = sf("y_stats", [P, 4, 6])
            y_mv = sf("y_mv", [P, 4, 2])
            y_var = sf("y_var", [P, 4])
            y_rs = sf("y_rs", [P, 4])
            y_mr = sf("y_mr", [P, 4])
            z_stats = sf("z_stats", [P, 4, 6])
            z_mv = sf("z_mv", [P, 4, 2])
            z_var = sf("z_var", [P, 4])
            z_rs = sf("z_rs", [P, 4])
            y_step, y_pool, y_rstd, z_rstd, z_ready, first_x_landed, x_landed = semaphores(
                ffn, "y_step", "y_pool", "y_rstd", "z_rstd", "z_ready", "first_x_landed", "x_res_landed")

            def norms(dve, c, part):
                tiles = range(4 * c, 4 * c + 4)
                if part == 0:
                    for t in tiles:
                        dve.bn_stats(y_stats[:, t % 4, :], acc[:, t, :]).then_inc(y_step, 1)
                    dve.wait_ge(y_step, 24 * c + 4)
                    for t in tiles:
                        dve.bn_aggr(y_mv[:, t % 4, :], y_stats[:, t % 4, :]).then_inc(y_step, 1)
                elif part == 1:
                    dve.wait_ge(y_rstd, c + 1)
                    for t in tiles:
                        dve.scalar_tensor_tensor(out=acc[:, t, :], in0=acc[:, t, :], scalar=y_rs[:, t % 4:t % 4 + 1],
                                                 in1=x_res[:, t, :], op0=ALU.mult, op1=ALU.add).then_inc(y_step, 1)
                    dve.wait_ge(y_step, 24 * c + 12)
                    for t in tiles:
                        dve.tensor_scalar(acc[:, t, :], acc[:, t, :], y_mr[:, t % 4:t % 4 + 1], None, ALU.subtract)\
                           .then_inc(y_step, 1)
                elif part == 2:
                    dve.wait_ge(y_step, 24 * c + 16)
                    for t in tiles:
                        dve.bn_stats(z_stats[:, t % 4, :], acc[:, t, :]).then_inc(y_step, 1)
                    dve.wait_ge(y_step, 24 * c + 20)
                    for t in tiles:
                        dve.bn_aggr(z_mv[:, t % 4, :], z_stats[:, t % 4, :]).then_inc(y_step, 1)
                else:
                    dve.wait_ge(z_rstd, c + 1)
                    for t in tiles:
                        dve.tensor_scalar(z[:, t % 4, :], acc[:, t, :], z_mv[:, t % 4, 0:1], z_rs[:, t % 4:t % 4 + 1],
                                          ALU.subtract, ALU.mult).then_inc(z_ready, 1)

            def rstds(pool, c, part):
                if part == 0:
                    pool.wait_ge(y_step, 24 * c + 8)
                    pool.tensor_scalar(y_var[:, :], y_mv[:, :, 1], 1.0, EPS, ALU.mult, ALU.add).then_inc(y_pool, 1)
                    pool.wait_ge(y_pool, 3 * c + 1)
                    pool.tensor_tensor(y_rs[:, :], y_var[:, :], half_neg[:, :], ALU.pow).then_inc(y_pool, 1)
                    pool.wait_ge(y_pool, 3 * c + 2)
                    pool.tensor_tensor(y_mr[:, :], y_rs[:, :], y_mv[:, :, 0], ALU.mult).then_inc(y_rstd, 1)
                else:
                    pool.wait_ge(y_step, 24 * c + 24)
                    pool.tensor_scalar(z_var[:, :], z_mv[:, :, 1], 1.0, EPS, ALU.mult, ALU.add).then_inc(y_pool, 1)
                    pool.wait_ge(y_pool, 3 * c + 3)
                    pool.tensor_tensor(z_rs[:, :], z_var[:, :], half_neg[:, :], ALU.pow).then_inc(z_rstd, 1)

            with ExitStack() as fold:
                sg = tensors(fold)
                raw = sg("raw", [P, 2 * JT, HID])
                raw_d = sg("raw_d", [P, CT, INTER])
                bf = [sg(f"bf{k}", [P, CT, INTER]) for k in range(2)]
                wt_hi = sg("wt_hi", [P, 2, CT, BANK], F32R)
                wt_lo = sg("wt_lo", [P, 2, CT, BANK], F32R)
                hd = [sg(f"hd{k}", [P, P]) for k in range(2)]
                had = sg("had", [P, P], F32R)
                had_neg = sg("had_neg", [P, P], F32R)
                scol = sg("scol", [P, 2 * JT])
                sdcol = sg("sdcol", [P, CT])
                su_col = sg("su_col", [P, CT])
                sud_col = sg("sud_col", [P, JT])
                scaled_col = sg("scaled_col", [P, 2 * JT + CT])
                raw_landed = semaphores(fold, *[f"raw_landed{q}" for q in range(4)])
                (down_landed, cols_landed, cols_ready, raw_scaled, raw_scaled_act, down_scaled, down_step, down_pool, ft_full, ft_hi, ft_lo, fs_full,
                 fs_hi, fs_lo, had_step) = semaphores(
                    fold, "down_landed", "cols_landed", "cols_ready", "raw_scaled", "raw_scaled_act", "down_scaled",
                    "down_step", "down_pool", "ft_full", "ft_hi",
                    "ft_lo", "fs_full", "fs_hi", "fs_lo", "had_step")
                block = fold.enter_context(nc.Block())

                @block.sync
                def _(sp):
                    sp.dma_start(scol[:, :], ws_ug.rearrange("(t p) -> p t", p=P)).then_inc(cols_landed, 16)
                    sp.dma_start(sdcol[:, :], ws_dp.rearrange("(t p) -> p t", p=P)).then_inc(cols_landed, 16)
                    sp.dma_start(su_col[:, :], su_ug.rearrange("(t p) -> p t", p=P)).then_inc(cols_landed, 16)
                    sp.dma_start(sud_col[:, :], su_dp.rearrange("(t p) -> p t", p=P)).then_inc(cols_landed, 16)
                    for q in range(4):
                        w = (w_up if q < 2 else w_gate).rearrange("(t p) c -> p t c", p=P)
                        sp.dma_start(raw[:, 4 * q:4 * q + 4, :], w[:, q % 2 * 4:q % 2 * 4 + 4, :])\
                          .then_inc(raw_landed[q], 16)
                        if q == 0:
                            sp.dma_start(x_res[:, 0:4, :], x_tiles[:, 0:4, :]).then_inc(first_x_landed, 16)
                    sp.dma_start(raw_d[:, :, :], w_down.rearrange("(t p) c -> p t c", p=P)).then_inc(down_landed, 16)
                    sp.dma_start(x_res[:, 4:, :], x_tiles[:, 4:, :]).then_inc(x_landed, 16)
                    sp.wait_ge(x_landed, 16)

                @block.tensor
                def _(pe):
                    def turn(u):
                        if u >= 2:
                            pe.wait_ge(ft_lo, u - 1)
                        if u < 8:
                            q, ct = divmod(u, CT)
                            if ct == 0:
                                pe.wait_ge(raw_scaled, 2 * q + 2)
                                pe.wait_ge(raw_scaled_act, 2 * q + 2)
                            for t in range(4):
                                mm = pe.transpose(T[u % 2][:, t * P:(t + 1) * P],
                                                  raw[:, 4 * q + t, ct * P:(ct + 1) * P], ident[:, :])
                        else:
                            if u == 8:
                                pe.wait_ge(down_step, 6)
                                pe.wait_ge(down_pool, 6)
                            for k in range(2):
                                for it in range(CT):
                                    jt = 2 * (u - 8) + k
                                    mm = pe.transpose(T[u % 2][:, k * HID + it * P:k * HID + (it + 1) * P],
                                                      bf[0][:, it, jt * P:(jt + 1) * P], ident[:, :])
                        mm.then_inc(ft_full, 1)

                    def bank(k):
                        if k >= NS:
                            pe.wait_ge(fs_lo, k - NS + 1)
                        return S[k % NS]

                    turn(0)
                    turn(1)
                    for q in range(4):
                        turn(2 * q + 2)
                        turn(2 * q + 3)
                        pe.wait_ge(ft_lo, 2 * q + 2)
                        if q == 0:
                            pe.wait_ge(had_step, 16)
                        for co in range(CT):
                            b, n = bank(2 * q + co), 0
                            for ct in range(CT):
                                h = had_neg if co == 1 and ct == 1 else had
                                for w in (wt_hi, wt_lo):
                                    mm = pe.matmul(b[:, :], h[:, :], w[:, q % 2, ct, :], start=(n == 0),
                                                   stop=(n == 3))
                                    n += 1
                            mm.then_inc(fs_full, 1)
                    for u in range(8, 12):
                        if u + 2 < 12:
                            turn(u + 2)
                        pe.wait_ge(ft_lo, u + 1)
                        b = bank(u)
                        pe.matmul(b[:, :], had[:, :], wt_hi[:, u // 2 % 2, u % 2, :], start=True, stop=False)
                        pe.matmul(b[:, :], had[:, :], wt_lo[:, u // 2 % 2, u % 2, :], start=False, stop=True)\
                          .then_inc(fs_full, 1)

                def hi_of_turn(act, u):
                    act.wait_ge(ft_full, u + 1)
                    if u >= 4:
                        act.wait_ge(fs_full, u - u % 2 - 2)
                    act.activation(wt_hi[:, u // 2 % 2, u % 2, :], T[u % 2][:, :], ACT.Copy).then_inc(ft_hi, 1)

                def hi_of_fold(act, k):
                    act.wait_ge(fs_full, k + 1)
                    if k < 8:
                        q, co = divmod(k, CT)
                        act.activation(wug_hi[:, co, q * BANK:(q + 1) * BANK], S[k % NS][:, :], ACT.Copy,
                                       scale=su_col[:, co:co + 1]).then_inc(fs_hi, 1)
                    else:
                        for a in range(2):
                            jt = 2 * (k - 8) + a
                            ins = act.activation(wd_hl[:, jt, 0:HID], S[k % NS][:, a * HID:(a + 1) * HID], ACT.Copy,
                                                 scale=sud_col[:, jt:jt + 1])
                        ins.then_inc(fs_hi, 1)

                def lo_of_turn(dve, u):
                    dve.wait_ge(ft_hi, u + 1)
                    dve.tensor_tensor(wt_lo[:, u // 2 % 2, u % 2, :], T[u % 2][:, :],
                                      wt_hi[:, u // 2 % 2, u % 2, :].bitcast(F32), ALU.subtract).then_inc(ft_lo, 1)

                def lo_of_fold(dve, k):
                    dve.wait_ge(fs_hi, k + 1)
                    if k < 8:
                        q, co = divmod(k, CT)
                        dve.scalar_tensor_tensor(out=wug_lo[:, co, q * BANK:(q + 1) * BANK], in0=S[k % NS][:, :],
                                                 scalar=su_col[:, co:co + 1],
                                                 in1=wug_hi[:, co, q * BANK:(q + 1) * BANK].bitcast(F32),
                                                 op0=ALU.mult, op1=ALU.subtract).then_inc(fs_lo, 1)
                    else:
                        for a in range(2):
                            jt = 2 * (k - 8) + a
                            ins = dve.scalar_tensor_tensor(out=wd_hl[:, jt, HID:2 * HID],
                                                           in0=S[k % NS][:, a * HID:(a + 1) * HID],
                                                           scalar=sud_col[:, jt:jt + 1],
                                                           in1=wd_hl[:, jt, 0:HID].bitcast(F32),
                                                           op0=ALU.mult, op1=ALU.subtract)
                        ins.then_inc(fs_lo, 1)

                @block.scalar
                def _(act):
                    def scale_raw(q):
                        act.wait_ge(raw_landed[q], 16)
                        for t in (4 * q, 4 * q + 1):
                            act.activation(raw[:, t, :], raw[:, t, :], ACT.Copy, scale=scaled_col[:, t:t + 1])\
                               .then_inc(raw_scaled_act, 1)

                    act.wait_ge(cols_ready, 2)
                    scale_raw(0)
                    scale_raw(1)
                    hi_of_turn(act, 0)
                    hi_of_turn(act, 1)
                    act.wait_ge(down_landed, 16)
                    for it in range(CT):
                        act.activation(bf[1][:, it, :], raw_d[:, it, :], ACT.Copy,
                                       scale=scaled_col[:, 2 * JT + it:2 * JT + it + 1]).then_inc(down_scaled, 1)
                    for q in range(4):
                        if q < 2:
                            scale_raw(q + 2)
                        hi_of_turn(act, 2 * q + 2)
                        hi_of_turn(act, 2 * q + 3)
                        hi_of_fold(act, 2 * q)
                        hi_of_fold(act, 2 * q + 1)
                    for u in range(8, 12):
                        if u + 2 < 12:
                            hi_of_turn(act, u + 2)
                        hi_of_fold(act, u)

                def butterflies(eng, it, step):
                    for stage in range(3):
                        src, dst = bf[(stage + 1) % 2], bf[stage % 2]
                        if stage == 0:
                            eng.wait_ge(down_scaled, it + 1)
                        else:
                            eng.wait_ge(step, 2 * stage)
                        a = src[:, it, :].rearrange("p (n two h) -> p n two h", two=2, h=P << stage)
                        b = dst[:, it, :].rearrange("p (n two h) -> p n two h", two=2, h=P << stage)
                        eng.tensor_tensor(b[:, :, 0, :], a[:, :, 0, :], a[:, :, 1, :], ALU.add).then_inc(step, 1)
                        eng.tensor_tensor(b[:, :, 1, :], a[:, :, 0, :], a[:, :, 1, :], ALU.subtract)\
                           .then_inc(step, 1)

                @block.gpsimd
                def _(pool):
                    def scale_raw(q):
                        pool.wait_ge(raw_landed[q], 16)
                        for t in (4 * q + 2, 4 * q + 3):
                            pool.tensor_scalar(raw[:, t, :], raw[:, t, :], scaled_col[:, t:t + 1], 0.0, ALU.mult,
                                               ALU.add).then_inc(raw_scaled, 1)

                    rstds(pool, 0, 0)
                    pool.wait_ge(cols_ready, 2)
                    scale_raw(0)
                    scale_raw(1)
                    rstds(pool, 0, 1)
                    scale_raw(2)
                    scale_raw(3)
                    butterflies(pool, 1, down_pool)

                @block.vector
                def _(dve):
                    norms(dve, 0, 0)
                    dve.wait_ge(cols_landed, 64)
                    dve.tensor_scalar(scaled_col[:, 0:2 * JT], scol[:, :], float(HID) ** -0.5, None, ALU.mult)\
                       .then_inc(cols_ready, 1)
                    dve.tensor_scalar(scaled_col[:, 2 * JT:], sdcol[:, :], float(INTER) ** -0.5, None, ALU.mult)\
                       .then_inc(cols_ready, 1)
                    src = ident
                    k = 0
                    for stage in range(7):
                        h = 1 << stage
                        dst = hd[stage % 2]
                        a = src[:, :].rearrange("p (n two h) -> p n two h", two=2, h=h)
                        b = dst[:, :].rearrange("p (n two h) -> p n two h", two=2, h=h)
                        dve.tensor_tensor(b[:, :, 0, :], a[:, :, 0, :], a[:, :, 1, :], ALU.add).then_inc(had_step, 1)
                        dve.tensor_tensor(b[:, :, 1, :], a[:, :, 0, :], a[:, :, 1, :], ALU.subtract)\
                           .then_inc(had_step, 1)
                        k += 2
                        dve.wait_ge(had_step, k)
                        src = dst
                    dve.tensor_copy(had[:, :], src[:, :]).then_inc(had_step, 1)
                    dve.tensor_scalar(had_neg[:, :], src[:, :], -1.0, None, ALU.mult).then_inc(had_step, 1)
                    dve.wait_ge(first_x_landed, 16)
                    norms(dve, 0, 1)
                    lo_of_turn(dve, 0)
                    norms(dve, 0, 2)
                    lo_of_turn(dve, 1)
                    norms(dve, 0, 3)
                    butterflies(dve, 0, down_step)
                    for q in range(4):
                        lo_of_turn(dve, 2 * q + 2)
                        lo_of_turn(dve, 2 * q + 3)
                        lo_of_fold(dve, 2 * q)
                        lo_of_fold(dve, 2 * q + 1)
                    for u in range(8, 12):
                        if u + 2 < 12:
                            lo_of_turn(dve, u + 2)
                        lo_of_fold(dve, u)

            h_hi = sf("h_hi", [P, 2, JT, BANK], F32R)
            h_lo = sf("h_lo", [P, 2, JT, BANK], F32R)
            gate = sf("gate", [P, 2, BANK])
            h_f = sf("h_f", [P, 2, BANK])
            d_half = sf("d_half", [P, 2, HID])
            d_sum = sf("d_sum", [P, 2, HID])
            d_out = sf("d_out", [P, 2, HID])
            st3 = sf("st6", [P, 2, 6])
            mv3 = sf("mv6", [P, 2, 2])
            ve3 = sf("ve6", [P, 2])
            rs3 = sf("rs6", [P, 2])
            mr3 = sf("mr6", [P, 2])
            (z_full, z_hi, z_lo, g_full, u_full, g_act, h_ready, h_hi_ready, h_lo_ready, d_full, d_half_ready,
             d_stats, d_rstd, d_final, stored_even, stored_odd, d_step, pool_step) = semaphores(
                ffn, "z_full", "z_hi", "z_lo", "g_full", "u_full", "g_act", "h_ready", "h_hi_ready", "h_lo_ready",
                "d_full", "d_half_ready", "d_stats", "d_rstd", "d_final", "stored_even", "stored_odd", "d_step",
                "pool_step")
            stored = (stored_even, stored_odd)
            NC = SEQ // BANK
            D_BANKS = (O, R)
            NORM_TURNS = (0, 2, 3, 5)
            block = ffn.enter_context(nc.Block())

            order = []
            for c in range(NC):
                order.append(("UG", c))
                if c >= 1:
                    order.append(("DN", c - 1))
            order.append(("DN", NC - 1))

            @block.sync
            def _(sp):
                for t in range(TILES):
                    sp.wait_ge(d_final, t + 1)
                    sp.dma_start(out_tiles[:, t, :], d_out[:, t % 2, :]).then_inc(stored[t % 2], 16)
                for parity in range(2):
                    sp.wait_ge(stored[parity], 16 * (TILES // 2))

            @block.tensor
            def _(pe):
                def turn_z(c):
                    pe.wait_ge(z_ready, 4 * c + 4)
                    for ct in range(CT):
                        u = CT * c + ct
                        if u >= 2:
                            pe.wait_ge(z_lo, u - 1)
                        for t in range(4):
                            mm = pe.transpose(T[u % 2][:, t * P:(t + 1) * P], z[:, t, ct * P:(ct + 1) * P],
                                              ident[:, :])
                        mm.then_inc(z_full, 1)

                turn_z(0)
                for kind, c in order:
                    if kind == "UG":
                        pe.wait_ge(z_lo, CT * c + CT)
                        for jt in range(JT):
                            k = JT * c + jt
                            for part, bank, full in ((1, S[2 * (k % 2)], g_full), (0, S[2 * (k % 2) + 1], u_full)):
                                if k >= 2:
                                    pe.wait_ge(g_act if part else h_ready, k - 1)
                                col, n = part * INTER + jt * P, 0
                                for ct in range(CT):
                                    for w, x in ((wug_hi, xT_hi), (wug_hi, xT_lo), (wug_lo, xT_hi)):
                                        mm = pe.matmul(bank[:, :], w[:, ct, col:col + P],
                                                       x[:, ct, c * BANK:(c + 1) * BANK], start=(n == 0),
                                                       stop=(n == 5))
                                        n += 1
                                mm.then_inc(full, 1)
                            if jt == JT - 2 and c + 1 < NC:
                                turn_z(c + 1)
                    else:
                        pe.wait_ge(h_lo_ready, JT * c + JT)
                        for tt in range(QB):
                            t = QB * c + tt
                            bank = D_BANKS[t % 2]
                            if t >= 2:
                                pe.wait_ge(d_step, t - 1)
                            for jt in range(JT):
                                pe.matmul(bank[:, :], h_hi[:, c % 2, jt, tt * P:(tt + 1) * P], wd_hl[:, jt, :],
                                          start=(jt == 0), stop=False)
                                mm = pe.matmul(bank[:, 0:HID], h_lo[:, c % 2, jt, tt * P:(tt + 1) * P],
                                               wd_hl[:, jt, 0:HID], start=False, stop=(jt == JT - 1))
                            mm.then_inc(d_full, 1)

            @block.scalar
            def _(act):
                def hi_z(c):
                    for ct in range(CT):
                        u = CT * c + ct
                        act.wait_ge(z_full, u + 1)
                        act.activation(xT_hi[:, ct, c * BANK:(c + 1) * BANK], T[u % 2][:, :], ACT.Copy)\
                           .then_inc(z_hi, 1)

                hi_z(0)
                for kind, c in order:
                    if kind == "UG":
                        for jt in range(JT + 1):
                            k = JT * c + jt
                            if jt < JT:
                                act.wait_ge(g_full, k + 1)
                                if k >= 2:
                                    act.wait_ge(h_ready, k - 1)
                                act.activation(gate[:, k % 2, :], S[2 * (k % 2)][:, :], ACT.Silu).then_inc(g_act, 1)
                            if jt >= 1:
                                act.wait_ge(h_ready, k)
                                if c >= 2:
                                    act.wait_ge(d_full, QB * (c - 1))
                                act.activation(h_hi[:, c % 2, jt - 1, :], h_f[:, (k - 1) % 2, :], ACT.Copy)\
                                   .then_inc(h_hi_ready, 1)
                            if jt == JT - 1 and c + 1 < NC:
                                hi_z(c + 1)
                    else:
                        for t in range(QB * c, QB * c + QB):
                            act.wait_ge(d_full, t + 1)
                            if t >= 2:
                                act.wait_ge(d_step, t - 1)
                            act.activation(d_half[:, t % 2, :], D_BANKS[t % 2][:, HID:2 * HID], ACT.Copy)\
                               .then_inc(d_half_ready, 1)

            @block.vector
            def _(dve):
                count = {"d": 0}

                def lo_z(c):
                    for ct in range(CT):
                        u = CT * c + ct
                        dve.wait_ge(z_hi, u + 1)
                        dve.tensor_tensor(xT_lo[:, ct, c * BANK:(c + 1) * BANK], T[u % 2][:, :],
                                          xT_hi[:, ct, c * BANK:(c + 1) * BANK].bitcast(F32), ALU.subtract)\
                           .then_inc(z_lo, 1)

                def finish(t):
                    dve.wait_ge(d_rstd, t + 1)
                    if t >= 2:
                        dve.wait_ge(stored[t % 2], 16 * (t // 2))
                    dve.scalar_tensor_tensor(out=d_out[:, t % 2, :], in0=d_sum[:, t % 2, :],
                                             scalar=rs3[:, t % 2:t % 2 + 1], in1=acc[:, t, :], op0=ALU.mult,
                                             op1=ALU.add).then_inc(d_stats, 1)
                    count["d"] += 1
                    dve.wait_ge(d_stats, count["d"])
                    dve.tensor_scalar(d_out[:, t % 2, :], d_out[:, t % 2, :], mr3[:, t % 2:t % 2 + 1], None,
                                      ALU.subtract).then_inc(d_final, 1)

                lo_z(0)
                for kind, c in order:
                    if kind == "UG":
                        for jt in range(JT):
                            k = JT * c + jt
                            dve.wait_ge(g_act, k + 1)
                            dve.wait_ge(u_full, k + 1)
                            if k >= 2:
                                dve.wait_ge(h_lo_ready, k - 1)
                            dve.tensor_tensor(h_f[:, k % 2, :], S[2 * (k % 2) + 1][:, :], gate[:, k % 2, :],
                                              ALU.mult).then_inc(h_ready, 1)
                            if c + 1 < NC and jt in NORM_TURNS:
                                part = NORM_TURNS.index(jt)
                                if part == 3:
                                    dve.wait_ge(z_full, CT * (c + 1))
                                norms(dve, c + 1, part)
                            if c + 1 < NC and jt == JT - 2:
                                lo_z(c + 1)
                    else:
                        for t in range(QB * c, QB * c + QB):
                            dve.wait_ge(d_half_ready, t + 1)
                            if t >= 2:
                                dve.wait_ge(d_final, t - 1)
                            dve.tensor_tensor(d_sum[:, t % 2, :], D_BANKS[t % 2][:, 0:HID], d_half[:, t % 2, :],
                                              ALU.add).then_inc(d_step, 1)
                            dve.wait_ge(d_step, t + 1)
                            dve.bn_stats(st3[:, t % 2, :], d_sum[:, t % 2, :]).then_inc(d_stats, 1)
                            count["d"] += 1
                            dve.wait_ge(d_stats, count["d"])
                            dve.bn_aggr(mv3[:, t % 2, :], st3[:, t % 2, :]).then_inc(d_stats, 1)
                            count["d"] += 1
                            dve.wait_ge(d_stats, count["d"])
                            if t >= 1:
                                finish(t - 1)
                finish(TILES - 1)

            def planned_d_counts():
                n, out_ = 0, []
                for t in range(TILES):
                    n += 2
                    out_.append(n)
                    if t >= 1:
                        n += 1
                return out_

            @block.gpsimd
            def _(pool):
                step = 0
                dc = planned_d_counts()

                def inverse_std(dst, tmp, var, w):
                    nonlocal step
                    pool.tensor_scalar(tmp, var, 1.0, EPS, ALU.mult, ALU.add).then_inc(pool_step, 1)
                    step += 1
                    pool.wait_ge(pool_step, step)
                    pool.tensor_tensor(dst, tmp, half_neg[:, 0:w], ALU.pow).then_inc(pool_step, 1)
                    step += 1
                    pool.wait_ge(pool_step, step)

                for kind, c in order:
                    if kind == "UG":
                        for jt in range(JT):
                            k = JT * c + jt
                            if c + 1 < NC and jt in (1, 4):
                                rstds(pool, c + 1, jt // 4)
                            pool.wait_ge(h_hi_ready, k + 1)
                            pool.tensor_tensor(h_lo[:, c % 2, jt, :], h_f[:, k % 2, :],
                                               h_hi[:, c % 2, jt, :].bitcast(F32), ALU.subtract)\
                                .then_inc(h_lo_ready, 1)
                    else:
                        for t in range(QB * c, QB * c + QB):
                            b = slice(t % 2, t % 2 + 1)
                            pool.wait_ge(d_stats, dc[t])
                            inverse_std(rs3[:, b], ve3[:, b], mv3[:, t % 2, 1:2], 1)
                            pool.tensor_tensor(mr3[:, b], rs3[:, b], mv3[:, t % 2, 0:1], ALU.mult)\
                                .then_inc(d_rstd, 1)


_INS = ['L0_attn_hidden_states', 'L0_attn_Wqkv_w', 'L0_attn_Wqkv_b', 'L0_attn_lambda_q1', 'L0_attn_lambda_k1',
        'L0_attn_lambda_q2', 'L0_attn_lambda_k2', 'L0_attn_subln_w', 'L0_attn_out_w', 'L0_attn_out_b',
        'L0_ffn_SU_ug', 'L0_ffn_SU_dp', 'L0_ffn_Wscale_ug', 'L0_ffn_Wscale_dp', 'L0_ffn_W_up', 'L0_ffn_W_gate',
        'L0_ffn_W_down']


def kernel(**inputs):
    import numpy as _np
    import concourse.bacc as _bacc
    from concourse import mybir as _mybir
    from concourse.bass_utils import run_bass_kernel_spmd as _run

    nc = _bacc.Bacc("TRN2", target_bir_lowering=False, num_devices=1)
    arrays, args = {}, []
    for name in _INS:
        a = _np.ascontiguousarray(inputs[name])
        arrays[f"in_{name}_dram"] = a
        args.append(nc.dram_tensor(f"in_{name}_dram", a.shape, _mybir.dt.from_np(a.dtype), kind="ExternalInput").ap())
    out = nc.dram_tensor("out_0_dram", (1, SEQ, HID), _mybir.dt.float32, kind="ExternalOutput").ap()
    build(nc, *args, out)
    r = _run(nc, [arrays], core_ids=[0])
    return r.results[0]["out_0_dram"]
```

```python
import math
from contextlib import ExitStack

import concourse.bass as bass
from concourse import mybir

F32 = mybir.dt.float32
F32R = mybir.dt.float32r
ALU = mybir.AluOpType
ACT = mybir.ActivationFunctionType
X = mybir.AxisListType.X

P = 128
SEQ = 2048
HID = 256
D = 128
NQH = 16
NKH = 8
GROUPS = NKH // 2
INTER = 1024
TILES = SEQ // P
CT = HID // P
LAMBDA_INIT = 0.8 - 0.6 * math.exp(-0.3 * 1)
SCALE = float(D) ** -0.5
EPS = 1e-5
BANK = 512
QB = BANK // P
DUOS = TILES
CHUNKS = 5
NS = 4
E1_SLOTS = 2 * CHUNKS
E2_SLOTS = CHUNKS
MASKED = -1e30
LOWEST = -3e38
K_USES = SEQ // BANK
V_USES = TILES // 2
PAIR_ORDER = (3, 7, 4, 2, 5, 1, 6, 0)
HALVES = ('TSSTSSPTSoQTPPPTO', 'TSTSSOSTPSoQTPPTP')
FIRST_HALVES = ('KQSKKKSVSVSSVVVVV', 'SVWSWSQSS')
LAST_HALVES = ('ToTPTToOP', 'TTOTPPTPO', 'ToTTTOoPo')
PT_SLOTS = 3
DVE_MIXES = (3,)
EXPS_AT = {'PV': 2, 'OT': 0, 'QP': 0, 'T': 0, 'S': 2, 'OP': 2}
FACTOR_LAG = 0
MIXES_A_STEP = 1
SCALAR_LAGS = {'K': 1, 'V': 1, 'QP': 0, 'OP': 0}
VECTOR_LAGS = {'PV': 1, 'T': 1, 'OT': 1, 'W': 1, 'K': 1, 'V': 1}


def duo_chunks(d):
    out = []
    e = 2 * PAIR_ORDER[d // 2] + d % 2
    for n, (i, s) in enumerate(sorted(((TILES - 1 - e, 0), (e, 1)))):
        keys = (i + 1) * P
        for c in range(-(-keys // BANK)):
            w = min(BANK, keys - c * BANK)
            out.append((2 * d + n, s, i, c, w, (c + 1) * BANK >= keys))
    assert len(out) == CHUNKS
    return out


def attention_steps():
    steps, exps_due, factors_due, mixes_due = [], [], [], []
    to_turn, to_project = [], []

    def emit(kind, what):
        n = len(steps)
        exps = [exps_due.pop(0)[0] for _ in range(EXPS_AT.get(kind, 1))
                if exps_due and exps_due[0][1] < n]
        factors = [f for f, at in factors_due if at <= n]
        factors_due[:] = [x for x in factors_due if x[1] > n]
        mixes = [mixes_due.pop(0) for _ in range(MIXES_A_STEP) if mixes_due]
        assert kind != "T" or what not in mixes + mixes_due
        steps.append((kind, what, exps, factors, mixes))
        for d, m, j in exps:
            if m == 1 and duo_chunks(d)[j][5]:
                factors_due.append((duo_chunks(d)[j][0], n + FACTOR_LAG))
        for o in factors:
            mixes_due.extend((o // 2, j) for j, ch in enumerate(duo_chunks(o // 2)) if ch[0] == o)
        if kind == "S":
            d, m, j = what
            o, last = duo_chunks(d)[j][0], duo_chunks(d)[j][5]
            if last:
                exps_due.extend(((d, m, jj), n) for jj, ch in enumerate(duo_chunks(d)) if ch[0] == o)
        if kind == "PV" and duo_chunks(what[0])[what[1]][5]:
            to_turn.append(duo_chunks(what[0])[what[1]][0])
        if kind == "OT":
            to_project.append(what)

    def pv_part(h):
        db = (h - 3) // 2 if h % 2 else (h - 4) // 2
        if not 0 <= db < DUOS:
            return []
        widths = [c[4] for c in duo_chunks(db)]
        cut = min(range(1, CHUNKS), key=lambda n: abs(sum(widths[:n]) - sum(widths[n:])))
        return [(db, j) for j in (range(cut) if h % 2 else range(cut, CHUNKS))]

    setup = {"K": [("K", c) for c in range(4)], "W": [("W", s) for s in range(2)],
             "V": [("V", v) for v in range(V_USES)]}
    for h in range(2 * DUOS + 3):
        d, m = divmod(h, 2)
        scores = [("S", (d, m, j)) for j in range(CHUNKS)] if d < DUOS else []
        part = pv_part(h)
        turns, products = [("T", x) for x in part], [("PV", x) for x in part]
        extra = [("QP", (h // 4 + 1, h % 4 // 2, h % 2))] if h // 4 + 1 < DUOS // 2 else []
        for what in (FIRST_HALVES[h] if h < 2 else HALVES[m] if d < DUOS else LAST_HALVES[h - 2 * DUOS]):
            if what == "o":
                if to_turn:
                    emit("OT", to_turn.pop(0))
            elif what == "O":
                if to_project:
                    emit("OP", to_project.pop(0))
            else:
                queue = {"T": turns, "S": scores, "P": products, "Q": extra, **setup}[what]
                if queue:
                    emit(*queue.pop(0))
        for what in (*turns, *scores, *products):
            emit(*what)
        assert h == 0 or not any(setup.values())
    while exps_due or factors_due or mixes_due:
        emit("END", None)
    for what in to_turn:
        emit("OT", what)
    for what in to_project:
        emit("OP", what)
    return steps


def with_lags(steps, lags):
    placed = []
    for n, (kind, what, exps, factors, mixes) in enumerate(steps):
        lag = lags.get(kind, 0)
        placed.append((n - 0.5, ("DUE", None, exps, [], [])))
        placed.append((n + lag + (0.25 if lag else 0), (kind, what, [], [], [])))
        placed.append((n + 0.5, ("DUE", None, [], factors, mixes)))
    return [step for _, step in sorted(placed, key=lambda p: p[0])]


def build(nc, hidden, wqkv, bqkv, lq1, lk1, lq2, lk2, subln, out_w, out_b, su_ug, su_dp, ws_ug, ws_dp,
          w_up, w_gate, w_down, out):
    x_tiles = hidden[0].rearrange("(t p) c -> p t c", p=P)
    out_tiles = out[0].rearrange("(t p) c -> p t c", p=P)
    K0 = NQH * D
    V0 = K0 + NKH * D
    steps = attention_steps()

    with ExitStack() as whole:
        def tensors(stack):
            return lambda name, shape, dt=F32: stack.enter_context(nc.sbuf_tensor(name, shape, dt))

        def semaphores(stack, *names):
            return [stack.enter_context(nc.semaphore(n)) for n in names]

        sb = tensors(whole)
        whole.enter_context(nc.allow_non_contiguous_dma(reason="short columns of biases and scales"))
        S = [whole.enter_context(nc.psum_tensor(f"score_bank{b}", [P, BANK], F32)) for b in range(NS)]
        T = [whole.enter_context(nc.psum_tensor(f"turn_bank{b}", [P, BANK], F32)) for b in range(2)]
        O = whole.enter_context(nc.psum_tensor("sum_bank", [P, BANK], F32))
        R = whole.enter_context(nc.psum_tensor("proj_bank", [P, BANK], F32))

        xT_hi = sb("xT_hi", [P, CT, SEQ], F32R)
        xT_lo = sb("xT_lo", [P, CT, SEQ], F32R)
        acc = sb("acc", [P, TILES, HID])
        ident = sb("ident", [P, P])
        mask = sb("mask", [P, BANK])
        half_neg = sb("half_neg", [P, 4])
        neg_one = sb("neg_one", [P, 1])
        neg_lam = sb("neg_lam", [P, 1])
        subln_col = sb("subln_col", [P, CT])

        with ExitStack() as att:
            sa = tensors(att)
            w_raw = sa("w_raw", [P, 8, HID])
            bqk_raw = sa("bqk_raw", [P, 6])
            bv = sa("bv", [P, 2, HID])

            with ExitStack() as pro:
                sp_ = tensors(pro)
                x_in = sp_("x_in", [P, TILES, HID])
                xn = sp_("xn", [P, TILES, HID])
                stats = sp_("stats", [P, TILES, 6])
                mv = sp_("mv", [P, TILES, 2])
                var_eps = sp_("var_eps", [P, TILES])
                rstd = sp_("rstd", [P, TILES])
                out_b_row = sp_("out_b_row", [P, HID])
                lam_in = sp_("lam_in", [P, 4, D])
                lam_junk = sp_("lam_junk", [P, 2, D])
                lam_dot = sp_("lam_dot", [P, 2])
                lam_exp = sp_("lam_exp", [P, 2])
                lam_diff = sp_("lam_diff", [P, 1])
                x_in_sems = semaphores(pro, *[f"x_landed{q}" for q in range(4)])
                (small_landed, out_b_landed, lam_landed, w_landed, ident_base, ident_ready, consts_ready, stats_ready,
                 rstd_step, rstd_ready, xn_ready, turned, hi_ready, lo_ready, lam_dots, lam_exps, lam_step
                 ) = semaphores(
                    pro, "small_landed", "out_b_landed", "lam_landed", "w_landed", "ident_base", "ident_ready",
                    "consts_ready",
                    "stats_ready", "rstd_step", "rstd_ready", "xn_ready", "turned", "hi_ready", "lo_ready",
                    "lam_dots", "lam_exps", "lam_step")
                TURNS = (*T, *S, O, R)
                block = pro.enter_context(nc.Block())

                @block.sync
                def _(sp):
                    for q in range(4):
                        sp.dma_start(x_in[:, 4 * q:4 * q + 4, :], x_tiles[:, 4 * q:4 * q + 4, :])\
                          .then_inc(x_in_sems[q], 16)
                    sp.dma_start(out_b_row[:, :], out_b.rearrange("(a d) -> a d", a=1).broadcast_to([P, HID]))\
                      .then_inc(out_b_landed, 16)
                    for k, v in enumerate((lq1, lk1, lq2, lk2)):
                        sp.dma_start(lam_in[:, k, :], v.rearrange("(a d) -> a d", a=1).broadcast_to([P, D]))\
                          .then_inc(lam_landed, 16)
                    sp.dma_start(subln_col[:, :], subln.rearrange("(t p) -> p t", p=P)).then_inc(small_landed, 16)
                    sp.dma_start(w_raw[:, 0:4, :], wqkv[0:4 * D, :].rearrange("(r p) c -> p r c", p=P))\
                      .then_inc(w_landed, 16)
                    sp.dma_start(w_raw[:, 4:6, :], wqkv[K0:K0 + 2 * D, :].rearrange("(r p) c -> p r c", p=P))\
                      .then_inc(w_landed, 16)
                    sp.dma_start(w_raw[:, 6:8, :], wqkv[V0:V0 + 2 * D, :].rearrange("(r p) c -> p r c", p=P))\
                      .then_inc(w_landed, 16)
                    sp.dma_start(bqk_raw[:, 0:4], bqkv[0:4 * D].rearrange("(r p) -> p r", p=P))\
                      .then_inc(w_landed, 16)
                    sp.dma_start(bqk_raw[:, 4:6], bqkv[K0:K0 + 2 * D].rearrange("(r p) -> p r", p=P))\
                      .then_inc(w_landed, 16)
                    for k in range(2):
                        sp.dma_start(bv[:, k, :], bqkv[V0:V0 + HID].rearrange("(a d) -> a d", a=1)
                                     .broadcast_to([P, HID])).then_inc(w_landed, 16)
                    sp.wait_ge(small_landed, 16)
                    sp.wait_ge(w_landed, 112)

                @block.gpsimd
                def _(pool):
                    pool.memset(ident[:, :], 0.0).then_inc(ident_base, 1)
                    pool.memset(mask[:, :], 0.0).then_inc(ident_base, 1)
                    pool.memset(half_neg[:, :], -0.5).then_inc(ident_base, 1)
                    pool.memset(neg_one[:, :], -1.0).then_inc(ident_base, 1)
                    pool.wait_ge(ident_base, 4)
                    pool.affine_select(out=ident[:, :], in_=ident[:, :], compare_op=ALU.not_equal, fill=1.0,
                                       base=0, pattern=[[-1, P]], channel_multiplier=1).then_inc(ident_ready, 1)
                    pool.affine_select(out=mask[:, BANK - P:], in_=mask[:, BANK - P:], compare_op=ALU.is_ge,
                                       fill=MASKED, base=0, pattern=[[-1, P]], channel_multiplier=1)\
                        .then_inc(consts_ready, 1)
                    for q in range(4):
                        t = slice(4 * q, 4 * q + 4)
                        pool.wait_ge(stats_ready, 4 * q + 4)
                        pool.tensor_scalar(var_eps[:, t], mv[:, t, 1], 1.0, EPS, ALU.mult, ALU.add)\
                            .then_inc(rstd_step, 1)
                        pool.wait_ge(rstd_step, q + 1)
                        pool.tensor_tensor(rstd[:, t], var_eps[:, t], half_neg[:, :], ALU.pow)\
                            .then_inc(rstd_ready, 1)

                @block.vector
                def _(dve):
                    def split_x(q):
                        for ct in range(CT):
                            u = CT * q + ct
                            dve.wait_ge(hi_ready, u + 1)
                            dve.tensor_tensor(xT_lo[:, ct, q * BANK:(q + 1) * BANK], TURNS[u][:, :],
                                              xT_hi[:, ct, q * BANK:(q + 1) * BANK].bitcast(F32), ALU.subtract)\
                               .then_inc(lo_ready, 1)

                    n = 0
                    for q in range(6):
                        if q < 4:
                            dve.wait_ge(x_in_sems[q], 16)
                            for t in range(4 * q, 4 * q + 4):
                                dve.bn_stats(stats[:, t, :], x_in[:, t, :]).then_inc(lam_step, 1)
                            n += 4
                            dve.wait_ge(lam_step, n)
                            for t in range(4 * q, 4 * q + 4):
                                dve.bn_aggr(mv[:, t, :], stats[:, t, :]).then_inc(stats_ready, 1)
                        if 1 <= q < 5:
                            dve.wait_ge(rstd_ready, q)
                            for t in range(4 * q - 4, 4 * q):
                                dve.tensor_scalar(xn[:, t, :], x_in[:, t, :], mv[:, t, 0:1], rstd[:, t:t + 1],
                                                  ALU.subtract, ALU.mult).then_inc(xn_ready, 1)
                        if q >= 2:
                            split_x(q - 2)
                    dve.wait_ge(lam_landed, 64)
                    for k in range(2):
                        dve.tensor_tensor_reduce(out=lam_junk[:, k, :], in0=lam_in[:, 2 * k, :],
                                                 in1=lam_in[:, 2 * k + 1, :], scale=1.0, scalar=0.0,
                                                 op0=ALU.mult, op1=ALU.add, accum_out=lam_dot[:, k:k + 1])\
                           .then_inc(lam_dots, 1)
                    dve.wait_ge(lam_exps, 1)
                    dve.tensor_tensor(lam_diff[:, :], lam_exp[:, 1:2], lam_exp[:, 0:1], ALU.subtract)\
                       .then_inc(lam_step, 1)
                    n += 1
                    dve.wait_ge(lam_step, n)
                    dve.tensor_scalar(neg_lam[:, :], lam_diff[:, :], -LAMBDA_INIT, None, ALU.add)\
                       .then_inc(lam_step, 1)

                @block.scalar
                def _(act):
                    for q in range(4):
                        for ct in range(CT):
                            act.wait_ge(turned, CT * q + ct + 1)
                            act.activation(xT_hi[:, ct, q * BANK:(q + 1) * BANK], TURNS[CT * q + ct][:, :],
                                           ACT.Copy).then_inc(hi_ready, 1)
                        if q == 0:
                            act.wait_ge(out_b_landed, 16)
                        for t in range(4 * q, 4 * q + 4):
                            act.activation(acc[:, t, :], out_b_row[:, :], ACT.Copy).then_inc(consts_ready, 1)
                    act.wait_ge(lam_dots, 2)
                    act.activation(lam_exp[:, :], lam_dot[:, :], ACT.Exp).then_inc(lam_exps, 1)

                @block.tensor
                def _(pe):
                    pe.wait_ge(ident_ready, 1)
                    for q in range(4):
                        pe.wait_ge(xn_ready, 4 * q + 4)
                        for ct in range(CT):
                            u = CT * q + ct
                            for t in range(4):
                                mm = pe.transpose(TURNS[u][:, t * P:(t + 1) * P],
                                                  xn[:, 4 * q + t, ct * P:(ct + 1) * P], ident[:, :])
                            mm.then_inc(turned, 1)

            with ExitStack() as shared:
                ss = tensors(shared)
                wkv_hi = ss("wkv_hi", [P, CT, 2 * HID], F32R)
                wkv_lo = ss("wkv_lo", [P, CT, 2 * HID], F32R)
            e2 = sa("e2", [P, E2_SLOTS, BANK])
            e1 = sa("e1", [P, E1_SLOTS, BANK])
            wo_raw = e1[:, 7:9, :]
            q_hi = sa("q_hi", [P, 2, 2, 2, HID], F32R)
            q_lo = sa("q_lo", [P, 2, 2, 2, HID], F32R)
            k_hi = sa("k_hi", [P, 2, SEQ], F32R)
            k_lo = sa("k_lo", [P, 2, SEQ], F32R)
            v_hl = sa("v_hl", [P, TILES, 2 * HID], F32R)
            pT_hi = sa("pT_hi", [P, PT_SLOTS, BANK], F32R)
            pT_lo = sa("pT_lo", [P, PT_SLOTS, BANK], F32R)
            wq_hi = sa("wq_hi", [P, CT, 4 * D], F32R)
            wq_lo = sa("wq_lo", [P, CT, 4 * D], F32R)
            wo_hi = sa("wo_hi", [P, 2, CT, HID], F32R)
            wo_lo = sa("wo_lo", [P, 2, CT, HID], F32R)
            o_half = sa("o_half", [P, 2, HID])
            o_sum = sa("o_sum", [P, 2, HID])
            oT_hi = sa("oT_hi", [P, 2, HID], F32R)
            oT_lo = sa("oT_lo", [P, 2, HID], F32R)
            bqk = sa("bqk", [P, 6])
            subln_s = sa("subln_s", [P, CT])
            mx = sa("mx", [P, 2, 2, 2, 4])
            negmx = sa("negmx", [P, 2, 2, 2])
            ssum = sa("ssum", [P, 4, 2, 2, 4])
            s12 = sa("s12", [P, 4, 2, 2])
            inv_s2 = sa("inv_s2", [P, 4, 2])
            ratio = sa("ratio", [P, 4, 2])
            msq = sa("msq", [P, 4])
            rms_a = sa("rms_a", [P, 4])
            rms_b = sa("rms_b", [P, 4])
            rms = sa("rms", [P, 4])

            names = ("wo_landed", "w_next", "b_ready", "s_full", "s_act", "s_dve", "t_full", "t_hi",
                     "t_lo", "r_full", "r_hi", "r_free", "kv_full", "kv_act", "kv_dve", "v_lo",
                     "neg_ready", "sums_ready", "ratio_step", "ratio_ready", "e2_scaled", "p_pool",
                     "p_dve", "pv_done", "o_half_ready", "o_ready", "msq_ready", "rms_step", "rms_ready")
            sems = semaphores(att, *names)
            (wo_landed, w_next, b_ready, s_full, s_act, s_dve, t_full, t_hi, t_lo, r_full, r_hi, r_free,
             kv_full, kv_act, kv_dve, v_lo, neg_ready, sums_ready, ratio_step, ratio_ready, e2_scaled,
             p_pool, p_dve, pv_done, o_half_ready, o_ready, msq_ready, rms_step, rms_ready) = sems
            assert [s.num for s in sems] == list(range(sems[0].num, sems[0].num + len(sems)))

            W_TURNS = 4
            W_PAIRS = (2, 0, 1, 3)
            W_BANKS = (T[0], T[1], S[2], S[3])
            FIRST_Q_BANKS = (R, O)
            t_use, r_use, n_qp = {}, {}, {}
            for n in range(4):
                r_use["QP", (0, n % 2, n // 2)] = n
                n_qp[(0, n % 2, n // 2)] = n
            for kind, what, *_ in steps:
                if kind in ("T", "OT", "W"):
                    t_use[kind, what] = W_TURNS + len(t_use)
                if kind in ("QP", "OP"):
                    r_use[kind, what] = len(r_use)
                if kind == "QP":
                    n_qp[what] = len(n_qp)
            WORK = (T[0], T[1], R, O)
            last_use = [(-4, ("W", "k")), (-3, ("W", "q")), (-2, ("QP", (0, 0, 1))), (-1, ("QP", (0, 1, 1)))]
            t_use["W", "k"], t_use["W", "q"] = 0, 1
            bank_of, before = {}, {}
            for n, (kind, what, *_) in enumerate(steps):
                use = (kind, what)
                if kind == "PV":
                    use = ("PV", duo_chunks(what[0])[what[1]][0])
                if kind in ("S", "END"):
                    continue
                if use not in bank_of:
                    b = min(range(4), key=lambda b: last_use[b][0])
                    bank_of[use], before[use] = b, last_use[b][1]
                held = kind == "PV" and not duo_chunks(what[0])[what[1]][5]
                last_use[bank_of[use]] = (len(steps) if held else n, use)

            pool_mixed, dve_mixed = [], []
            for q in range(CHUNKS * DUOS):
                on_dve = q % CHUNKS in DVE_MIXES
                pool_mixed.append((pool_mixed or [0])[-1] + (not on_dve))
                dve_mixed.append((dve_mixed or [0])[-1] + on_dve)

            def bank_for(*use):
                return WORK[bank_of[use]]

            def wait_mixed(eng, q):
                if q % CHUNKS in DVE_MIXES:
                    eng.wait_ge(p_dve, dve_mixed[q])
                else:
                    eng.wait_ge(p_pool, pool_mixed[q])

            def v_staged(v):
                return e1[:, CHUNKS + v % 2, :]

            def tile_of(o):
                return next(ch[1:3] for ch in duo_chunks(o // 2) if ch[0] == o)

            def kv_use(kind, n):
                return n if kind == "K" else K_USES + n

            def s_use(d, m, j):
                return K_USES + CHUNKS * (2 * d + m) + j

            def q_cols(s, i):
                return (i % 2) * P

            def first_q_token(u, s):
                first = 2 * PAIR_ORDER[u]
                return (TILES - 2 - first) * P if s == 0 else first * P

            with nc.Fori(0, GROUPS) as g:
                with nc.Block() as block:

                    @block.sync
                    def _(sp):
                        sp.dma_start(wo_raw, out_w[:, bass.ds(g * (2 * HID), 2 * HID)]
                                     .rearrange("(t p) c -> p t c", p=P)).then_inc(wo_landed, 16)
                        nxt = (g + 1) % GROUPS
                        sp.wait_ge(t_full, 4)
                        sp.dma_start(w_raw[:, 0:4, :], wqkv[bass.ds(nxt * (4 * D), 4 * D), :]
                                     .rearrange("(r p) c -> p r c", p=P)).then_inc(w_next, 16)
                        sp.dma_start(w_raw[:, 4:6, :], wqkv[bass.ds(nxt * (2 * D) + K0, 2 * D), :]
                                     .rearrange("(r p) c -> p r c", p=P)).then_inc(w_next, 16)
                        sp.dma_start(w_raw[:, 6:8, :], wqkv[bass.ds(nxt * (2 * D) + V0, 2 * D), :]
                                     .rearrange("(r p) c -> p r c", p=P)).then_inc(w_next, 16)
                        sp.wait_ge(b_ready, 2)
                        sp.dma_start(bqk_raw[:, 0:4], bqkv[bass.ds(nxt * (4 * D), 4 * D)]
                                     .rearrange("(r p) -> p r", p=P)).then_inc(w_next, 16)
                        sp.dma_start(bqk_raw[:, 4:6], bqkv[bass.ds(nxt * (2 * D) + K0, 2 * D)]
                                     .rearrange("(r p) -> p r", p=P)).then_inc(w_next, 16)
                        sp.wait_ge(kv_dve, K_USES + V_USES)
                        for k in range(2):
                            sp.dma_start(bv[:, k, :], bqkv[bass.ds(nxt * HID + V0, HID)]
                                         .rearrange("(a d) -> a d", a=1).broadcast_to([P, HID])).then_inc(w_next, 16)
                        sp.wait_ge(w_next, 7 * 16)

                    @block.tensor
                    def _(pe):
                        def free_bank(*use):
                            last = before[use]
                            if last and last[0] in ("T", "OT", "W"):
                                pe.wait_ge(t_lo, t_use[last] + 1)
                            elif last and last[0] in ("QP", "OP"):
                                pe.wait_ge(r_free, r_use[last] + 1)
                            elif last and last[0] in ("K", "V"):
                                pe.wait_ge(kv_dve, kv_use(*last) + 1)
                            elif last:
                                pe.wait_ge(o_ready, last[1] + 1)
                            return bank_for(*use)

                        def score_bank(k):
                            if k >= NS:
                                pe.wait_ge(s_act, k - NS + 1)
                                pe.wait_ge(s_dve, k - NS + 1)
                            return S[k % NS]

                        def project_q(what):
                            u, s, m = what
                            if u == 0:
                                if m == 1:
                                    pe.wait_ge(r_free, 1 + s)
                                bank = FIRST_Q_BANKS[s]
                            else:
                                bank = free_bank("QP", what)
                            head, tok = (2 * s + m) * D, first_q_token(u, s)
                            n = 0
                            for ct in range(CT):
                                for w, x in ((wq_hi, xT_hi), (wq_hi, xT_lo), (wq_lo, xT_hi)):
                                    mm = pe.matmul(bank[:, 0:HID], w[:, ct, head:head + D],
                                                   x[:, ct, tok:tok + HID], start=(n == 0), stop=(n == 5))
                                    n += 1
                            mm.then_inc(r_full, 1)

                        for n, u in enumerate(W_PAIRS):
                            for rr in range(2):
                                for ct in range(CT):
                                    mm = pe.transpose(W_BANKS[n][:, ct * HID + rr * P:ct * HID + (rr + 1) * P],
                                                      w_raw[:, 2 * u + rr, ct * P:(ct + 1) * P], ident[:, :])
                            mm.then_inc(t_full, 1)
                        def project_k(bank, m, c, full):
                            n = 0
                            for ct in range(CT):
                                for w, x in ((wkv_hi, xT_hi), (wkv_hi, xT_lo), (wkv_lo, xT_hi)):
                                    mm = pe.matmul(bank[:, :], w[:, ct, m * D:(m + 1) * D],
                                                   x[:, ct, c * BANK:(c + 1) * BANK], start=(n == 0), stop=(n == 5))
                                    n += 1
                            mm.then_inc(full, 1)

                        pe.wait_ge(t_lo, 1)
                        for c in range(K_USES):
                            if c == 2:
                                pe.wait_ge(t_lo, 4)
                            project_k(score_bank(c), 0, c, s_full)
                            if c < 2:
                                pe.wait_ge(t_lo, 2 + c)
                            project_q((0, c % 2, c // 2))
                        pe.wait_ge(s_dve, K_USES)

                        for kind, what, *_ in steps:
                            if kind == "S":
                                d, m, j = what
                                _, s, i, c, w, _ = duo_chunks(d)[j]
                                if d % 2 == 0:
                                    pe.wait_ge(r_free, r_use["QP", (d // 2, s, m)] + 1)
                                if d == 0 and m == 1:
                                    pe.wait_ge(kv_dve, K_USES)
                                bank = score_bank(s_use(d, m, j))
                                col = q_cols(s, i)
                                qh = q_hi[:, d // 2 % 2, s, m, col:col + P]
                                ql = q_lo[:, d // 2 % 2, s, m, col:col + P]
                                kh = k_hi[:, m, c * BANK:c * BANK + w]
                                kl = k_lo[:, m, c * BANK:c * BANK + w]
                                pe.matmul(bank[:, 0:w], qh, kh, start=True, stop=False)
                                pe.matmul(bank[:, 0:w], qh, kl, start=False, stop=False)
                                pe.matmul(bank[:, 0:w], ql, kh, start=False, stop=True).then_inc(s_full, 1)
                            elif kind == "T":
                                d, j = what
                                w, q = duo_chunks(d)[j][4], CHUNKS * d + j
                                wait_mixed(pe, q)
                                bank = free_bank(kind, what)
                                for b in range(w // P):
                                    mm = pe.transpose(bank[:, b * P:(b + 1) * P],
                                                      e1[:, q % E1_SLOTS, b * P:(b + 1) * P], ident[:, :])
                                mm.then_inc(t_full, 1)
                            elif kind == "PV":
                                d, j = what
                                o, _, i, c, w, _ = duo_chunks(d)[j]
                                q = CHUNKS * d + j
                                if q == 0:
                                    pe.wait_ge(v_lo, V_USES)
                                bank = free_bank(kind, o) if c == 0 else bank_for(kind, o)
                                pe.wait_ge(t_lo, t_use["T", what] + 1)
                                for b in range(w // P):
                                    kt = c * QB + b
                                    pe.matmul(bank[:, :], pT_hi[:, q % PT_SLOTS, b * P:(b + 1) * P], v_hl[:, kt, :],
                                              start=(kt == 0), stop=False)
                                    mm = pe.matmul(bank[:, 0:HID], pT_lo[:, q % PT_SLOTS, b * P:(b + 1) * P],
                                                   v_hl[:, kt, 0:HID], start=False, stop=(kt == i))
                                mm.then_inc(pv_done, 1)
                            elif kind == "K":
                                project_k(free_bank(kind, what), 1, what, kv_full)
                            elif kind == "V":
                                bank = free_bank(kind, what)
                                for tt in range(2):
                                    tok, n = (2 * what + tt) * P, 0
                                    for ct in range(CT):
                                        for x, w in ((xT_hi, wkv_hi), (xT_hi, wkv_lo), (xT_lo, wkv_hi)):
                                            mm = pe.matmul(bank[:, tt * HID:(tt + 1) * HID], x[:, ct, tok:tok + P],
                                                           w[:, ct, HID:2 * HID], start=(n == 0), stop=(n == 5))
                                            n += 1
                                mm.then_inc(kv_full, 1)
                            elif kind == "W":
                                pe.wait_ge(wo_landed, 16)
                                bank = free_bank(kind, what)
                                for et in range(CT):
                                    for nt in range(CT):
                                        mm = pe.transpose(bank[:, et * HID + nt * P:et * HID + (nt + 1) * P],
                                                          wo_raw[:, nt, what * HID + et * P:what * HID + (et + 1) * P],
                                                          ident[:, :])
                                mm.then_inc(t_full, 1)
                            elif kind == "OT":
                                pe.wait_ge(o_ready, what + 1)
                                bank = free_bank(kind, what)
                                for et in range(CT):
                                    mm = pe.transpose(bank[:, et * P:(et + 1) * P],
                                                      o_sum[:, what % 2, et * P:(et + 1) * P], ident[:, :])
                                mm.then_inc(t_full, 1)
                            elif kind == "OP":
                                o, s = what, tile_of(what)[0]
                                bank = free_bank(kind, what)
                                pe.wait_ge(t_lo, t_use["OT", o] + 1)
                                n = 0
                                for et in range(CT):
                                    for a, w in ((oT_hi, wo_hi), (oT_hi, wo_lo), (oT_lo, wo_hi)):
                                        mm = pe.matmul(bank[:, 0:HID], a[:, o % 2, et * P:(et + 1) * P],
                                                       w[:, s, et, :], start=(n == 0), stop=(n == 5))
                                        n += 1
                                mm.then_inc(r_full, 1)
                            elif kind == "QP":
                                project_q(what)

                    @block.scalar
                    def _(act):
                        def q_high(what):
                            u, s, m = what
                            act.wait_ge(r_full, r_use["QP", what] + 1)
                            bank = FIRST_Q_BANKS[s] if u == 0 else bank_for("QP", what)
                            act.activation(q_hi[:, u % 2, s, m, :], bank[:, 0:HID], ACT.Identity,
                                           bias=bqk[:, 2 * s + m:2 * s + m + 1]).then_inc(r_hi, 1)

                        for n, u in enumerate(W_PAIRS):
                            act.wait_ge(t_full, n + 1)
                            src = W_BANKS[n][:, :].rearrange("p (c n) -> p c n", c=CT)
                            dst = wq_hi if u < 2 else wkv_hi
                            act.activation(dst[:, :, u % 2 * HID:(u % 2 + 1) * HID], src, ACT.Copy,
                                           scale=SCALE if u < 2 else 1.0).then_inc(t_hi, 1)
                        act.wait_ge(b_ready, 3)
                        for c in range(K_USES):
                            act.wait_ge(s_full, c + 1)
                            act.activation(k_hi[:, 0, c * BANK:(c + 1) * BANK], S[c][:, :], ACT.Identity,
                                           bias=bqk[:, 4:5]).then_inc(s_act, 1)
                            q_high((0, c % 2, c // 2))

                        def exponentials(exps):
                            for d, m, j in exps:
                                o, s, _, c, w, _ = duo_chunks(d)[j]
                                q, k = CHUNKS * d + j, s_use(d, m, j)
                                act.wait_ge(neg_ready, 4 * d + 2 * m + o % 2 + 1)
                                if m == 0 and q >= E1_SLOTS:
                                    act.wait_ge(t_full, t_use["T", divmod(q - E1_SLOTS, CHUNKS)] + 1)
                                elif m == 0 and q >= CHUNKS:
                                    act.wait_ge(v_lo, V_USES)
                                if m == 1 and q >= E2_SLOTS:
                                    wait_mixed(act, q - E2_SLOTS)
                                elif m == 1:
                                    act.wait_ge(kv_full, K_USES + V_USES)
                                e = e1[:, q % E1_SLOTS, 0:w] if m == 0 else e2[:, q % E2_SLOTS, 0:w]
                                act.activation(e, S[k % NS][:, 0:w], ACT.Exp, bias=negmx[:, d % 2, m, s:s + 1],
                                               accum_out=ssum[:, d % 4, s, m, c:c + 1]).then_inc(s_act, 1)

                        for kind, what, exps, _, _ in with_lags(steps, SCALAR_LAGS):
                            exponentials(exps)
                            if kind == "T":
                                d, j = what
                                w, q, u = duo_chunks(d)[j][4], CHUNKS * d + j, t_use[kind, what]
                                act.wait_ge(t_full, u + 1)
                                if q >= PT_SLOTS:
                                    act.wait_ge(pv_done, q - PT_SLOTS + 1)
                                act.activation(pT_hi[:, q % PT_SLOTS, 0:w], bank_for(kind, what)[:, 0:w],
                                               ACT.Copy).then_inc(t_hi, 1)
                            elif kind == "PV":
                                d, j = what
                                o, _, _, _, _, last = duo_chunks(d)[j]
                                if last:
                                    act.wait_ge(pv_done, CHUNKS * d + j + 1)
                                    if o >= 2:
                                        act.wait_ge(msq_ready, o - 1)
                                    act.activation(o_half[:, o % 2, :], bank_for(kind, o)[:, HID:2 * HID], ACT.Copy)\
                                       .then_inc(o_half_ready, 1)
                            elif kind == "OT":
                                o, u = what, t_use[kind, what]
                                act.wait_ge(t_full, u + 1)
                                if o >= 2:
                                    act.wait_ge(r_full, r_use["OP", o - 2] + 1)
                                act.activation(oT_hi[:, o % 2, :], bank_for(kind, o)[:, 0:HID],
                                               ACT.Copy).then_inc(t_hi, 1)
                                act.activation(o_half[:, o % 2, :], o_sum[:, o % 2, :], ACT.Square,
                                               scale=float(2 * D) ** -0.5, accum_out=msq[:, o % 4:o % 4 + 1])\
                                   .then_inc(msq_ready, 1)
                            elif kind == "QP":
                                q_high(what)
                            elif kind == "K":
                                act.wait_ge(kv_full, kv_use(kind, what) + 1)
                                act.activation(k_hi[:, 1, what * BANK:(what + 1) * BANK], bank_for(kind, what)[:, :],
                                               ACT.Identity, bias=bqk[:, 5:6]).then_inc(kv_act, 1)
                            elif kind == "V":
                                act.wait_ge(kv_dve, kv_use(kind, what) + 1)
                                act.activation(v_hl[:, 2 * what:2 * what + 2, 0:HID],
                                               v_staged(what).rearrange("p (t n) -> p t n", t=2), ACT.Copy)\
                                   .then_inc(kv_act, 1)
                            elif kind == "W":
                                act.wait_ge(t_full, t_use[kind, what] + 1)
                                for et in range(CT):
                                    ins = act.activation(wo_hi[:, what, et, :],
                                                         bank_for(kind, what)[:, et * HID:(et + 1) * HID], ACT.Copy,
                                                         scale=subln_s[:, et:et + 1])
                                ins.then_inc(t_hi, 1)

                    @block.vector
                    def _(dve):
                        def q_low(what):
                            u, s, m = what
                            dve.wait_ge(r_hi, n_qp[what] + 1)
                            bank = FIRST_Q_BANKS[s] if u == 0 else bank_for("QP", what)
                            dve.scalar_tensor_tensor(out=q_lo[:, u % 2, s, m, :], in0=bank[:, 0:HID],
                                                     scalar=bqk[:, 2 * s + m:2 * s + m + 1],
                                                     in1=q_hi[:, u % 2, s, m, :].bitcast(F32),
                                                     op0=ALU.add, op1=ALU.subtract).then_inc(r_free, 1)

                        dve.tensor_scalar(bqk[:, 0:4], bqk_raw[:, 0:4], SCALE, None, ALU.mult).then_inc(b_ready, 1)
                        dve.tensor_copy(bqk[:, 4:6], bqk_raw[:, 4:6]).then_inc(b_ready, 1)
                        dve.tensor_scalar(subln_s[:, :], subln_col[:, :], 1.0 - LAMBDA_INIT, None, ALU.mult)\
                           .then_inc(b_ready, 1)
                        for n, u in enumerate(W_PAIRS):
                            dve.wait_ge(t_hi, n + 1)
                            src = W_BANKS[n][:, :].rearrange("p (c n) -> p c n", c=CT)
                            hi, lo = (wq_hi, wq_lo) if u < 2 else (wkv_hi, wkv_lo)
                            cols = slice(u % 2 * HID, (u % 2 + 1) * HID)
                            dve.scalar_tensor_tensor(out=lo[:, :, cols], in0=src, scalar=SCALE if u < 2 else 1.0,
                                                     in1=hi[:, :, cols].bitcast(F32), op0=ALU.mult,
                                                     op1=ALU.subtract).then_inc(t_lo, 1)
                        dve.wait_ge(b_ready, 3)
                        def k_low(bank, m, c, read):
                            cols = slice(c * BANK, (c + 1) * BANK)
                            dve.scalar_tensor_tensor(out=k_lo[:, m, cols], in0=bank[:, :],
                                                     scalar=bqk[:, 4 + m:5 + m], in1=k_hi[:, m, cols].bitcast(F32),
                                                     op0=ALU.add, op1=ALU.subtract).then_inc(read, 1)

                        for c in range(K_USES):
                            dve.wait_ge(s_act, c + 1)
                            k_low(S[c], 0, c, s_dve)
                            q_low((0, c % 2, c // 2))

                        for kind, what, _, factors, mixes in with_lags(steps, VECTOR_LAGS):
                            if kind == "S":
                                d, m, j = what
                                _, s, _, c, w, last = duo_chunks(d)[j]
                                k = s_use(d, m, j)
                                dve.wait_ge(s_full, k + 1)
                                if last:
                                    dve.tensor_tensor_reduce(out=S[k % NS][:, 0:w], in0=S[k % NS][:, 0:w],
                                                             in1=mask[:, BANK - w:], scale=1.0, scalar=LOWEST,
                                                             op0=ALU.add, op1=ALU.max,
                                                             accum_out=mx[:, d % 2, m, s, c:c + 1]).then_inc(s_dve, 1)
                                else:
                                    dve.tensor_reduce(mx[:, d % 2, m, s, c:c + 1], S[k % NS][:, 0:w], X, ALU.max)\
                                       .then_inc(s_dve, 1)
                                if last:
                                    dve.wait_ge(s_dve, k + 1)
                                    dve.tensor_reduce(negmx[:, d % 2, m, s:s + 1], mx[:, d % 2, m, s, 0:c + 1], X,
                                                      ALU.max, negate=True).then_inc(neg_ready, 1)
                            elif kind == "T":
                                d, j = what
                                w, q, u = duo_chunks(d)[j][4], CHUNKS * d + j, t_use[kind, what]
                                dve.wait_ge(t_hi, u + 1)
                                dve.tensor_tensor(pT_lo[:, q % PT_SLOTS, 0:w], bank_for(kind, what)[:, 0:w],
                                                  pT_hi[:, q % PT_SLOTS, 0:w].bitcast(F32), ALU.subtract)\
                                   .then_inc(t_lo, 1)
                            elif kind == "PV":
                                d, j = what
                                o, _, _, _, _, last = duo_chunks(d)[j]
                                if last:
                                    dve.wait_ge(o_half_ready, o + 1)
                                    if o >= 2:
                                        dve.wait_ge(t_full, t_use["OT", o - 2] + 1)
                                        dve.wait_ge(msq_ready, o - 1)
                                    dve.tensor_tensor(o_sum[:, o % 2, :], bank_for(kind, o)[:, 0:HID],
                                                      o_half[:, o % 2, :], ALU.add)\
                                       .then_inc(o_ready, 1)
                            elif kind == "OT":
                                o, u = what, t_use[kind, what]
                                dve.wait_ge(t_hi, u + 1)
                                dve.tensor_tensor(oT_lo[:, o % 2, :], bank_for(kind, o)[:, 0:HID],
                                                  oT_hi[:, o % 2, :].bitcast(F32), ALU.subtract).then_inc(t_lo, 1)
                            elif kind == "QP":
                                q_low(what)
                            elif kind == "K":
                                dve.wait_ge(kv_act, kv_use(kind, what) + 1)
                                k_low(bank_for(kind, what), 1, what, kv_dve)
                            elif kind == "V":
                                dve.wait_ge(kv_full, kv_use(kind, what) + 1)
                                if what >= 2:
                                    dve.wait_ge(v_lo, what - 1)
                                dve.tensor_tensor(v_staged(what), bank_for(kind, what)[:, :],
                                                  bv[:, :, :].rearrange("p t n -> p (t n)"), ALU.add)\
                                   .then_inc(kv_dve, 1)
                            elif kind == "W":
                                dve.wait_ge(t_hi, t_use[kind, what] + 1)
                                for et in range(CT):
                                    ins = dve.scalar_tensor_tensor(
                                        out=wo_lo[:, what, et, :], in0=bank_for(kind, what)[:, et * HID:(et + 1) * HID],
                                        scalar=subln_s[:, et:et + 1], in1=wo_hi[:, what, et, :].bitcast(F32),
                                        op0=ALU.mult, op1=ALU.subtract)
                                ins.then_inc(t_lo, 1)
                            elif kind == "OP":
                                o, u = what, r_use[kind, what]
                                _, i = tile_of(o)
                                dve.wait_ge(r_full, u + 1)
                                dve.wait_ge(rms_ready, o + 1)
                                dve.wait_ge(r_free, u)
                                dve.scalar_tensor_tensor(out=acc[:, i, :], in0=bank_for(kind, o)[:, 0:HID],
                                                         scalar=rms[:, o % 4:o % 4 + 1], in1=acc[:, i, :],
                                                         op0=ALU.mult, op1=ALU.add).then_inc(r_free, 1)
                            for o in factors:
                                d, chunks = o // 2, [ch for ch in duo_chunks(o // 2) if ch[0] == o]
                                s, nch = chunks[0][1], len(chunks)
                                last_j = max(j for j, ch in enumerate(duo_chunks(d)) if ch[0] == o)
                                dve.wait_ge(s_act, s_use(d, 1, last_j) + 1)
                                dve.tensor_reduce(s12[:, d % 4, s, :], ssum[:, d % 4, s, :, 0:nch], X, ALU.add)\
                                   .then_inc(sums_ready, 1)
                            for d, j in mixes:
                                if j in DVE_MIXES:
                                    o, s, _, _, w, _ = duo_chunks(d)[j]
                                    q = CHUNKS * d + j
                                    a, b = e1[:, q % E1_SLOTS, 0:w], e2[:, q % E2_SLOTS, 0:w]
                                    dve.wait_ge(ratio_ready, o + 1)
                                    dve.scalar_tensor_tensor(out=a, in0=b, scalar=ratio[:, d % 4, s:s + 1], in1=a,
                                                             op0=ALU.mult, op1=ALU.add).then_inc(p_dve, 1)

                    @block.gpsimd
                    def _(pool):
                        def factor(o):
                            d, s = o // 2, tile_of(o)[0]
                            pool.wait_ge(sums_ready, o + 1)
                            pool.tensor_tensor(inv_s2[:, d % 4, s:s + 1], s12[:, d % 4, s, 1:2], neg_one[:, :],
                                               ALU.pow).then_inc(ratio_step, 1)
                            pool.wait_ge(ratio_step, o + 1)
                            pool.tensor_scalar(ratio[:, d % 4, s:s + 1], s12[:, d % 4, s, 0:1],
                                               inv_s2[:, d % 4, s:s + 1], neg_lam[:, 0:1], ALU.mult, ALU.mult)\
                                .then_inc(ratio_ready, 1)

                        def mix(d, j):
                            o, s, _, _, w, _ = duo_chunks(d)[j]
                            q = CHUNKS * d + j
                            a, b = e1[:, q % E1_SLOTS, 0:w], e2[:, q % E2_SLOTS, 0:w]
                            pool.wait_ge(ratio_ready, o + 1)
                            pool.tensor_scalar(b, b, ratio[:, d % 4, s:s + 1], 0.0, ALU.mult, ALU.add)\
                                .then_inc(e2_scaled, 1)
                            pool.wait_ge(e2_scaled, pool_mixed[q])
                            pool.tensor_tensor(a, a, b, ALU.add).then_inc(p_pool, 1)

                        def norm(o):
                            d, s, c = o // 2, tile_of(o)[0], slice(o % 4, o % 4 + 1)
                            s1 = s12[:, d % 4, s, 0:1]
                            pool.wait_ge(msq_ready, o + 1)
                            pool.tensor_tensor(rms_a[:, c], s1, s1, ALU.mult).then_inc(rms_step, 1)
                            pool.wait_ge(rms_step, 2 * o + 1)
                            pool.tensor_scalar(rms_b[:, c], rms_a[:, c], EPS, msq[:, c], ALU.mult, ALU.add)\
                                .then_inc(rms_step, 1)
                            pool.wait_ge(rms_step, 2 * o + 2)
                            if o >= 4:
                                pool.wait_ge(r_free, r_use["OP", o - 4] + 1)
                            pool.tensor_tensor(rms[:, c], rms_b[:, c], half_neg[:, 0:1], ALU.pow)\
                                .then_inc(rms_ready, 1)

                        for kind, what, _, factors, mixes in steps:
                            for o in factors:
                                factor(o)
                            if kind == "OT":
                                norm(what)
                            elif kind == "V":
                                pool.wait_ge(kv_act, kv_use(kind, what) + 1)
                                pool.tensor_tensor(v_hl[:, 2 * what:2 * what + 2, HID:2 * HID],
                                                   v_staged(what).rearrange("p (t n) -> p t n", t=2),
                                                   v_hl[:, 2 * what:2 * what + 2, 0:HID].bitcast(F32), ALU.subtract)\
                                    .then_inc(v_lo, 1)
                            for d, j in mixes:
                                if j not in DVE_MIXES:
                                    mix(d, j)

                nc.all_engine_barrier(sems_to_clear=range(sems[0].num, sems[-1].num + 1))

        with ExitStack() as ffn:
            sf = tensors(ffn)
            wug_hi = sf("wug_hi", [P, CT, 2 * INTER], F32R)
            wug_lo = sf("wug_lo", [P, CT, 2 * INTER], F32R)
            JT = INTER // P
            wd_hl = sf("wd_hl", [P, JT, 2 * HID], F32R)
            x_res = sf("x_res", [P, TILES, HID])
            z = sf("z", [P, 4, HID])
            y_stats = sf("y_stats", [P, 4, 6])
            y_mv = sf("y_mv", [P, 4, 2])
            y_var = sf("y_var", [P, 4])
            y_rs = sf("y_rs", [P, 4])
            y_mr = sf("y_mr", [P, 4])
            z_stats = sf("z_stats", [P, 4, 6])
            z_mv = sf("z_mv", [P, 4, 2])
            z_var = sf("z_var", [P, 4])
            z_rs = sf("z_rs", [P, 4])
            y_step, y_pool, y_rstd, z_rstd, z_ready, first_x_landed, x_landed = semaphores(
                ffn, "y_step", "y_pool", "y_rstd", "z_rstd", "z_ready", "first_x_landed", "x_res_landed")

            def norms(dve, c, part):
                tiles = range(4 * c, 4 * c + 4)
                if part == 0:
                    for t in tiles:
                        dve.bn_stats(y_stats[:, t % 4, :], acc[:, t, :]).then_inc(y_step, 1)
                    dve.wait_ge(y_step, 24 * c + 4)
                    for t in tiles:
                        dve.bn_aggr(y_mv[:, t % 4, :], y_stats[:, t % 4, :]).then_inc(y_step, 1)
                elif part == 1:
                    dve.wait_ge(y_rstd, c + 1)
                    for t in tiles:
                        dve.scalar_tensor_tensor(out=acc[:, t, :], in0=acc[:, t, :], scalar=y_rs[:, t % 4:t % 4 + 1],
                                                 in1=x_res[:, t, :], op0=ALU.mult, op1=ALU.add).then_inc(y_step, 1)
                    dve.wait_ge(y_step, 24 * c + 12)
                    for t in tiles:
                        dve.tensor_scalar(acc[:, t, :], acc[:, t, :], y_mr[:, t % 4:t % 4 + 1], None, ALU.subtract)\
                           .then_inc(y_step, 1)
                elif part == 2:
                    dve.wait_ge(y_step, 24 * c + 16)
                    for t in tiles:
                        dve.bn_stats(z_stats[:, t % 4, :], acc[:, t, :]).then_inc(y_step, 1)
                    dve.wait_ge(y_step, 24 * c + 20)
                    for t in tiles:
                        dve.bn_aggr(z_mv[:, t % 4, :], z_stats[:, t % 4, :]).then_inc(y_step, 1)
                else:
                    dve.wait_ge(z_rstd, c + 1)
                    for t in tiles:
                        dve.tensor_scalar(z[:, t % 4, :], acc[:, t, :], z_mv[:, t % 4, 0:1], z_rs[:, t % 4:t % 4 + 1],
                                          ALU.subtract, ALU.mult).then_inc(z_ready, 1)

            def rstds(pool, c, part):
                if part == 0:
                    pool.wait_ge(y_step, 24 * c + 8)
                    pool.tensor_scalar(y_var[:, :], y_mv[:, :, 1], 1.0, EPS, ALU.mult, ALU.add).then_inc(y_pool, 1)
                    pool.wait_ge(y_pool, 3 * c + 1)
                    pool.tensor_tensor(y_rs[:, :], y_var[:, :], half_neg[:, :], ALU.pow).then_inc(y_pool, 1)
                    pool.wait_ge(y_pool, 3 * c + 2)
                    pool.tensor_tensor(y_mr[:, :], y_rs[:, :], y_mv[:, :, 0], ALU.mult).then_inc(y_rstd, 1)
                else:
                    pool.wait_ge(y_step, 24 * c + 24)
                    pool.tensor_scalar(z_var[:, :], z_mv[:, :, 1], 1.0, EPS, ALU.mult, ALU.add).then_inc(y_pool, 1)
                    pool.wait_ge(y_pool, 3 * c + 3)
                    pool.tensor_tensor(z_rs[:, :], z_var[:, :], half_neg[:, :], ALU.pow).then_inc(z_rstd, 1)

            with ExitStack() as fold:
                sg = tensors(fold)
                raw = sg("raw", [P, 2 * JT, HID])
                raw_d = sg("raw_d", [P, CT, INTER])
                bf = [sg(f"bf{k}", [P, CT, INTER]) for k in range(2)]
                wt_hi = sg("wt_hi", [P, 2, CT, BANK], F32R)
                wt_lo = sg("wt_lo", [P, 2, CT, BANK], F32R)
                hd = [sg(f"hd{k}", [P, P]) for k in range(2)]
                had = sg("had", [P, P], F32R)
                had_neg = sg("had_neg", [P, P], F32R)
                scol = sg("scol", [P, 2 * JT])
                sdcol = sg("sdcol", [P, CT])
                su_col = sg("su_col", [P, CT])
                sud_col = sg("sud_col", [P, JT])
                scaled_col = sg("scaled_col", [P, 2 * JT + CT])
                raw_landed = semaphores(fold, *[f"raw_landed{q}" for q in range(4)])
                (down_landed, cols_landed, cols_ready, raw_scaled, raw_scaled_act, down_scaled, down_step, down_pool, ft_full, ft_hi, ft_lo, fs_full,
                 fs_hi, fs_lo, had_step) = semaphores(
                    fold, "down_landed", "cols_landed", "cols_ready", "raw_scaled", "raw_scaled_act", "down_scaled",
                    "down_step", "down_pool", "ft_full", "ft_hi",
                    "ft_lo", "fs_full", "fs_hi", "fs_lo", "had_step")
                block = fold.enter_context(nc.Block())

                @block.sync
                def _(sp):
                    sp.dma_start(scol[:, :], ws_ug.rearrange("(t p) -> p t", p=P)).then_inc(cols_landed, 16)
                    sp.dma_start(sdcol[:, :], ws_dp.rearrange("(t p) -> p t", p=P)).then_inc(cols_landed, 16)
                    sp.dma_start(su_col[:, :], su_ug.rearrange("(t p) -> p t", p=P)).then_inc(cols_landed, 16)
                    sp.dma_start(sud_col[:, :], su_dp.rearrange("(t p) -> p t", p=P)).then_inc(cols_landed, 16)
                    for q in range(4):
                        w = (w_up if q < 2 else w_gate).rearrange("(t p) c -> p t c", p=P)
                        sp.dma_start(raw[:, 4 * q:4 * q + 4, :], w[:, q % 2 * 4:q % 2 * 4 + 4, :])\
                          .then_inc(raw_landed[q], 16)
                        if q == 0:
                            sp.dma_start(x_res[:, 0:4, :], x_tiles[:, 0:4, :]).then_inc(first_x_landed, 16)
                    sp.dma_start(raw_d[:, :, :], w_down.rearrange("(t p) c -> p t c", p=P)).then_inc(down_landed, 16)
                    sp.dma_start(x_res[:, 4:, :], x_tiles[:, 4:, :]).then_inc(x_landed, 16)
                    sp.wait_ge(x_landed, 16)

                TURN_BANKS = (*T, O, R)

                @block.tensor
                def _(pe):
                    def turn(u):
                        if u >= 4:
                            pe.wait_ge(ft_lo, u - 3)
                        if u < 8:
                            q, ct = divmod(u, CT)
                            if ct == 0:
                                pe.wait_ge(raw_scaled, 2 * q + 2)
                                pe.wait_ge(raw_scaled_act, 2 * q + 2)
                            for t in range(4):
                                mm = pe.transpose(TURN_BANKS[u % 4][:, t * P:(t + 1) * P],
                                                  raw[:, 4 * q + t, ct * P:(ct + 1) * P], ident[:, :])
                        else:
                            if u == 8:
                                pe.wait_ge(down_step, 6)
                                pe.wait_ge(down_pool, 6)
                            for k in range(2):
                                for it in range(CT):
                                    jt = 2 * (u - 8) + k
                                    mm = pe.transpose(TURN_BANKS[u % 4][:, k * HID + it * P:k * HID + (it + 1) * P],
                                                      bf[0][:, it, jt * P:(jt + 1) * P], ident[:, :])
                        mm.then_inc(ft_full, 1)

                    def bank(k):
                        if k >= NS:
                            pe.wait_ge(fs_lo, k - NS + 1)
                        return S[k % NS]

                    turn(0)
                    turn(1)
                    for q in range(4):
                        turn(2 * q + 2)
                        turn(2 * q + 3)
                        pe.wait_ge(ft_lo, 2 * q + 2)
                        if q == 0:
                            pe.wait_ge(had_step, 16)
                        for co in range(CT):
                            b, n = bank(2 * q + co), 0
                            for ct in range(CT):
                                h = had_neg if co == 1 and ct == 1 else had
                                for w in (wt_hi, wt_lo):
                                    mm = pe.matmul(b[:, :], h[:, :], w[:, q % 2, ct, :], start=(n == 0),
                                                   stop=(n == 3))
                                    n += 1
                            mm.then_inc(fs_full, 1)
                    for u in range(8, 12):
                        if u + 2 < 12:
                            turn(u + 2)
                        pe.wait_ge(ft_lo, u + 1)
                        b = bank(u)
                        pe.matmul(b[:, :], had[:, :], wt_hi[:, u // 2 % 2, u % 2, :], start=True, stop=False)
                        pe.matmul(b[:, :], had[:, :], wt_lo[:, u // 2 % 2, u % 2, :], start=False, stop=True)\
                          .then_inc(fs_full, 1)

                def hi_of_turn(act, u):
                    act.wait_ge(ft_full, u + 1)
                    if u >= 4:
                        act.wait_ge(fs_full, u - u % 2 - 2)
                    act.activation(wt_hi[:, u // 2 % 2, u % 2, :], TURN_BANKS[u % 4][:, :], ACT.Copy).then_inc(ft_hi, 1)

                def hi_of_fold(act, k):
                    act.wait_ge(fs_full, k + 1)
                    if k < 8:
                        q, co = divmod(k, CT)
                        act.activation(wug_hi[:, co, q * BANK:(q + 1) * BANK], S[k % NS][:, :], ACT.Copy,
                                       scale=su_col[:, co:co + 1]).then_inc(fs_hi, 1)
                    else:
                        for a in range(2):
                            jt = 2 * (k - 8) + a
                            ins = act.activation(wd_hl[:, jt, 0:HID], S[k % NS][:, a * HID:(a + 1) * HID], ACT.Copy,
                                                 scale=sud_col[:, jt:jt + 1])
                        ins.then_inc(fs_hi, 1)

                def lo_of_turn(dve, u):
                    dve.wait_ge(ft_hi, u + 1)
                    dve.tensor_tensor(wt_lo[:, u // 2 % 2, u % 2, :], TURN_BANKS[u % 4][:, :],
                                      wt_hi[:, u // 2 % 2, u % 2, :].bitcast(F32), ALU.subtract).then_inc(ft_lo, 1)

                def lo_of_fold(dve, k):
                    dve.wait_ge(fs_hi, k + 1)
                    if k < 8:
                        q, co = divmod(k, CT)
                        dve.scalar_tensor_tensor(out=wug_lo[:, co, q * BANK:(q + 1) * BANK], in0=S[k % NS][:, :],
                                                 scalar=su_col[:, co:co + 1],
                                                 in1=wug_hi[:, co, q * BANK:(q + 1) * BANK].bitcast(F32),
                                                 op0=ALU.mult, op1=ALU.subtract).then_inc(fs_lo, 1)
                    else:
                        for a in range(2):
                            jt = 2 * (k - 8) + a
                            ins = dve.scalar_tensor_tensor(out=wd_hl[:, jt, HID:2 * HID],
                                                           in0=S[k % NS][:, a * HID:(a + 1) * HID],
                                                           scalar=sud_col[:, jt:jt + 1],
                                                           in1=wd_hl[:, jt, 0:HID].bitcast(F32),
                                                           op0=ALU.mult, op1=ALU.subtract)
                        ins.then_inc(fs_lo, 1)

                @block.scalar
                def _(act):
                    def scale_raw(q):
                        act.wait_ge(raw_landed[q], 16)
                        for t in (4 * q, 4 * q + 1):
                            act.activation(raw[:, t, :], raw[:, t, :], ACT.Copy, scale=scaled_col[:, t:t + 1])\
                               .then_inc(raw_scaled_act, 1)

                    act.wait_ge(cols_ready, 2)
                    scale_raw(0)
                    scale_raw(1)
                    hi_of_turn(act, 0)
                    hi_of_turn(act, 1)
                    scale_raw(2)
                    for q in range(4):
                        if q == 1:
                            scale_raw(3)
                            act.wait_ge(down_landed, 16)
                            for it in range(CT):
                                act.activation(bf[1][:, it, :], raw_d[:, it, :], ACT.Copy,
                                               scale=scaled_col[:, 2 * JT + it:2 * JT + it + 1])\
                                   .then_inc(down_scaled, 1)
                        hi_of_turn(act, 2 * q + 2)
                        hi_of_turn(act, 2 * q + 3)
                        hi_of_fold(act, 2 * q)
                        hi_of_fold(act, 2 * q + 1)
                    for u in range(8, 12):
                        if u + 2 < 12:
                            hi_of_turn(act, u + 2)
                        hi_of_fold(act, u)

                def butterflies(eng, it, step):
                    for stage in range(3):
                        src, dst = bf[(stage + 1) % 2], bf[stage % 2]
                        if stage == 0:
                            eng.wait_ge(down_scaled, it + 1)
                        else:
                            eng.wait_ge(step, 2 * stage)
                        a = src[:, it, :].rearrange("p (n two h) -> p n two h", two=2, h=P << stage)
                        b = dst[:, it, :].rearrange("p (n two h) -> p n two h", two=2, h=P << stage)
                        eng.tensor_tensor(b[:, :, 0, :], a[:, :, 0, :], a[:, :, 1, :], ALU.add).then_inc(step, 1)
                        eng.tensor_tensor(b[:, :, 1, :], a[:, :, 0, :], a[:, :, 1, :], ALU.subtract)\
                           .then_inc(step, 1)

                @block.gpsimd
                def _(pool):
                    def scale_raw(q):
                        pool.wait_ge(raw_landed[q], 16)
                        for t in (4 * q + 2, 4 * q + 3):
                            pool.tensor_scalar(raw[:, t, :], raw[:, t, :], scaled_col[:, t:t + 1], 0.0, ALU.mult,
                                               ALU.add).then_inc(raw_scaled, 1)

                    rstds(pool, 0, 0)
                    pool.wait_ge(cols_ready, 2)
                    scale_raw(0)
                    scale_raw(1)
                    rstds(pool, 0, 1)
                    scale_raw(2)
                    scale_raw(3)
                    butterflies(pool, 1, down_pool)

                @block.vector
                def _(dve):
                    norms(dve, 0, 0)
                    dve.wait_ge(cols_landed, 64)
                    dve.tensor_scalar(scaled_col[:, 0:2 * JT], scol[:, :], float(HID) ** -0.5, None, ALU.mult)\
                       .then_inc(cols_ready, 1)
                    dve.tensor_scalar(scaled_col[:, 2 * JT:], sdcol[:, :], float(INTER) ** -0.5, None, ALU.mult)\
                       .then_inc(cols_ready, 1)
                    src = ident
                    k = 0
                    for stage in range(7):
                        h = 1 << stage
                        dst = hd[stage % 2]
                        a = src[:, :].rearrange("p (n two h) -> p n two h", two=2, h=h)
                        b = dst[:, :].rearrange("p (n two h) -> p n two h", two=2, h=h)
                        dve.tensor_tensor(b[:, :, 0, :], a[:, :, 0, :], a[:, :, 1, :], ALU.add).then_inc(had_step, 1)
                        dve.tensor_tensor(b[:, :, 1, :], a[:, :, 0, :], a[:, :, 1, :], ALU.subtract)\
                           .then_inc(had_step, 1)
                        k += 2
                        dve.wait_ge(had_step, k)
                        src = dst
                    dve.tensor_copy(had[:, :], src[:, :]).then_inc(had_step, 1)
                    dve.tensor_scalar(had_neg[:, :], src[:, :], -1.0, None, ALU.mult).then_inc(had_step, 1)
                    dve.wait_ge(first_x_landed, 16)
                    norms(dve, 0, 1)
                    lo_of_turn(dve, 0)
                    lo_of_turn(dve, 1)
                    norms(dve, 0, 2)
                    for q in range(4):
                        if q == 1:
                            norms(dve, 0, 3)
                        if q == 2:
                            butterflies(dve, 0, down_step)
                        lo_of_turn(dve, 2 * q + 2)
                        lo_of_turn(dve, 2 * q + 3)
                        lo_of_fold(dve, 2 * q)
                        lo_of_fold(dve, 2 * q + 1)
                    for u in range(8, 12):
                        if u + 2 < 12:
                            lo_of_turn(dve, u + 2)
                        lo_of_fold(dve, u)

            h_hi = sf("h_hi", [P, 2, JT, BANK], F32R)
            h_lo = sf("h_lo", [P, 2, JT, BANK], F32R)
            gate = sf("gate", [P, 2, BANK])
            h_f = sf("h_f", [P, 2, BANK])
            d_half = sf("d_half", [P, 2, HID])
            d_sum = sf("d_sum", [P, 2, HID])
            d_out = sf("d_out", [P, 2, HID])
            st3 = sf("st6", [P, 2, 6])
            mv3 = sf("mv6", [P, 2, 2])
            ve3 = sf("ve6", [P, 2])
            rs3 = sf("rs6", [P, 2])
            mr3 = sf("mr6", [P, 2])
            (z_full, z_hi, z_lo, g_full, u_full, g_act, h_ready, h_hi_ready, h_lo_ready, d_full, d_half_ready,
             d_stats, d_rstd, d_final, stored_even, stored_odd, d_step, pool_step) = semaphores(
                ffn, "z_full", "z_hi", "z_lo", "g_full", "u_full", "g_act", "h_ready", "h_hi_ready", "h_lo_ready",
                "d_full", "d_half_ready", "d_stats", "d_rstd", "d_final", "stored_even", "stored_odd", "d_step",
                "pool_step")
            stored = (stored_even, stored_odd)
            NC = SEQ // BANK
            D_BANKS = (O, R)
            NORM_TURNS = (0, 2, 3, 5)
            block = ffn.enter_context(nc.Block())

            order = []
            for c in range(NC):
                order.append(("UG", c))
                if c >= 1:
                    order.append(("DN", c - 1))
            order.append(("DN", NC - 1))

            @block.sync
            def _(sp):
                for t in range(TILES):
                    sp.wait_ge(d_final, t + 1)
                    sp.dma_start(out_tiles[:, t, :], d_out[:, t % 2, :]).then_inc(stored[t % 2], 16)
                for parity in range(2):
                    sp.wait_ge(stored[parity], 16 * (TILES // 2))

            @block.tensor
            def _(pe):
                def turn_z(c):
                    pe.wait_ge(z_ready, 4 * c + 4)
                    for ct in range(CT):
                        u = CT * c + ct
                        if u >= 2:
                            pe.wait_ge(z_lo, u - 1)
                        for t in range(4):
                            mm = pe.transpose(T[u % 2][:, t * P:(t + 1) * P], z[:, t, ct * P:(ct + 1) * P],
                                              ident[:, :])
                        mm.then_inc(z_full, 1)

                turn_z(0)
                for kind, c in order:
                    if kind == "UG":
                        pe.wait_ge(z_lo, CT * c + CT)
                        for jt in range(JT):
                            k = JT * c + jt
                            for part, bank, full in ((1, S[2 * (k % 2)], g_full), (0, S[2 * (k % 2) + 1], u_full)):
                                if k >= 2:
                                    pe.wait_ge(g_act if part else h_ready, k - 1)
                                col, n = part * INTER + jt * P, 0
                                for ct in range(CT):
                                    for w, x in ((wug_hi, xT_hi), (wug_hi, xT_lo), (wug_lo, xT_hi)):
                                        mm = pe.matmul(bank[:, :], w[:, ct, col:col + P],
                                                       x[:, ct, c * BANK:(c + 1) * BANK], start=(n == 0),
                                                       stop=(n == 5))
                                        n += 1
                                mm.then_inc(full, 1)
                            if jt == JT - 2 and c + 1 < NC:
                                turn_z(c + 1)
                    else:
                        pe.wait_ge(h_lo_ready, JT * c + JT)
                        for tt in range(QB):
                            t = QB * c + tt
                            bank = D_BANKS[t % 2]
                            if t >= 2:
                                pe.wait_ge(d_step, t - 1)
                            for jt in range(JT):
                                pe.matmul(bank[:, :], h_hi[:, c % 2, jt, tt * P:(tt + 1) * P], wd_hl[:, jt, :],
                                          start=(jt == 0), stop=False)
                                mm = pe.matmul(bank[:, 0:HID], h_lo[:, c % 2, jt, tt * P:(tt + 1) * P],
                                               wd_hl[:, jt, 0:HID], start=False, stop=(jt == JT - 1))
                            mm.then_inc(d_full, 1)

            @block.scalar
            def _(act):
                def hi_z(c):
                    for ct in range(CT):
                        u = CT * c + ct
                        act.wait_ge(z_full, u + 1)
                        act.activation(xT_hi[:, ct, c * BANK:(c + 1) * BANK], T[u % 2][:, :], ACT.Copy)\
                           .then_inc(z_hi, 1)

                hi_z(0)
                for kind, c in order:
                    if kind == "UG":
                        for jt in range(JT + 1):
                            k = JT * c + jt
                            if jt < JT:
                                act.wait_ge(g_full, k + 1)
                                if k >= 2:
                                    act.wait_ge(h_ready, k - 1)
                                act.activation(gate[:, k % 2, :], S[2 * (k % 2)][:, :], ACT.Silu).then_inc(g_act, 1)
                            if jt >= 1:
                                act.wait_ge(h_ready, k)
                                if c >= 2:
                                    act.wait_ge(d_full, QB * (c - 1))
                                act.activation(h_hi[:, c % 2, jt - 1, :], h_f[:, (k - 1) % 2, :], ACT.Copy)\
                                   .then_inc(h_hi_ready, 1)
                            if jt == JT - 1 and c + 1 < NC:
                                hi_z(c + 1)
                    else:
                        for t in range(QB * c, QB * c + QB):
                            act.wait_ge(d_full, t + 1)
                            if t >= 2:
                                act.wait_ge(d_step, t - 1)
                            act.activation(d_half[:, t % 2, :], D_BANKS[t % 2][:, HID:2 * HID], ACT.Copy)\
                               .then_inc(d_half_ready, 1)

            @block.vector
            def _(dve):
                count = {"d": 0}

                def lo_z(c):
                    for ct in range(CT):
                        u = CT * c + ct
                        dve.wait_ge(z_hi, u + 1)
                        dve.tensor_tensor(xT_lo[:, ct, c * BANK:(c + 1) * BANK], T[u % 2][:, :],
                                          xT_hi[:, ct, c * BANK:(c + 1) * BANK].bitcast(F32), ALU.subtract)\
                           .then_inc(z_lo, 1)

                def finish(t):
                    dve.wait_ge(d_rstd, t + 1)
                    if t >= 2:
                        dve.wait_ge(stored[t % 2], 16 * (t // 2))
                    dve.scalar_tensor_tensor(out=d_out[:, t % 2, :], in0=d_sum[:, t % 2, :],
                                             scalar=rs3[:, t % 2:t % 2 + 1], in1=acc[:, t, :], op0=ALU.mult,
                                             op1=ALU.add).then_inc(d_stats, 1)
                    count["d"] += 1
                    dve.wait_ge(d_stats, count["d"])
                    dve.tensor_scalar(d_out[:, t % 2, :], d_out[:, t % 2, :], mr3[:, t % 2:t % 2 + 1], None,
                                      ALU.subtract).then_inc(d_final, 1)

                lo_z(0)
                for kind, c in order:
                    if kind == "UG":
                        for jt in range(JT):
                            k = JT * c + jt
                            dve.wait_ge(g_act, k + 1)
                            dve.wait_ge(u_full, k + 1)
                            if k >= 2:
                                dve.wait_ge(h_lo_ready, k - 1)
                            dve.tensor_tensor(h_f[:, k % 2, :], S[2 * (k % 2) + 1][:, :], gate[:, k % 2, :],
                                              ALU.mult).then_inc(h_ready, 1)
                            if c + 1 < NC and jt in NORM_TURNS:
                                part = NORM_TURNS.index(jt)
                                if part == 3:
                                    dve.wait_ge(z_full, CT * (c + 1))
                                norms(dve, c + 1, part)
                            if c + 1 < NC and jt == JT - 2:
                                lo_z(c + 1)
                    else:
                        for t in range(QB * c, QB * c + QB):
                            dve.wait_ge(d_half_ready, t + 1)
                            if t >= 2:
                                dve.wait_ge(d_final, t - 1)
                            dve.tensor_tensor(d_sum[:, t % 2, :], D_BANKS[t % 2][:, 0:HID], d_half[:, t % 2, :],
                                              ALU.add).then_inc(d_step, 1)
                            dve.wait_ge(d_step, t + 1)
                            dve.bn_stats(st3[:, t % 2, :], d_sum[:, t % 2, :]).then_inc(d_stats, 1)
                            count["d"] += 1
                            dve.wait_ge(d_stats, count["d"])
                            dve.bn_aggr(mv3[:, t % 2, :], st3[:, t % 2, :]).then_inc(d_stats, 1)
                            count["d"] += 1
                            dve.wait_ge(d_stats, count["d"])
                            if t >= 1:
                                finish(t - 1)
                finish(TILES - 1)

            def planned_d_counts():
                n, out_ = 0, []
                for t in range(TILES):
                    n += 2
                    out_.append(n)
                    if t >= 1:
                        n += 1
                return out_

            @block.gpsimd
            def _(pool):
                step = 0
                dc = planned_d_counts()

                def inverse_std(dst, tmp, var, w):
                    nonlocal step
                    pool.tensor_scalar(tmp, var, 1.0, EPS, ALU.mult, ALU.add).then_inc(pool_step, 1)
                    step += 1
                    pool.wait_ge(pool_step, step)
                    pool.tensor_tensor(dst, tmp, half_neg[:, 0:w], ALU.pow).then_inc(pool_step, 1)
                    step += 1
                    pool.wait_ge(pool_step, step)

                for kind, c in order:
                    if kind == "UG":
                        for jt in range(JT):
                            k = JT * c + jt
                            if c + 1 < NC and jt in (1, 4):
                                rstds(pool, c + 1, jt // 4)
                            pool.wait_ge(h_hi_ready, k + 1)
                            pool.tensor_tensor(h_lo[:, c % 2, jt, :], h_f[:, k % 2, :],
                                               h_hi[:, c % 2, jt, :].bitcast(F32), ALU.subtract)\
                                .then_inc(h_lo_ready, 1)
                    else:
                        for t in range(QB * c, QB * c + QB):
                            b = slice(t % 2, t % 2 + 1)
                            pool.wait_ge(d_stats, dc[t])
                            inverse_std(rs3[:, b], ve3[:, b], mv3[:, t % 2, 1:2], 1)
                            pool.tensor_tensor(mr3[:, b], rs3[:, b], mv3[:, t % 2, 0:1], ALU.mult)\
                                .then_inc(d_rstd, 1)


_INS = ['L0_attn_hidden_states', 'L0_attn_Wqkv_w', 'L0_attn_Wqkv_b', 'L0_attn_lambda_q1', 'L0_attn_lambda_k1',
        'L0_attn_lambda_q2', 'L0_attn_lambda_k2', 'L0_attn_subln_w', 'L0_attn_out_w', 'L0_attn_out_b',
        'L0_ffn_SU_ug', 'L0_ffn_SU_dp', 'L0_ffn_Wscale_ug', 'L0_ffn_Wscale_dp', 'L0_ffn_W_up', 'L0_ffn_W_gate',
        'L0_ffn_W_down']


def kernel(**inputs):
    import numpy as _np
    import concourse.bacc as _bacc
    from concourse import mybir as _mybir
    from concourse.bass_utils import run_bass_kernel_spmd as _run

    nc = _bacc.Bacc("TRN2", target_bir_lowering=False, num_devices=1)
    arrays, args = {}, []
    for name in _INS:
        a = _np.ascontiguousarray(inputs[name])
        arrays[f"in_{name}_dram"] = a
        args.append(nc.dram_tensor(f"in_{name}_dram", a.shape, _mybir.dt.from_np(a.dtype), kind="ExternalInput").ap())
    out = nc.dram_tensor("out_0_dram", (1, SEQ, HID), _mybir.dt.float32, kind="ExternalOutput").ap()
    build(nc, *args, out)
    r = _run(nc, [arrays], core_ids=[0])
    return r.results[0]["out_0_dram"]
```
